# Optimizing a Trainium2 kernel written in Bass

```python
import numpy as np
import jax
import jax.numpy as jnp

def _softmax(x, axis=-1):
    return jax.nn.softmax(x, axis=axis)

def _gelu(x):
    return jax.nn.gelu(x, approximate=True)

def _silu(x):
    return jax.nn.silu(x)

def _sigmoid(x):
    return jax.nn.sigmoid(x)

def _layernorm(x, axis=-1, eps=1e-05):
    m = jnp.mean(x, axis=axis, keepdims=True)
    v = jnp.var(x, axis=axis, keepdims=True)
    return (x - m) / jnp.sqrt(v + eps)

def _scatter_add(tgt, idx, src, axis=0):
    return tgt.at[idx].add(src)

def _segment_sum(src, seg, n):
    return jax.ops.segment_sum(src, seg, n)
kernel_name = 'mk_seq_preln_d1_jaxref_r4_5e5b03'

def setup_inputs(seed: int=0):
    np.random.seed(seed)
    _w = jnp.asarray

    def _L0_attn_setup():
        import jax, jax.numpy as jnp
        import numpy as np
        HID = 256
        RATIO = 4
        SELECT_K = 128
        WINDOW = 64
        N_HEADS = 16
        SCALE = 1.0 / np.sqrt(HID // N_HEADS)

        def _adjust(t, L):
            cur = t.shape[1]
            if cur < L:
                return jnp.pad(t, ((0, 0), (0, L - cur), (0, 0)))
            return t[:, :L]

        def _attend(x, Wq, bq, Wk, bk, Wv, bv):
            q = x @ Wq + bq
            k = x @ Wk + bk
            v = x @ Wv + bv
            s = jnp.einsum('...qd,...kd->...qk', q, k) * SCALE
            p = jax.nn.softmax(s, axis=-1)
            return jnp.einsum('...qk,...kd->...qd', p, v)
        key = jax.random.key(seed)
        ks = jax.random.split(key, 12)
        std = 0.02
        d = {'hidden_states': jax.random.normal(ks[0], (4, 1024, HID), jnp.float32), 'Wq': jax.random.normal(ks[1], (HID, HID), jnp.float32) * std, 'bq': jnp.zeros((HID,), jnp.float32), 'Wk': jax.random.normal(ks[2], (HID, HID), jnp.float32) * std, 'bk': jnp.zeros((HID,), jnp.float32), 'Wv': jax.random.normal(ks[3], (HID, HID), jnp.float32) * std, 'bv': jnp.zeros((HID,), jnp.float32), 'Wo': jax.random.normal(ks[4], (3 * HID, HID), jnp.float32) * std, 'bo': jnp.zeros((HID,), jnp.float32), 'Wg': jax.random.normal(ks[5], (HID, 3), jnp.float32) * std, 'bg': jnp.zeros((3,), jnp.float32), 'Wc': jax.random.normal(ks[6], (RATIO * HID, HID), jnp.float32) * std, 'bc': jnp.zeros((HID,), jnp.float32), 'Ws': jax.random.normal(ks[7], (HID, 1), jnp.float32) * std, 'bs': jnp.zeros((1,), jnp.float32)}
        return d
    _L0_attn_in = _L0_attn_setup()

    def _L0_ffn_setup():
        import jax, jax.numpy as jnp
        import numpy as np
        HID = 256
        NH = 16
        NKV = 4
        HD = HID // NH
        E = 8
        TOPK = 2
        FFN = 512
        EPS = 1e-05
        THETA = 10000.0

        def _rmsnorm(x, w):
            var = jnp.mean(x * x, axis=-1, keepdims=True)
            return x * jax.lax.rsqrt(var + EPS) * w

        def _rope_tables(S):
            inv_freq = 1.0 / THETA ** (jnp.arange(0, HD, 2, dtype=jnp.float32) / HD)
            freqs = jnp.arange(S, dtype=jnp.float32)[:, None] * inv_freq[None, :]
            emb = jnp.concatenate([freqs, freqs], axis=-1)
            return (jnp.cos(emb), jnp.sin(emb))

        def _apply_rope(t, cos, sin):
            t1, t2 = jnp.split(t, 2, axis=-1)
            rot = jnp.concatenate([-t2, t1], axis=-1)
            return t * cos[None, :, None, :] + rot * sin[None, :, None, :]
        key = jax.random.key(seed)
        ks = jax.random.split(key, 6)
        B, S = (1, 512)
        x = jax.random.normal(ks[0], (B, S, HID), dtype=jnp.float32)
        wqkv = jax.random.normal(ks[1], ((NH + 2 * NKV) * HD, HID), dtype=jnp.float32) * 0.02
        wo = jax.random.normal(ks[2], (HID, NH * HD), dtype=jnp.float32) * 0.02
        gate_w = jax.random.normal(ks[3], (E, HID), dtype=jnp.float32) * 0.02
        w13 = jax.random.normal(ks[4], (E, 2 * FFN, HID), dtype=jnp.float32) * 0.02
        w2 = jax.random.normal(ks[5], (E, HID, FFN), dtype=jnp.float32) * 0.02
        return {'x': x, 'ln1_w': jnp.ones((HID,), jnp.float32), 'ln2_w': jnp.ones((HID,), jnp.float32), 'wqkv': wqkv, 'wo': wo, 'gate_w': gate_w, 'w13': w13, 'w2': w2}
    _L0_ffn_in = _L0_ffn_setup()
    _d = {'L0_attn_hidden_states': _L0_attn_in['hidden_states'], 'L0_attn_Wq': _L0_attn_in['Wq'], 'L0_attn_bq': _L0_attn_in['bq'], 'L0_attn_Wk': _L0_attn_in['Wk'], 'L0_attn_bk': _L0_attn_in['bk'], 'L0_attn_Wv': _L0_attn_in['Wv'], 'L0_attn_bv': _L0_attn_in['bv'], 'L0_attn_Wo': _L0_attn_in['Wo'], 'L0_attn_bo': _L0_attn_in['bo'], 'L0_attn_Wg': _L0_attn_in['Wg'], 'L0_attn_bg': _L0_attn_in['bg'], 'L0_attn_Wc': _L0_attn_in['Wc'], 'L0_attn_bc': _L0_attn_in['bc'], 'L0_attn_Ws': _L0_attn_in['Ws'], 'L0_attn_bs': _L0_attn_in['bs'], 'L0_ffn_ln1_w': _L0_ffn_in['ln1_w'], 'L0_ffn_ln2_w': _L0_ffn_in['ln2_w'], 'L0_ffn_wqkv': _L0_ffn_in['wqkv'], 'L0_ffn_wo': _L0_ffn_in['wo'], 'L0_ffn_gate_w': _L0_ffn_in['gate_w'], 'L0_ffn_w13': _L0_ffn_in['w13'], 'L0_ffn_w2': _L0_ffn_in['w2']}
    _x0 = _d['L0_attn_hidden_states']
    _d['L0_attn_hidden_states'] = jax.random.normal(jax.random.fold_in(jax.random.key(seed), 1), (2, 2048, 256), dtype=_x0.dtype)
    del _x0
    return _d

def reference(L0_attn_hidden_states, L0_attn_Wq, L0_attn_bq, L0_attn_Wk, L0_attn_bk, L0_attn_Wv, L0_attn_bv, L0_attn_Wo, L0_attn_bo, L0_attn_Wg, L0_attn_bg, L0_attn_Wc, L0_attn_bc, L0_attn_Ws, L0_attn_bs, L0_ffn_ln1_w, L0_ffn_ln2_w, L0_ffn_wqkv, L0_ffn_wo, L0_ffn_gate_w, L0_ffn_w13, L0_ffn_w2):

    def _L0_attn_ref(hidden_states, Wq, bq, Wk, bk, Wv, bv, Wo, bo, Wg, bg, Wc, bc, Ws, bs):
        import jax, jax.numpy as jnp
        import numpy as np
        HID = 256
        RATIO = 4
        SELECT_K = 128
        WINDOW = 64
        N_HEADS = 16
        SCALE = 1.0 / np.sqrt(HID // N_HEADS)

        def _adjust(t, L):
            cur = t.shape[1]
            if cur < L:
                return jnp.pad(t, ((0, 0), (0, L - cur), (0, 0)))
            return t[:, :L]

        def _attend(x, Wq, bq, Wk, bk, Wv, bv):
            q = x @ Wq + bq
            k = x @ Wk + bk
            v = x @ Wv + bv
            s = jnp.einsum('...qd,...kd->...qk', q, k) * SCALE
            p = jax.nn.softmax(s, axis=-1)
            return jnp.einsum('...qk,...kd->...qd', p, v)
        B, L, H = hidden_states.shape
        gates = jax.nn.sigmoid(hidden_states @ Wg + bg)
        gates = gates / (gates.sum(-1, keepdims=True) + 1e-06)
        pad_c = -L % RATIO
        xc = jnp.pad(hidden_states, ((0, 0), (0, pad_c), (0, 0)))
        blocks = xc.reshape(B, -1, RATIO * H)
        compressed = blocks @ Wc + bc
        comp_out = _adjust(_attend(compressed, Wq, bq, Wk, bk, Wv, bv), L)
        k_eff = min(SELECT_K, L)
        scores = (hidden_states @ Ws + bs)[..., 0]
        _, idx = jax.lax.top_k(scores, k_eff)
        idx = jnp.sort(idx, axis=-1)
        selected = jnp.take_along_axis(hidden_states, idx[..., None], axis=1)
        sel_out = _adjust(_attend(selected, Wq, bq, Wk, bk, Wv, bv), L)
        W = min(WINDOW, L)
        pad_w = -L % W
        xw = jnp.pad(hidden_states, ((0, 0), (0, pad_w), (0, 0)))
        Lp = xw.shape[1]
        starts = np.arange(0, Lp - W + 1, W // 2)
        widx = starts[:, None] + np.arange(W)
        win = xw[:, widx]
        win_ctx = _attend(win, Wq, bq, Wk, bk, Wv, bv)
        win_out = _adjust(win_ctx.reshape(B, -1, H), L)
        combined = jnp.concatenate([comp_out * gates[..., 0:1], sel_out * gates[..., 1:2], win_out * gates[..., 2:3]], axis=-1)
        out = combined @ Wo + bo
        out = out * 0.5 + hidden_states * 0.5
        mu = out.mean(-1, keepdims=True)
        var = out.var(-1, keepdims=True)
        return (out - mu) * jax.lax.rsqrt(var + 1e-06)

    def _L0_ffn_ref(x, ln1_w, ln2_w, wqkv, wo, gate_w, w13, w2):
        import jax, jax.numpy as jnp
        import numpy as np
        HID = 256
        NH = 16
        NKV = 4
        HD = HID // NH
        E = 8
        TOPK = 2
        FFN = 512
        EPS = 1e-05
        THETA = 10000.0

        def _rmsnorm(x, w):
            var = jnp.mean(x * x, axis=-1, keepdims=True)
            return x * jax.lax.rsqrt(var + EPS) * w

        def _rope_tables(S):
            inv_freq = 1.0 / THETA ** (jnp.arange(0, HD, 2, dtype=jnp.float32) / HD)
            freqs = jnp.arange(S, dtype=jnp.float32)[:, None] * inv_freq[None, :]
            emb = jnp.concatenate([freqs, freqs], axis=-1)
            return (jnp.cos(emb), jnp.sin(emb))

        def _apply_rope(t, cos, sin):
            t1, t2 = jnp.split(t, 2, axis=-1)
            rot = jnp.concatenate([-t2, t1], axis=-1)
            return t * cos[None, :, None, :] + rot * sin[None, :, None, :]
        B, S, _ = x.shape
        h = _rmsnorm(x, ln1_w)
        qkv = jnp.einsum('bsh,oh->bso', h, wqkv)
        q = qkv[..., :NH * HD].reshape(B, S, NH, HD)
        k = qkv[..., NH * HD:(NH + NKV) * HD].reshape(B, S, NKV, HD)
        v = qkv[..., (NH + NKV) * HD:].reshape(B, S, NKV, HD)
        cos, sin = _rope_tables(S)
        q = _apply_rope(q, cos, sin)
        k = _apply_rope(k, cos, sin)
        groups = NH // NKV
        k = jnp.repeat(k, groups, axis=2)
        v = jnp.repeat(v, groups, axis=2)
        scale = HD ** (-0.5)
        scores = jnp.einsum('bqhd,bkhd->bhqk', q, k) * scale
        causal = jnp.tril(jnp.ones((S, S), dtype=bool))
        scores = jnp.where(causal[None, None], scores, jnp.finfo(scores.dtype).min)
        probs = jax.nn.softmax(scores, axis=-1)
        attn = jnp.einsum('bhqk,bkhd->bqhd', probs, v).reshape(B, S, NH * HD)
        x = x + jnp.einsum('bso,ho->bsh', attn, wo)
        h = _rmsnorm(x, ln2_w).reshape(-1, HID)
        T = h.shape[0]
        logits = jnp.einsum('th,eh->te', h, gate_w)
        rprobs = jax.nn.softmax(logits.astype(jnp.float32), axis=-1)
        topw, topi = jax.lax.top_k(rprobs, TOPK)
        topw = topw / jnp.sum(topw, axis=-1, keepdims=True)
        wfull = jnp.zeros((T, E), jnp.float32).at[jnp.arange(T)[:, None], topi].set(topw)
        wfull = wfull.astype(h.dtype)
        out = jnp.zeros((T, HID), h.dtype)
        for e in range(E):
            w1 = w13[e, :FFN]
            w3 = w13[e, FFN:]
            g = jax.nn.silu(h @ w1.T) * (h @ w3.T)
            out = out + jnp.einsum('tf,hf->th', g, w2[e]) * wfull[:, e:e + 1]
        return x + out.reshape(B, S, HID)
    x = L0_attn_hidden_states
    x = x + _L0_attn_ref(_layernorm(x, axis=-1), L0_attn_Wq, L0_attn_bq, L0_attn_Wk, L0_attn_bk, L0_attn_Wv, L0_attn_bv, L0_attn_Wo, L0_attn_bo, L0_attn_Wg, L0_attn_bg, L0_attn_Wc, L0_attn_bc, L0_attn_Ws, L0_attn_bs)
    x = x + _L0_ffn_ref(_layernorm(x, axis=-1), L0_ffn_ln1_w, L0_ffn_ln2_w, L0_ffn_wqkv, L0_ffn_wo, L0_ffn_gate_w, L0_ffn_w13, L0_ffn_w2)
    return x

_drawn_inputs = setup_inputs


def setup_inputs(seed=0):
    import zlib

    import numpy as np

    out = dict(_drawn_inputs(seed))
    spreads = {'L0_attn_bq': (0.0, 0.8),
     'L0_attn_bk': (0.0, 0.8),
     'L0_attn_bv': (0.0, 0.8),
     'L0_attn_bo': (0.0, 0.1),
     'L0_attn_bg': (0.0, 0.8),
     'L0_attn_bc': (0.0, 0.8),
     'L0_ffn_ln1_w': (1.0, 0.6),
     'L0_ffn_ln2_w': (1.0, 0.6)}
    factors = {'L0_attn_Wq': 8.0,
     'L0_attn_Wk': 8.0,
     'L0_attn_Wv': 8.0,
     'L0_attn_Wo': 8.0,
     'L0_attn_Wg': 8.0,
     'L0_attn_Wc': 8.0,
     'L0_attn_Ws': 8.0,
     'L0_ffn_wqkv': 8.0,
     'L0_ffn_wo': 8.0,
     'L0_ffn_gate_w': 8.0,
     'L0_ffn_w13': 8.0,
     'L0_ffn_w2': 8.0}
    for name, (base, spread) in spreads.items():
        noise = np.random.default_rng([zlib.crc32(name.encode()), seed]).standard_normal(out[name].shape)
        drawn = base * np.exp(spread * noise) if base else spread * noise
        out[name] = jnp.asarray(drawn.astype(out[name].dtype))
    for name, factor in factors.items():
        out[name] = (out[name] * factor).astype(out[name].dtype)
    return out
```

```python
from contextlib import ExitStack

import concourse.bass as bass
import numpy as np
from concourse import mybir

F32 = mybir.dt.float32
BF16 = mybir.dt.bfloat16
I32 = mybir.dt.int32
U32 = mybir.dt.uint32
ALU = mybir.AluOpType
ACT = mybir.ActivationFunctionType
AX = mybir.AxisListType

P = 128
B, L, H = 2, 2048, 256
C = H // P
T = B * L // P
TB = L // P
RATIO = 4
NBLK = L // RATIO
CT = NBLK // P
SEL = 128
WIN = 64
SCALE = 0.25
NH, NKV, HD = 16, 4, 16
GRP = NH // NKV
QKVW = (NH + 2 * NKV) * HD
E = 8
FFN = 512
NEG = -1e30


class Names(dict):

    def __getattr__(self, name):
        return self[name]


class Chain:

    def __init__(self, eng, sem, base=0):
        self.eng, self.sem, self.base, self.k = eng, sem, base, 0

    def at(self, base):
        self.base, self.k = base, 0

    def link(self, ins, apart=False):
        self.k += 1
        ins.then_inc(self.sem, 1)
        if apart:
            wait_apart(self.eng, self.sem, self.base + self.k)
        else:
            self.eng.wait_ge(self.sem, self.base + self.k)


PASSED = []


def wait_apart(eng, sem, value):
    eng.wait_ge(sem, value)
    eng.sem_inc(PASSED[0], 1)


def build(nc, x, Wq, bq, Wk, bk, Wv, bv, Wo, bo, Wg, bg, Wc, bc, Ws, bs,
          ln1_w, ln2_w, wqkv, wo, gate_w, w13, w2, cos_t, sin_t, out):
    with ExitStack() as whole:
        def sb(name, shape, dt=F32, ctx=whole):
            return ctx.enter_context(nc.sbuf_tensor(name, shape, dt))

        def ps(name, shape, dt=F32, ctx=whole):
            return ctx.enter_context(nc.psum_tensor(name, shape, dt))

        stage_sems = []

        def sem(name):
            stage_sems.append(nc.alloc_semaphore(name=name))
            return stage_sems[-1]

        def free_semaphores():
            nc.clear_and_free_semaphores(list(stage_sems))
            stage_sems.clear()
            nc.all_engine_barrier()

        PASSED[:] = [nc.alloc_semaphore(name="passed")]
        ident = sb("ident", [P, P])
        ones = sb("ones", [P, P])
        x1 = sb("x1", [P, T, H])
        halfpow = sb("halfpow", [P, 1])
        x_rows = x.rearrange("b (t p) h -> p (b t) h", p=P)

        with ExitStack() as layer1:
            def sb1(name, shape, dt=F32):
                return sb(name, shape, dt, layer1)
            base = sb1("base", [P, T, H])
            xnT = sb1("xnT", [P, C, B * L])
            wq_s, wk_s, wv_s = (sb1(n, [P, C, H]) for n in ("wq_s", "wk_s", "wv_s"))
            wo_s = sb1("wo_s", [P, 3 * C, H])
            wc_s = sb1("wc_s", [P, RATIO * C, H])
            wgs = sb1("wgs", [P, C, 4])
            bgs = sb1("bgs", [1, 4])
            bqk = sb1("bqk", [P, 3, C])
            bv_r = sb1("bv_r", [1, H])
            bo_b = sb1("bo_b", [P, H])
            GS = sb1("GS", [P, T, 4])

            stage1(nc, layer1, sb, ps, sem, locals())
            stage23(nc, layer1, sb, ps, sem, locals())
            stage4(nc, layer1, sb, ps, sem, locals())
            free_semaphores()
        stages_layer2(nc, whole, sb, ps, sem, locals())


def stage1(nc, layer, sb, ps, sem, env):
    v = Names(env)
    x_rows, x1, base, xnT, ident, ones, GS = v.x_rows, v.x1, v.base, v.xnT, v.ident, v.ones, v.GS
    G = 4
    with ExitStack() as ctx:
        stats = sb("stats", [P, 2, G, 6], F32, ctx)
        mv = sb("mv", [P, 2, G, 2], F32, ctx)
        rstd = sb("rstd", [P, 2, G], F32, ctx)
        xf = sb("xf", [P, G, H], F32, ctx)
        xTf = sb("xTf", [P, 2, 2, C, P], F32, ctx)
        pT = ps("pT", [P, 2, 2, C, P], F32, ctx)
        pG = ps("pG", [P, 512], F32, ctx)
        x_in = [sem(f"x_in{k}") for k in range(G)]
        w_in, small_in, const0, const1 = sem("w_in"), sem("small_in"), sem("const0"), sem("const1")
        stats_v, stats_done, var_eps, rstd_done, normed, base_copied = (sem(n) for n in
            ("stats_v", "stats_done", "var_eps", "rstd_done", "normed", "base_copied"))
        transposed, xT_done, xnT_copied, gates_mm, gates_out = (sem(n) for n in
            ("transposed", "xT_done", "xnT_copied", "gates_mm", "gates_out"))
        with nc.Block() as block:
            @block.sync
            def _(sp):
                def load(i, k):
                    sp.dma_start(x1[:, i * G + k, :], x_rows[:, i * G + k, :]).then_inc(x_in[k], 16)
                for k in range(G):
                    load(0, k)
                with sp.Fori(1, T // G) as i:
                    for k in range(G):
                        sp.wait_ge(x_in[k], 16 * i)
                        load(i, k)

            @block.scalar
            def _(act):
                act.dma_start(v.wgs[:, :, 0:3], v.Wg.rearrange("(c p) n -> p c n", p=P)).then_inc(small_in, 16)
                act.dma_start(v.wgs[:, :, 3:4], v.Ws.rearrange("(c p) n -> p c n", p=P), allow_slow_non_contiguous=True).then_inc(small_in, 16)
                act.dma_start(v.bgs[:, 0:3], v.bg.rearrange("(a n) -> a n", a=1)).then_inc(small_in, 16)
                act.dma_start(v.bgs[:, 3:4], v.bs.rearrange("(a n) -> a n", a=1)).then_inc(small_in, 16)
                for dst, src in ((v.wc_s, v.Wc), (v.wq_s, v.Wq), (v.wk_s, v.Wk), (v.wv_s, v.Wv), (v.wo_s, v.Wo)):
                    act.dma_start(dst[:, :, :], src.rearrange("(c p) n -> p c n", p=P)).then_inc(w_in, 16)
                for n, src in enumerate((v.bq, v.bk, v.bc)):
                    act.dma_start(v.bqk[:, n, :], src.rearrange("(c p) -> p c", p=P), allow_slow_non_contiguous=True).then_inc(w_in, 16)
                act.dma_start(v.bv_r[:, :], v.bv.rearrange("(a n) -> a n", a=1)).then_inc(w_in, 16)
                act.dma_start(v.bo_b[:, :], v.bo.partition_broadcast(P)).then_inc(w_in, 16)
                with act.Fori(0, T // G) as i:
                    for g in range(2):
                        act.wait_ge(transposed, 2 * i + g + 3)
                        act.wait_ge(gates_mm, 2 * i + g + 1)
                        act.wait_ge(xnT_copied, 2 * i + g + 1)
                        nc.scalar.copy(xTf[:, g], pT[:, g]).then_inc(xT_done, 1)
                act.wait_ge(w_in, 160)

            @block.gpsimd
            def _(pool):
                nc.gpsimd.memset(ident[:, :], 0.0).then_inc(const0, 1)
                nc.gpsimd.memset(ones[:, :], 1.0).then_inc(const0, 1)
                nc.gpsimd.memset(v.halfpow[:, :], -0.5).then_inc(const0, 1)
                pool.wait_ge(const0, 3)
                nc.gpsimd.affine_select(out=ident[:, :], in_=ident[:, :], compare_op=ALU.not_equal, fill=1.0,
                                        base=0, pattern=[[-1, P]], channel_multiplier=1).then_inc(const1, 1)
                pool.sem_inc(xnT_copied, 2)
                pool.sem_inc(base_copied, 1)
                with pool.Fori(0, T // G) as i:
                    wait_apart(pool, stats_done, G * i + G)
                    nc.gpsimd.tensor_scalar(rstd[:, 0, :], mv[:, 0, :, 1], 1e-5, None, ALU.add).then_inc(var_eps, 1)
                    pool.wait_ge(var_eps, i + 1)
                    nc.gpsimd.tensor_tensor(rstd[:, 1, :], rstd[:, 0, :], v.halfpow[:, :].to_broadcast([P, G]),
                                            ALU.pow).then_inc(rstd_done, 1)
                    wait_apart(pool, normed, G * i + G)
                    nc.gpsimd.tensor_copy(base[:, bass.ds(i * G, G), :], xf[:, :, :]).then_inc(base_copied, 1)
                    for g in range(2):
                        wait_apart(pool, xT_done, 2 * i + g + 1)
                        nc.gpsimd.tensor_copy(
                            xnT[:, :, bass.ds((i * G + 2 * g) * P, 2 * P)].rearrange("p c (t n) -> p c t n", t=2),
                            xTf[:, g].rearrange("p t c n -> p c t n")).then_inc(xnT_copied, 1)

            @block.vector
            def _(dve):
                with dve.Fori(0, T // G) as i:
                    for k in range(G):
                        dve.wait_ge(x_in[k], 16 * i + 16)
                        nc.vector.bn_stats(stats[:, 0, k, :], x1[:, i * G + k, :]).then_inc(stats_v, 1)
                    for k in range(G):
                        wait_apart(dve, stats_v, G * i + k + 1)
                        nc.vector.bn_aggr(mv[:, 0, k, :], stats[:, 0, k, :]).then_inc(stats_done, 1)
                    dve.wait_ge(rstd_done, i + 1)
                    dve.wait_ge(stats_done, G * i + G)
                    dve.wait_ge(transposed, 2 * i + 2)
                    dve.wait_ge(base_copied, i + 1)
                    for k in range(G):
                        nc.vector.tensor_scalar(xf[:, k, :], x1[:, i * G + k, :], mv[:, 0, k, 0:1],
                                                rstd[:, 1, k:k + 1], ALU.subtract, ALU.mult).then_inc(normed, 1)
                    dve.wait_ge(gates_mm, 2 * i + 4)
                    nc.vector.tensor_copy(GS[:, bass.ds(i * G, G), :],
                                          pG[:, 0:4 * G].rearrange("p (t n) -> p t n", n=4)).then_inc(gates_out, 1)

            @block.tensor
            def _(pe):
                pe.wait_ge(const1, 1)
                pe.wait_ge(small_in, 64)
                pe.sem_inc(transposed, 2)
                pe.sem_inc(gates_mm, 2)
                with pe.Fori(0, T // G) as i:
                    for g in range(2):
                        pe.wait_ge(normed, G * i + 2 * g + 2)
                        for k in range(2):
                            for c in range(C):
                                last = nc.tensor.transpose(pT[:, g, k, c, :],
                                                           xf[:, 2 * g + k, c * P:(c + 1) * P], ident[:, :])
                        last.then_inc(transposed, 1)
                    for g in range(2):
                        pe.wait_ge(xT_done, 2 * i + g + 1)
                        for k in range(2):
                            n = 4 * (2 * g + k)
                            nc.tensor.matmul(pG[:, n:n + 4], xTf[:, g, k, 0, :], v.wgs[:, 0, :], start=True, stop=False)
                            nc.tensor.matmul(pG[:, n:n + 4], xTf[:, g, k, 1, :], v.wgs[:, 1, :], start=False, stop=False)
                            last = nc.tensor.matmul(pG[:, n:n + 4], ones[0:1, :], v.bgs[:, :], start=False, stop=True)
                        last.then_inc(gates_mm, 1)


def stage23(nc, layer, sb, ps, sem, env):
    v = Names(env)
    base, xnT, ident, ones, GS = v.base, v.xnT, v.ident, v.ones, v.GS
    with ExitStack() as ctx:
        compT, qcT, kcT = (sb(n, [P, B, C, NBLK], F32, ctx) for n in ("compT", "qcT", "kcT"))
        Vc = sb("Vc", [P, B, CT, H], F32, ctx)
        PC = sb("PC", [P, TB, B], F32, ctx)
        with ExitStack() as c2:
            S32 = sb("S32", [T, P], F32, c2)
            srow = sb("srow", [B, L], F32, c2)
            work = sb("work", [B, L], F32, c2)
            above, equal, cum = work, sb("equal", [B, L], F32, c2), sb("cum", [B, L], F32, c2)
            ones_row = sb("ones_row", [B, L], F32, c2)
            best = sb("best", [B, 8], F32, c2)
            need = sb("need", [B, 2], F32, c2)
            eg = sb("eg", [P, T, 3], F32, c2)
            gsum = sb("gsum", [P, T], F32, c2)
            pJ = ps("pJ", [P, 2, 512], F32, c2)
            pS32 = ps("pS32", [T, P], F32, c2)
            pPC = ps("pPC", [P, TB, B], F32, c2)
            proj_mm, proj_out, s32_T, s32_out, srow_in, gate_exp, dve2, place_ready, place_T, place_out = (sem(n) for n in (
                "proj_mm", "proj_out", "s32_T", "s32_out", "srow_in", "gate_exp", "dve2", "place_ready", "place_T",
                "place_out"))
            with nc.Block() as block:
                @block.sync
                def _(sp):
                    sp.wait_ge(s32_out, 1)
                    for b in range(B):
                        sp.dma_start(srow[b:b + 1, :].rearrange("a (t n) -> a t n", n=P),
                                     S32[b * TB:(b + 1) * TB, :]).then_inc(srow_in, 16)
                    sp.wait_ge(srow_in, 16 * B)

                @block.tensor
                def _(pe):
                    nc.tensor.transpose(pS32[:, :], GS[:, :, 3], ident[:, :]).then_inc(s32_T, 1)
                    n = 0

                    def bank():
                        if n >= 2:
                            pe.wait_ge(proj_out, n - 1)
                        return pJ[:, n % 2]
                    for b in range(B):
                        for m in range(C):
                            o = bank()
                            for k in range(RATIO * C):
                                r, c = k // C, k % C
                                last = nc.tensor.matmul(o, v.wc_s[:, k, m * P:(m + 1) * P],
                                                        xnT[:, c, bass.ds(b * L + r, NBLK, RATIO)],
                                                        start=(k == 0), stop=(k == RATIO * C - 1))
                            last.then_inc(proj_mm, 1)
                            n += 1
                    for b in range(B):
                        pe.wait_ge(proj_out, 2 * b + 2)
                        for w in (v.wq_s, v.wk_s):
                            for m in range(C):
                                o = bank()
                                for c in range(C):
                                    last = nc.tensor.matmul(o, w[:, c, m * P:(m + 1) * P], compT[:, b, c, :],
                                                            start=(c == 0), stop=(c == C - 1))
                                last.then_inc(proj_mm, 1)
                                n += 1
                    for b in range(B):
                        for i in range(CT):
                            o = bank()[:, 0:H]
                            for c in range(C):
                                nc.tensor.matmul(o, compT[:, b, c, i * P:(i + 1) * P], v.wv_s[:, c, :],
                                                 start=(c == 0), stop=False)
                            nc.tensor.matmul(o, ones[0:1, :], v.bv_r[:, :], start=False, stop=True).then_inc(proj_mm, 1)
                            n += 1
                    pe.wait_ge(place_ready, 1)
                    for t in range(TB):
                        last = nc.tensor.transpose(pPC[:, t, :], srow[:, t * P:(t + 1) * P], ident[0:B, 0:B])
                    last.then_inc(place_T, 1)

                @block.scalar
                def _(act):
                    nc.scalar.activation(eg[:, :, :], GS[:, :, 0:3], ACT.Exp, scale=-1.0).then_inc(gate_exp, 1)
                    n = 0
                    for b in range(B):
                        for m in range(C):
                            act.wait_ge(proj_mm, n + 1)
                            nc.scalar.activation(compT[:, b, m, :], pJ[:, n % 2], ACT.Identity,
                                                 bias=v.bqk[:, 2, m:m + 1]).then_inc(proj_out, 1)
                            n += 1
                    for b in range(B):
                        for w, dst in ((0, qcT), (1, kcT)):
                            for m in range(C):
                                act.wait_ge(proj_mm, n + 1)
                                nc.scalar.activation(dst[:, b, m, :], pJ[:, n % 2], ACT.Identity,
                                                     bias=v.bqk[:, w, m:m + 1]).then_inc(proj_out, 1)
                                n += 1
                    for b in range(B):
                        for i in range(CT):
                            act.wait_ge(proj_mm, n + 1)
                            nc.scalar.copy(Vc[:, b, i, :], pJ[:, n % 2, 0:H]).then_inc(proj_out, 1)
                            n += 1

                @block.vector
                def _(dve):
                    ch = Chain(dve, dve2)
                    dve.wait_ge(s32_T, 1)
                    nc.vector.tensor_copy(S32[:, :], pS32[:, :]).then_inc(s32_out, 1)
                    dve.wait_ge(gate_exp, 1)
                    ch.link(nc.vector.tensor_scalar(eg[:, :, :], eg[:, :, :], 1.0, None, ALU.add))
                    ch.link(nc.vector.reciprocal(eg[:, :, :], eg[:, :, :]))
                    ch.link(nc.vector.reduce_sum(gsum[:, :], eg[:, :, :], AX.X))
                    ch.link(nc.vector.tensor_scalar(gsum[:, :], gsum[:, :], 1e-6, None, ALU.add))
                    ch.link(nc.vector.reciprocal(gsum[:, :], gsum[:, :]))
                    ch.link(nc.vector.tensor_tensor(GS[:, :, 0:3], eg[:, :, :],
                                                    gsum[:, :].unsqueeze(2).to_broadcast([P, T, 3]), ALU.mult))
                    ch.link(nc.vector.memset(ones_row[:, :], 1.0))
                    dve.wait_ge(srow_in, 16 * B)
                    ch.link(nc.vector.tensor_copy(work[:, :], srow[:, :]))
                    done = ch.k
                    with dve.Fori(0, SEL // 8) as i:
                        ch.at(2 * i + done)
                        ch.link(nc.vector.max(best[:, :], work[:, :]), apart=True)
                        ch.link(nc.vector.match_replace(work[:, :], best[:, :], work[:, :], -3e38), apart=True)
                    ch.at(done + 2 * (SEL // 8))
                    least = best[:, 7:8]
                    ch.link(nc.vector.tensor_scalar(above[:, :], srow[:, :], least, 0.0, ALU.is_gt, ALU.add,
                                                    accum_out=need[:, 0:1]))
                    ch.link(nc.vector.tensor_scalar(equal[:, :], srow[:, :], least, None, ALU.is_equal))
                    ch.link(nc.vector.tensor_scalar(need[:, 1:2], need[:, 0:1], -1.0, float(SEL), ALU.mult, ALU.add))
                    ch.link(nc.vector.tensor_tensor_scan(cum[:, :], ones_row[:, :], equal[:, :], 0.0, ALU.mult, ALU.add))
                    ch.link(nc.vector.scalar_tensor_tensor(out=equal[:, :], in0=cum[:, :], scalar=need[:, 1:2],
                                                           in1=equal[:, :], op0=ALU.is_le, op1=ALU.mult))
                    ch.link(nc.vector.tensor_tensor(above[:, :], above[:, :], equal[:, :], ALU.add))
                    ch.link(nc.vector.tensor_tensor_scan(cum[:, :], ones_row[:, :], above[:, :], 0.0, ALU.mult, ALU.add))
                    nc.vector.tensor_tensor(srow[:, :], cum[:, :], above[:, :], ALU.mult).then_inc(place_ready, 1)
                    dve.wait_ge(place_T, 1)
                    nc.vector.tensor_scalar(PC[:, :, :], pPC[:, :, :], -1.0, None, ALU.add).then_inc(place_out, 1)
                    dve.wait_ge(place_out, 1)

        with ExitStack() as c3:
            iota_i = sb("iota_i", [P, P], I32, c3)
            iota_f = sb("iota_f", [P, P], F32, c3)
            OH = sb("OH", [P, B, TB, P], F32, c3)
            selT = sb("selT", [P, B, C, SEL], F32, c3)
            qksT = sb("qksT", [P, B, 2, C, SEL], F32, c3)
            Vs = sb("Vs", [P, B, H], F32, c3)
            nmax = sb("nmax", [P, 2, 2], F32, c3)
            rs = sb("rs", [P, 2, 2], F32, c3)
            prob = sb("prob", [P, 2, 512], F32, c3)
            probT = sb("probT", [P, 2, 4, P], F32, c3)
            ctxT = sb("ctxT", [P, 2, C, P], F32, c3)
            pS = ps("pS3", [P, 2, 512], F32, c3)
            pPT = ps("pPT3", [P, 4, P], F32, c3)
            pC = ps("pC3", [P, C, P], F32, c3)
            pO = ps("pO3", [P, H], F32, c3)
            pX = ps("pX3", [P, 512], F32, c3)
            pV = ps("pV3", [P, H], F32, c3)
            iota_in, iota_done, onehot, sel_mm, sel_out, selqk_mm, selqk_out, selv_mm, selv_out, bo_in = (sem(n) for n in (
                "iota_in", "iota_done", "onehot", "sel_mm", "sel_out", "selqk_mm", "selqk_out", "selv_mm", "selv_out",
                "bo_in"))
            scores, rowmax, negmax, expd, rowsum, share, weighed, probT_mm, probT_out, ctx_mm, ctx_out, out_mm, added = (
                sem("a_" + n) for n in ("scores", "rowmax", "negmax", "expd", "rowsum", "share", "weighed", "probT_mm",
                                        "probT_out", "ctx_mm", "ctx_out", "out_mm", "added"))
            tiles = [(b, i, CT, 0) for b in range(B) for i in range(CT)] + [(b, 0, 1, 1) for b in range(B)]
            N = len(tiles)
            with nc.Block() as block:
                @block.gpsimd
                def _(pool):
                    nc.gpsimd.iota(iota_i[:, :], pattern=[[1, P]], base=0, channel_multiplier=0).then_inc(iota_in, 1)
                    pool.wait_ge(iota_in, 1)
                    nc.gpsimd.tensor_copy(iota_f[:, :], iota_i[:, :]).then_inc(iota_done, 1)
                    pool.wait_ge(sel_mm, B)
                    for t in list(range(0, TB * B, CT)):
                        last = nc.gpsimd.tensor_tensor(base[:, t:t + CT, :], base[:, t:t + CT, :],
                                                       v.bo_b[:, :].unsqueeze(1).to_broadcast([P, CT, H]), ALU.add)
                        last.then_inc(bo_in, 1)

                @block.tensor
                def _(pe):
                    for b in range(B):
                        pe.wait_ge(onehot, TB * (b + 1))
                        if b:
                            pe.wait_ge(sel_out, b)
                        for c in range(C):
                            for t in range(TB):
                                last = nc.tensor.matmul(pX[:, c * P:(c + 1) * P], base[:, b * TB + t, c * P:(c + 1) * P],
                                                        OH[:, b, t, :], start=(t == 0), stop=(t == TB - 1))
                        last.then_inc(sel_mm, 1)
                    for b in range(B):
                        pe.wait_ge(sel_out, b + 1 if b == 0 else B)
                        if b == 0:
                            pe.wait_ge(sel_out, B)
                        else:
                            pe.wait_ge(selqk_out, 2 * C * b)
                            pe.wait_ge(selv_out, b)
                        for w, W in ((0, v.wq_s), (1, v.wk_s)):
                            for m in range(C):
                                for c in range(C):
                                    last = nc.tensor.matmul(pX[:, (w * C + m) * P:(w * C + m + 1) * P],
                                                            W[:, c, m * P:(m + 1) * P], selT[:, b, c, :],
                                                            start=(c == 0), stop=(c == C - 1))
                        last.then_inc(selqk_mm, 1)
                        for c in range(C):
                            nc.tensor.matmul(pV[:, :], selT[:, b, c, :], v.wv_s[:, c, :], start=(c == 0), stop=False)
                        nc.tensor.matmul(pV[:, :], ones[0:1, :], v.bv_r[:, :], start=False, stop=True).then_inc(selv_mm, 1)

                    def tile_scores(n):
                        b, i, kt, sel = tiles[n]
                        if n >= 2:
                            pe.wait_ge(expd, n - 1)
                        if sel:
                            pe.wait_ge(selqk_out, 2 * C * (b + 1))
                        for c in range(C):
                            q = qksT[:, b, 0, c, :] if sel else qcT[:, b, c, i * P:(i + 1) * P]
                            k = qksT[:, b, 1, c, :] if sel else kcT[:, b, c, :]
                            last = nc.tensor.matmul(pS[:, n % 2, 0:kt * P], q, k, start=(c == 0), stop=(c == C - 1))
                        last.then_inc(scores, 1)

                    def tile_transposes(n):
                        pe.wait_ge(weighed, n + 1)
                        if n >= 1:
                            pe.wait_ge(probT_out, n)
                        for k in range(tiles[n][2]):
                            last = nc.tensor.transpose(pPT[:, k, :], prob[:, n % 2, k * P:(k + 1) * P], ident[:, :])
                        last.then_inc(probT_mm, 1)

                    def tile_context(n):
                        b, i, kt, sel = tiles[n]
                        pe.wait_ge(probT_out, n + 1)
                        if n >= 1:
                            pe.wait_ge(ctx_out, n)
                        if sel:
                            pe.wait_ge(selv_out, b + 1)
                        for m in range(C):
                            for k in range(kt):
                                val = Vs[:, b, m * P:(m + 1) * P] if sel else Vc[:, b, k, m * P:(m + 1) * P]
                                last = nc.tensor.matmul(pC[:, m, :], val, probT[:, n % 2, k, :], start=(k == 0),
                                                        stop=(k == kt - 1))
                        last.then_inc(ctx_mm, 1)

                    def tile_output(n):
                        sel = tiles[n][3]
                        pe.wait_ge(ctx_out, n + 1)
                        if n >= 1:
                            pe.wait_ge(added, n)
                        for m in range(C):
                            last = nc.tensor.matmul(pO[:, :], ctxT[:, n % 2, m, :], v.wo_s[:, sel * C + m, :],
                                                    start=(m == 0), stop=(m == C - 1))
                        last.then_inc(out_mm, 1)
                    tile_scores(0)
                    for n in range(N):
                        if n + 1 < N:
                            tile_scores(n + 1)
                        tile_transposes(n)
                        if n >= 1:
                            tile_output(n - 1)
                        tile_context(n)
                    tile_output(N - 1)

                @block.scalar
                def _(act):
                    for b in range(B):
                        act.wait_ge(sel_mm, b + 1)
                        nc.scalar.copy(selT[:, b], pX[:, 0:C * P].rearrange("p (c n) -> p c n", n=P)).then_inc(sel_out, 1)
                    for b in range(B):
                        act.wait_ge(selqk_mm, b + 1)
                        for w in range(2):
                            for m in range(C):
                                nc.scalar.activation(qksT[:, b, w, m, :], pX[:, (w * C + m) * P:(w * C + m + 1) * P],
                                                     ACT.Identity, bias=v.bqk[:, w, m:m + 1]).then_inc(selqk_out, 1)
                        act.wait_ge(selv_mm, b + 1)
                        nc.scalar.copy(Vs[:, b, :], pV[:, :]).then_inc(selv_out, 1)

                    def tile_exp(n):
                        w = tiles[n][2] * P
                        act.wait_ge(negmax, n + 1)
                        if n >= 2:
                            act.wait_ge(probT_mm, n - 1)
                        nc.scalar.activation(prob[:, n % 2, 0:w], pS[:, n % 2, 0:w], ACT.Exp, scale=SCALE,
                                             bias=nmax[:, n % 2, 1:2], accum_out=rs[:, n % 2, 0:1]).then_inc(expd, 1)

                    def tile_ctx(n):
                        act.wait_ge(ctx_mm, n + 1)
                        if n >= 2:
                            act.wait_ge(out_mm, n - 1)
                        nc.scalar.copy(ctxT[:, n % 2], pC[:, :, :]).then_inc(ctx_out, 1)
                    tile_exp(0)
                    for n in range(N):
                        if n + 1 < N:
                            tile_exp(n + 1)
                        tile_ctx(n)

                @block.vector
                def _(dve):
                    dve.wait_ge(iota_done, 1)
                    for b in range(B):
                        for t in range(TB):
                            nc.vector.tensor_scalar(OH[:, b, t, :], iota_f[:, :], PC[:, t, b:b + 1], None,
                                                    ALU.is_equal).then_inc(onehot, 1)

                    def tile_max(n):
                        w = tiles[n][2] * P
                        dve.wait_ge(scores, n + 1)
                        nc.vector.reduce_max(nmax[:, n % 2, 0:1], pS[:, n % 2, 0:w], AX.X).then_inc(rowmax, 1)
                        dve.wait_ge(rowmax, n + 1)
                        nc.vector.tensor_scalar(nmax[:, n % 2, 1:2], nmax[:, n % 2, 0:1], -SCALE, None,
                                                ALU.mult).then_inc(negmax, 1)

                    def tile_share(n):
                        b, i, kt, sel = tiles[n]
                        w = kt * P
                        dve.wait_ge(expd, n + 1)
                        nc.vector.reciprocal(rs[:, n % 2, 1:2], rs[:, n % 2, 0:1]).then_inc(rowsum, 1)
                        dve.wait_ge(rowsum, n + 1)
                        nc.vector.tensor_scalar(prob[:, n % 2, 0:w], prob[:, n % 2, 0:w], rs[:, n % 2, 1:2],
                                                GS[:, b * TB + i, sel:sel + 1], ALU.mult, ALU.mult).then_inc(weighed, 1)
                        dve.wait_ge(probT_mm, n + 1)
                        if n >= 2:
                            dve.wait_ge(ctx_mm, n - 1)
                        nc.vector.tensor_copy(probT[:, n % 2, 0:kt, :], pPT[:, 0:kt, :]).then_inc(probT_out, 1)

                    def tile_add(n):
                        b, i, _, _ = tiles[n]
                        t = b * TB + i
                        dve.wait_ge(out_mm, n + 1)
                        dve.wait_ge(bo_in, t // CT + 1)
                        if n:
                            dve.wait_ge(added, n)
                        nc.vector.tensor_tensor(base[:, t, :], base[:, t, :], pO[:, :], ALU.add).then_inc(added, 1)
                    tile_max(0)
                    for n in range(N):
                        if n + 1 < N:
                            tile_max(n + 1)
                        tile_share(n)
                        if n >= 1:
                            tile_add(n - 1)
                    tile_add(N - 1)


def stage4(nc, layer, sb, ps, sem, env):
    v = Names(env)
    base, xnT, ident, ones, GS, x1 = v.base, v.xnT, v.ident, v.ones, v.GS, v.x1
    HALF = WIN // 2
    with ExitStack() as ctx:
        xs = sb("xs4", [P, 2, C, 2, WIN], F32, ctx)
        qkT = sb("qkT4", [P, 2, 2, C, P], F32, ctx)
        V = sb("V4", [P, 2, H], F32, ctx)
        nmax = sb("nmax4", [P, 2, 2], F32, ctx)
        rs = sb("rs4", [P, 2, 2], F32, ctx)
        prob = sb("prob4", [P, 2, WIN], F32, ctx)
        block_p = sb("block_p4", [P, 2, P], F32, ctx)
        probT = sb("probT4", [P, 2, P], F32, ctx)
        ctxT = sb("ctxT4", [P, 2, C, P], F32, ctx)
        z = sb("z4", [P, 2, H], F32, ctx)
        stats = sb("stats4", [P, 2, 6], F32, ctx)
        mv = sb("mv4", [P, 2, 2], F32, ctx)
        rstd = sb("rstd4", [P, 2, 3], F32, ctx)
        pQK = ps("pQK4", [P, 2, 2, C, P], F32, ctx)
        pV = ps("pV4", [P, H], F32, ctx)
        pS = ps("pS4", [P, 512], F32, ctx)
        pPT = ps("pPT4", [P, 512], F32, ctx)
        pC = ps("pC4", [P, C, P], F32, ctx)
        pO = ps("pO4", [P, H], F32, ctx)
        names = ("xs_in", "qk_mm", "qk_out", "v_mm", "v_out", "scores", "rowmax", "negmax", "expd", "rowsum", "weighed",
                 "probT_mm", "probT_out", "ctx_mm", "ctx_out", "out_mm", "z_sum", "z_stats", "z_mv", "z_rstd", "pow_in",
                 "z_norm", "x1_out", "zero4")
        s = Names({n: sem("w_" + n) for n in names})

        def pipelined(eng, step, body=2):
            for t in (0, 1):
                step(t, t, t)
            with eng.Fori(1, T // 2) as i:
                for k in range(2):
                    step(2 * i + k, k, 2)

        with nc.Block() as block:
            @block.gpsimd
            def _(pool):
                nc.gpsimd.memset(block_p[:, :, :], 0.0).then_inc(s.zero4, 1)

                def take(t, off, k, late):
                    if late:
                        pool.wait_ge(s.qk_mm, t - 1)
                        wait_apart(pool, s.v_mm, t - 1)
                    for w in range(2):
                        nc.gpsimd.tensor_copy(xs[:, k, :, w, :], xnT[:, :, bass.ds(off + w * HALF, WIN)]).then_inc(s.xs_in, 1)

                def root(t, k, late):
                    wait_apart(pool, s.z_mv, t + 1)
                    nc.gpsimd.tensor_scalar(rstd[:, k, 0:1], mv[:, k, 1:2], 0.25, 1e-6, ALU.mult, ALU.add).then_inc(s.pow_in, 1)
                    pool.wait_ge(s.pow_in, t + 1)
                    if late:
                        pool.wait_ge(s.x1_out, t - 1)
                    nc.gpsimd.tensor_tensor(rstd[:, k, 1:2], rstd[:, k, 0:1], v.halfpow[:, :], ALU.pow).then_inc(s.z_rstd, 1)
                take(0, 0, 0, False)
                take(1, WIN, 1, False)
                take(2, 2 * WIN, 0, True)
                root(0, 0, False)
                take(3, 3 * WIN, 1, True)
                root(1, 1, False)
                with pool.Fori(2, TB // 2) as i:
                    for k in range(2):
                        take(2 * i + k, i * 2 * WIN + k * WIN, k, True)
                        root(2 * i - 2 + k, k, True)
                with pool.Fori(0, TB // 2) as i:
                    for k in range(2):
                        take(TB + 2 * i + k, L + i * 2 * WIN + k * WIN, k, True)
                        root(TB - 2 + 2 * i + k, k, True)
                for t in (T - 2, T - 1):
                    root(t, t % 2, True)

            @block.tensor
            def _(pe):
                def project(t, k, first):
                    pe.wait_ge(s.xs_in, 2 * t + 2)
                    if first >= 2:
                        pe.wait_ge(s.qk_out, 4 * t - 4)
                    x_k = xs[:, k].rearrange("p c w n -> p c (w n)")
                    for w, W in ((0, v.wq_s), (1, v.wk_s)):
                        for m in range(C):
                            for c in range(C):
                                last = nc.tensor.matmul(pQK[:, k, w, m, :], W[:, c, m * P:(m + 1) * P], x_k[:, c, :],
                                                        start=(c == 0), stop=(c == C - 1))
                    last.then_inc(s.qk_mm, 1)
                    if first:
                        pe.wait_ge(s.v_out, t)
                    for c in range(C):
                        nc.tensor.matmul(pV[:, :], x_k[:, c, :], v.wv_s[:, c, :], start=(c == 0), stop=False)
                    nc.tensor.matmul(pV[:, :], ones[0:1, :], v.bv_r[:, :], start=False, stop=True).then_inc(s.v_mm, 1)

                def tile_scores(t, k, first):
                    pe.wait_ge(s.qk_out, 4 * t + 4)
                    if first:
                        pe.wait_ge(s.expd, t)
                    for w in range(2):
                        for c in range(C):
                            last = nc.tensor.matmul(pS[w * WIN:(w + 1) * WIN, 0:WIN],
                                                    qkT[:, k, 0, c, w * WIN:(w + 1) * WIN],
                                                    qkT[:, k, 1, c, w * WIN:(w + 1) * WIN],
                                                    start=(c == 0), stop=(c == C - 1))
                    last.then_inc(s.scores, 1)

                def tile_transposes(t, k, first):
                    pe.wait_ge(s.weighed, 2 * t + 2)
                    if first:
                        pe.wait_ge(s.probT_out, t)
                    nc.tensor.transpose(pPT[:, 0:P], block_p[:, k, :], ident[:, :]).then_inc(s.probT_mm, 1)

                def tile_context(t, k, first):
                    pe.wait_ge(s.probT_out, t + 1)
                    pe.wait_ge(s.v_out, t + 1)
                    if first:
                        pe.wait_ge(s.ctx_out, t)
                    for m in range(C):
                        last = nc.tensor.matmul(pC[:, m, :], V[:, k, m * P:(m + 1) * P], probT[:, k, :],
                                                start=True, stop=True)
                    last.then_inc(s.ctx_mm, 1)

                def tile_output(t, k, first):
                    pe.wait_ge(s.ctx_out, t + 1)
                    if first:
                        pe.wait_ge(s.z_sum, t)
                    for m in range(C):
                        last = nc.tensor.matmul(pO[:, :], ctxT[:, k, m, :], v.wo_s[:, 2 * C + m, :],
                                                start=(m == 0), stop=(m == C - 1))
                    last.then_inc(s.out_mm, 1)

                def step(t, k, first, before=True, after=True):
                    tile_scores(t, k, first)
                    if after:
                        project(t + 1, 1 - k, 2 if first == 2 else first + 1)
                    tile_transposes(t, k, first)
                    if before:
                        tile_output(t - 1, 1 - k, first if first == 2 else 0)
                    tile_context(t, k, first)
                project(0, 0, 0)
                step(0, 0, 0, before=False)
                step(1, 1, 1)
                with pe.Fori(1, T // 2 - 1) as i:
                    for k in range(2):
                        step(2 * i + k, k, 2)
                step(T - 2, 0, 2)
                step(T - 1, 1, 2, after=False)
                tile_output(T - 1, 1, 2)

            @block.scalar
            def _(act):
                def step(t, k, first):
                    act.wait_ge(s.qk_mm, t + 1)
                    if first >= 2:
                        act.wait_ge(s.scores, t - 1)
                    for w in range(2):
                        for m in range(C):
                            nc.scalar.activation(qkT[:, k, w, m, :], pQK[:, k, w, m, :], ACT.Identity,
                                                 bias=v.bqk[:, w, m:m + 1]).then_inc(s.qk_out, 1)
                    act.wait_ge(s.v_mm, t + 1)
                    if first >= 2:
                        act.wait_ge(s.ctx_mm, t - 1)
                    nc.scalar.copy(V[:, k, :], pV[:, :]).then_inc(s.v_out, 1)

                def soft(t, k, first):
                    act.wait_ge(s.negmax, t + 1)
                    if first >= 2:
                        act.wait_ge(s.weighed, 2 * t - 2)
                    nc.scalar.activation(prob[:, k, :], pS[:, 0:WIN], ACT.Exp, scale=SCALE,
                                         bias=nmax[:, k, 1:2], accum_out=rs[:, k, 0:1]).then_inc(s.expd, 1)

                def context(t, k, first):
                    act.wait_ge(s.ctx_mm, t + 1)
                    if first >= 2:
                        act.wait_ge(s.out_mm, t - 1)
                    nc.scalar.copy(ctxT[:, k], pC[:, :, :]).then_inc(s.ctx_out, 1)

                def turn(t, k, first, after=True):
                    soft(t, k, first)
                    if after:
                        step(t + 1, 1 - k, 2 if first >= 1 else 0)
                    context(t, k, first)
                step(0, 0, 0)
                turn(0, 0, 0)
                turn(1, 1, 1)
                with act.Fori(1, T // 2 - 1) as i:
                    for k in range(2):
                        turn(2 * i + k, k, 2)
                turn(T - 2, 0, 2)
                turn(T - 1, 1, 2, after=False)

            @block.vector
            def _(dve):
                dve.wait_ge(s.zero4, 1)

                def soft(t, k, first):
                    dve.wait_ge(s.scores, t + 1)
                    nc.vector.reduce_max(nmax[:, k, 0:1], pS[:, 0:WIN], AX.X).then_inc(s.rowmax, 1)
                    dve.wait_ge(s.rowmax, t + 1)
                    nc.vector.tensor_scalar(nmax[:, k, 1:2], nmax[:, k, 0:1], -SCALE, None, ALU.mult).then_inc(s.negmax, 1)

                def weigh(t, k, first):
                    dve.wait_ge(s.expd, t + 1)
                    nc.vector.reciprocal(rs[:, k, 1:2], rs[:, k, 0:1]).then_inc(s.rowsum, 1)
                    dve.wait_ge(s.rowsum, t + 1)
                    for w in range(2):
                        r = slice(w * WIN, (w + 1) * WIN)
                        nc.vector.tensor_scalar(block_p[r, k, w * WIN:(w + 1) * WIN], prob[r, k, :], rs[r, k, 1:2],
                                                GS[r, t, 2:3], ALU.mult, ALU.mult).then_inc(s.weighed, 1)
                    dve.wait_ge(s.probT_mm, t + 1)
                    if first >= 2:
                        dve.wait_ge(s.ctx_mm, t - 1)
                    nc.vector.tensor_copy(probT[:, k, :], pPT[:, 0:P]).then_inc(s.probT_out, 1)

                def finish(t, k, first):
                    dve.wait_ge(s.out_mm, t + 1)
                    nc.vector.tensor_tensor(z[:, k, :], base[:, t, :], pO[:, :], ALU.add).then_inc(s.z_sum, 1)
                    dve.wait_ge(s.z_sum, t + 1)
                    nc.vector.bn_stats(stats[:, k, :], z[:, k, :]).then_inc(s.z_stats, 1)
                    wait_apart(dve, s.z_stats, t + 1)
                    nc.vector.bn_aggr(mv[:, k, :], stats[:, k, :]).then_inc(s.z_mv, 1)

                def norm(t, k, first):
                    dve.wait_ge(s.z_rstd, t + 1)
                    nc.vector.tensor_scalar(z[:, k, :], z[:, k, :], mv[:, k, 0:1], 0.5, ALU.subtract,
                                            ALU.mult).then_inc(s.z_norm, 1)
                    dve.wait_ge(s.z_norm, t + 1)
                    nc.vector.scalar_tensor_tensor(out=x1[:, t, :], in0=z[:, k, :], scalar=rstd[:, k, 1:2],
                                                   in1=x1[:, t, :], op0=ALU.mult, op1=ALU.add).then_inc(s.x1_out, 1)

                def turn(t, k, first):
                    soft(t, k, first)
                    if first >= 2:
                        norm(t - 2, k, first)
                    weigh(t, k, first)
                    if first:
                        finish(t - 1, 1 - k, first)
                pipelined(dve, turn)
                norm(T - 2, 0, 2)
                finish(T - 1, 1, 2)
                norm(T - 1, 1, 2)


def stages_layer2(nc, whole, sb, ps, sem, env):
    v = Names(env)
    with ExitStack() as late:
        ln2_b = sb("ln2_b", [P, H], F32, late)
        woT = sb("woT", [P, C, H], F32, late)
        gwT = sb("gwT", [P, C, E], F32, late)
        weights = sb("weights", [P, T, 2], F32, late)
        rows = sb("rows", [P, T, 2], I32, late)
        rowsf, shift, shifts = (sb(n, [P, T, 2], F32, late) for n in ("rowsf", "shift", "shifts"))
        pad_rows = sb("pad_rows", [P, E], I32, late)
        jrow_i = sb("jrow_i", [P, NTAB], I32, late)
        jrow, jc, ej, before, rowf = (sb(n, [P, NTAB], F32, late) for n in ("jrow", "jc", "ej", "before", "rowf"))
        cmp = sb("cmp", [P, E, NTAB], F32, late)
        steps = sb("steps", [P, T], F32, late)
        padf, ntile, ends = (sb(n, [P, E], F32, late) for n in ("padf", "ntile", "ends"))
        lastt = sb("lastt", [P, 1], F32, late)
        tile_expert, tile_in = (sb(n, [P, NTAB], I32, late) for n in ("tile_expert", "tile_in"))
        queue = nc.dram_tensor("queue", [E * CAP, H], F32).ap()
        results = nc.dram_tensor("results", [MAXT * P, H], F32).ap()
        with ExitStack() as att:
            QKV = sb("QKV", [P, T, QKVW], F32, att)
            stage5(nc, sb, ps, sem, locals(), v)
            stage6(nc, sb, ps, sem, locals(), v)
            v.free_semaphores()
            stage7(nc, sb, ps, sem, locals(), v)
        stage8(nc, sb, ps, sem, locals(), v)
        stage9(nc, sb, ps, sem, locals(), v)


def stage5(nc, sb, ps, sem, env, base_env):
    v, u = Names(env), base_env
    x1, ident, ones = u.x1, u.ident, u.ones
    G = 4
    with ExitStack() as ctx:
        ln1_b = sb("ln1_b", [P, H], F32, ctx)
        wqkvT = sb("wqkvT", [P, C, QKVW], F32, ctx)
        raw = sb("raw5", [P, 6, H], F32, ctx)
        cosb = sb("cosb", [P, TB, HD // 2], F32, ctx)
        sinb = sb("sinb", [P, TB, HD // 2], F32, ctx)
        stats = sb("stats5", [P, G, 6], F32, ctx)
        mv = sb("mv5", [P, G, 2], F32, ctx)
        rstd = sb("rstd5", [P, 4, G], F32, ctx)
        sq = sb("sq5", [P, G], F32, ctx)
        junk = sb("junk5", [P, G, H], F32, ctx)
        xl = sb("xl5", [P, G, H], F32, ctx)
        h = sb("h5", [P, G, H], F32, ctx)
        hT = sb("hT5", [P, 2, 2, C, P], F32, ctx)
        qk = sb("qk5", [P, 2, 320], F32, ctx)
        byc = sb("byc5", [P, 2, 320], F32, ctx)
        bys = sb("bys5", [P, 2, 320], F32, ctx)
        pT = ps("pT5", [P, 2, 2, C, P], F32, ctx)
        pQ = ps("pQ5", [P, 2, 512], F32, ctx)
        names = ("raw_in", "small_in", "wT_mm", "wT_out", "stats", "mv", "eps1", "rstd1", "xl", "square", "eps2", "eps3",
                 "rstd2", "h", "hT_mm", "hT_out", "qkv_mm", "qk_out", "v_out", "turned", "byc", "bys")
        s = Names({n: sem("q_" + n) for n in names})
        nwT = (QKVW // P + C) * C + C
        with nc.Block() as block:
            @block.sync
            def _(sp):
                sp.dma_start(raw[:, 0:3, :], u.wqkv.rearrange("(t p) h -> p t h", p=P)).then_inc(s.raw_in, 16)
                sp.dma_start(raw[:, 3:5, :], u.wo.rearrange("(t p) h -> p t h", p=P)).then_inc(s.raw_in, 16)
                sp.dma_start(raw[0:E, 5, :], u.gate_w).then_inc(s.raw_in, 16)
                sp.dma_start(ln1_b[:, :], u.ln1_w.partition_broadcast(P)).then_inc(s.small_in, 16)
                sp.dma_start(v.ln2_b[:, :], u.ln2_w.partition_broadcast(P)).then_inc(s.small_in, 16)
                sp.dma_start(cosb[:, :, :], u.cos_t.rearrange("(t p) n -> p t n", p=P)).then_inc(s.small_in, 16)
                sp.dma_start(sinb[:, :, :], u.sin_t.rearrange("(t p) n -> p t n", p=P)).then_inc(s.small_in, 16)

            @block.tensor
            def _(pe):
                pe.wait_ge(s.raw_in, 48)
                for n in range(6):
                    rows = E if n == 5 else P
                    for c in range(C):
                        k = 2 * n + c
                        if k >= 2:
                            pe.wait_ge(s.wT_out, k - 1)
                        nc.tensor.transpose(pT[:, k % 2, 0, 0, 0:rows], raw[0:rows, n, c * P:(c + 1) * P],
                                            ident[0:rows, 0:rows]).then_inc(s.wT_mm, 1)
                pe.wait_ge(s.wT_out, 12)
                pe.sem_inc(s.hT_mm, 2)
                pe.sem_inc(s.qkv_mm, 2)
                with pe.Fori(0, T // G) as i:
                    for g in range(2):
                        pe.wait_ge(s.h, G * i + 2 * g + 2)
                        for k in range(2):
                            for c in range(C):
                                last = nc.tensor.transpose(pT[:, g, k, c, :], h[:, 2 * g + k, c * P:(c + 1) * P], ident[:, :])
                        last.then_inc(s.hT_mm, 1)
                    for g in range(2):
                        pe.wait_ge(s.hT_out, 2 * i + g + 1)
                        for k in range(2):
                            pe.wait_ge(s.v_out, 4 * i + 2 * g + k + 1)
                            pe.wait_ge(s.qk_out, 4 * i + 2 * g + k + 1)
                            for c in range(C):
                                last = nc.tensor.matmul(pQ[:, k, 0:QKVW], hT[:, g, k, c, :], wqkvT[:, c, :],
                                                        start=(c == 0), stop=(c == C - 1))
                            last.then_inc(s.qkv_mm, 1)

            @block.scalar
            def _(act):
                act.sem_inc(s.v_out, 2)
                act.sem_inc(s.qk_out, 2)
                with act.Fori(0, T // G) as i:
                    for g in range(2):
                        act.wait_ge(s.hT_mm, 2 * i + g + 3)
                        act.wait_ge(s.qkv_mm, 4 * i + 2 * g + 2)
                        nc.scalar.copy(hT[:, g], pT[:, g]).then_inc(s.hT_out, 1)
                    for g in range(2):
                        for k in range(2):
                            t = 4 * i + 2 * g + k
                            act.wait_ge(s.qkv_mm, t + 3)
                            act.wait_ge(s.turned, t + 1)
                            nc.scalar.copy(qk[:, k, :], pQ[:, k, 0:320]).then_inc(s.qk_out, 1)
                            nc.scalar.copy(v.QKV[:, t, 320:QKVW], pQ[:, k, 320:QKVW]).then_inc(s.v_out, 1)

            @block.gpsimd
            def _(pool):
                pool.sem_inc(s.turned, 2)
                with pool.Fori(0, T // G) as i:
                    wait_apart(pool, s.mv, G * i + G)
                    nc.gpsimd.tensor_scalar(rstd[:, 0, :], mv[:, :, 1], 1e-5, None, ALU.add).then_inc(s.eps1, 1)
                    pool.wait_ge(s.eps1, i + 1)
                    nc.gpsimd.tensor_tensor(rstd[:, 1, :], rstd[:, 0, :], u.halfpow[:, :].to_broadcast([P, G]),
                                            ALU.pow).then_inc(s.rstd1, 1)
                    wait_apart(pool, s.square, G * i + G)
                    nc.gpsimd.tensor_scalar(rstd[:, 2, :], sq[:, :], 1.0 / H, 1e-5, ALU.mult, ALU.add).then_inc(s.eps2, 1)
                    pool.wait_ge(s.eps2, i + 1)
                    nc.gpsimd.tensor_tensor(rstd[:, 3, :], rstd[:, 2, :], u.halfpow[:, :].to_broadcast([P, G]),
                                            ALU.pow).then_inc(s.rstd2, 1)
                    for k in range(G):
                        t = G * i + k
                        pos = G * (i % (TB // G)) + k
                        pool.wait_ge(s.qk_out, t + 3)
                        src = qk[:, k % 2, :].rearrange("p (n d) -> p n d", d=8)
                        for name, dst, table in (("byc", byc, cosb), ("bys", bys, sinb)):
                            nc.gpsimd.tensor_tensor(dst[:, k % 2, :].rearrange("p (n d) -> p n d", d=8), src,
                                                    table[:, pos, :].unsqueeze(1).to_broadcast([P, 40, 8]),
                                                    ALU.mult).then_inc(s.byc if name == "byc" else s.bys, 1)
                        pool.wait_ge(s.byc, t + 1)
                        pool.wait_ge(s.bys, t + 1)
                        o = v.QKV[:, t, 0:320].rearrange("p (n a d) -> p n a d", a=2, d=8)
                        yc = byc[:, k % 2, :].rearrange("p (n a d) -> p n a d", a=2, d=8)
                        ys = bys[:, k % 2, :].rearrange("p (n a d) -> p n a d", a=2, d=8)
                        nc.gpsimd.tensor_tensor(o[:, :, 0, :], yc[:, :, 0, :], ys[:, :, 1, :], ALU.subtract)
                        nc.gpsimd.tensor_tensor(o[:, :, 1, :], yc[:, :, 1, :], ys[:, :, 0, :], ALU.add).then_inc(s.turned, 1)

            @block.vector
            def _(dve):
                k = 0
                for n in range(6):
                    for c in range(C):
                        dve.wait_ge(s.wT_mm, k + 1)
                        rows = E if n == 5 else P
                        dst = (wqkvT[:, c, n * P:(n + 1) * P] if n < 3 else v.woT[:, c, (n - 3) * P:(n - 2) * P]
                               if n < 5 else v.gwT[:, c, :])
                        nc.vector.tensor_copy(dst, pT[:, k % 2, 0, 0, 0:rows]).then_inc(s.wT_out, 1)
                        k += 1
                dve.wait_ge(s.small_in, 64)
                with dve.Fori(0, T // G) as i:
                    for k in range(G):
                        nc.vector.bn_stats(stats[:, k, :], x1[:, G * i + k, :]).then_inc(s.stats, 1)
                    for k in range(G):
                        wait_apart(dve, s.stats, G * i + k + 1)
                        nc.vector.bn_aggr(mv[:, k, :], stats[:, k, :]).then_inc(s.mv, 1)
                    dve.wait_ge(s.mv, G * i + G)
                    dve.wait_ge(s.rstd1, i + 1)
                    for k in range(G):
                        nc.vector.tensor_scalar(xl[:, k, :], x1[:, G * i + k, :], mv[:, k, 0:1], rstd[:, 1, k:k + 1],
                                                ALU.subtract, ALU.mult).then_inc(s.xl, 1)
                    for k in range(G):
                        dve.wait_ge(s.xl, G * i + k + 1)
                        nc.vector.tensor_tensor_reduce(junk[:, k, :], xl[:, k, :], xl[:, k, :], 1.0, 0.0, ALU.mult, ALU.add,
                                                       sq[:, k:k + 1]).then_inc(s.square, 1)
                    dve.wait_ge(s.rstd2, i + 1)
                    dve.wait_ge(s.hT_mm, 2 * i + 2)
                    for k in range(G):
                        nc.vector.scalar_tensor_tensor(out=h[:, k, :], in0=xl[:, k, :], scalar=rstd[:, 3, k:k + 1],
                                                       in1=ln1_b[:, :], op0=ALU.mult, op1=ALU.mult).then_inc(s.h, 1)


PARTS_Q = (0, 0, 1, 1, 0, 2)
PARTS_K = (0, 1, 0, 1, 2, 0)
NPART = len(PARTS_Q)
ROWS = NPART * HD
CH = L // 512
KSTEPS = [(c, kt) for c in range(CH) for kt in range(4 * c + 4)]
UNITS = [(h, qt, part) for h in range(GRP) for qt in range(TB) for part in range(1 if qt < 8 else 2)]


def background():
    items = [("K", 0), ("K", 1)] + [("Q", h, f) for h in range(2) for f in range(2)]
    for h in range(GRP):
        items += [("U", n) for n, unit in enumerate(UNITS) if unit[0] == h]
        if h + 2 < GRP:
            items += [("Q", h + 2, f) for f in range(2)]
    return items + [("M", 0), ("M", 1)]


def interleave(steps):
    items = background()
    ends = [min(len(items), -(-len(items) * (n + 1) // (steps - 2))) for n in range(steps)]
    return [items[a:b] for a, b in zip([0] + ends, ends)]


def stage6(nc, sb, ps, sem, env, base_env):
    v, u = Names(env), base_env
    QKV, ident = v.QKV, u.ident
    NG = B * NKV
    NT = 12
    NU, NS_ = len(UNITS), len(KSTEPS)
    BESIDE = interleave(NS_)
    with ExitStack() as ctx:
        identb = sb("identb", [P, P], BF16, ctx)
        maskf = sb("maskf", [P, P], F32, ctx)
        mask_qk = sb("mask_qk", [P, P], BF16, ctx)
        mask_kq = sb("mask_kq", [P, P], BF16, ctx)
        Qt = sb("Qt", [P, TB, GRP, ROWS], BF16, ctx)
        Kt = sb("Kt", [P, TB, ROWS], BF16, ctx)
        rem = sb("rem", [P, 2, TB, GRP * HD], F32, ctx)
        KT = sb("KT", [P, 2, L], BF16, ctx)
        QT = sb("QT", [P, 2, GRP, L], BF16, ctx)
        VV = sb("VV", [P, 2, TB, 32], F32, ctx)
        prob = sb("prob6", [P, 2, 2, 2, 512], F32, ctx)
        mx = sb("mx", [P, 2, GRP, TB], F32, ctx)
        mrem = sb("mrem", [P, 3, TB, GRP], F32, ctx)
        mpart = sb("mpart", [P, TB, GRP, 3], BF16, ctx)
        mrow = sb("mrow", [GRP * 3, L], BF16, ctx)
        oS = sb("oS", [P, 512], F32, ctx)
        den = sb("den", [P, 4, GRP], F32, ctx)
        pS = ps("pS6", [P, 2, 2, 512], F32, ctx)
        pO = ps("pO6", [P, 512], F32, ctx)
        pM = ps("pM6", [P, 1024], F32, ctx)
        pT = ps("pT6", [P, 512], F32, ctx)
        pTb = pT[:, :].bitcast(BF16)
        names = ("zero", "masks", "masks_b", "maskT", "maskT_out", "qparts", "kparts", "vparts", "T_mm", "T_out", "unit_mm", "unit_max",
                 "mparts", "mrow_in", "pair_mm", "pair_exp", "pv", "o_out", "den_out", "o_put", "vv_init", "ones_in",
                 "qchain", "mchain")
        s = Names({n: sem("c_" + n) for n in names})

        def group(gi):
            b, g = gi // NKV, gi % NKV
            return b * TB, g

        with nc.Block() as block:
            @block.sync
            def _(sp):
                def send(gi, par, maxima_out):
                    sp.wait_ge(s.T_out, maxima_out)
                    for h in range(GRP):
                        sp.dma_start(QT[ROWS:ROWS + 3, par, h, :], mrow[3 * h:3 * h + 3, :]).then_inc(s.mrow_in, 16)
                sp.wait_ge(s.ones_in, 1)
                send(0, 0, 1 + NT)
                send(1, 1, 1 + NT + (NT + CH - 1))
                with sp.Fori(1, NG // 2) as i:
                    for k in range(2):
                        gi = 2 * i + k
                        send(gi, k, (NT + CH) * gi + NT)
                sp.wait_ge(s.mrow_in, 64 * NG)

            @block.gpsimd
            def _(pool):
                nc.gpsimd.memset(maskf[:, :], 0.0).then_inc(s.zero, 1)
                nc.gpsimd.memset(VV[:, :, :, :], 0.0).then_inc(s.zero, 1)
                nc.gpsimd.tensor_copy(identb[:, :], ident[:, :]).then_inc(s.masks_b, 1)
                pool.wait_ge(s.zero, 2)
                nc.gpsimd.affine_select(out=maskf[:, :], in_=maskf[:, :], compare_op=ALU.is_ge, fill=NEG, base=0,
                                        pattern=[[-1, P]], channel_multiplier=1).then_inc(s.masks, 1)
                nc.gpsimd.memset(VV[:, :, :, HD:HD + 1], 1.0).then_inc(s.vv_init, 1)
                pool.wait_ge(s.masks, 1)
                nc.gpsimd.tensor_copy(mask_qk[:, :], maskf[:, :]).then_inc(s.masks_b, 1)
                pool.wait_ge(s.masks_b, 2)
                nc.gpsimd.memset(maskf[:, :], 0.0).then_inc(s.zero, 1)
                pool.wait_ge(s.zero, 3)
                nc.gpsimd.affine_select(out=maskf[:, :], in_=maskf[:, :], compare_op=ALU.is_ge, fill=NEG, base=0,
                                        pattern=[[1, P]], channel_multiplier=-1).then_inc(s.masks, 1)
                pool.wait_ge(s.masks, 2)
                nc.gpsimd.tensor_copy(mask_kq[:, :], maskf[:, :]).then_inc(s.masks_b, 1)
                pool.wait_ge(s.vv_init, 1)
                ch = Chain(pool, s.qchain)

                def split(src, parts, slots, rem_ap, per):
                    for part in range(3):
                        at = [n for n in range(NPART) if slots[n] == part]
                        now = src if part == 0 else rem_ap[part - 1]
                        ch.link(nc.gpsimd.tensor_copy(parts(at[0]), now), apart=True)
                        for n in at[1:]:
                            last = nc.gpsimd.tensor_copy(parts(n), parts(at[0]))
                            if part == 2:
                                return last
                            last.then_inc(s.kparts, 1)
                        if part < 2:
                            ch.link(nc.gpsimd.tensor_tensor(rem_ap[part], now, parts(at[0]), ALU.subtract), apart=True)

                def prepare(gi, par):
                    t0, g = group(gi)
                    tiles = bass.ds(t0, TB)
                    ch.at(10 * gi)
                    q = QKV[:, tiles, bass.ds(g * GRP * HD, GRP * HD)].rearrange("p t (h d) -> p t h d", d=HD)
                    k = QKV[:, tiles, bass.ds(NH * HD + g * HD, HD)]
                    split(k, lambda n: Kt[:, :, n * HD:(n + 1) * HD], PARTS_K,
                          [rem[:, r, :, 0:HD] for r in range(2)], 0)
                    r4 = [rem[:, r].rearrange("p t (h d) -> p t h d", d=HD) for r in range(2)]
                    split(q, lambda n: Qt[:, :, :, n * HD:(n + 1) * HD], PARTS_Q, r4, 0)
                    assert ch.k == 10
                    nc.gpsimd.tensor_copy(VV[:, par, :, 0:HD],
                                          QKV[:, tiles, bass.ds((NH + NKV) * HD + g * HD, HD)]).then_inc(s.vparts, 1)
                prepare(0, 0)
                pool.wait_ge(s.unit_mm, NU)
                prepare(1, 1)
                with pool.Fori(1, NG // 2) as i:
                    for k in range(2):
                        gi = 2 * i + k
                        pool.wait_ge(s.unit_mm, NU * gi)
                        pool.wait_ge(s.pv, NS_ * (gi - 1) + 2)
                        prepare(gi, k)

            @block.tensor
            def _(pe):
                pe.wait_ge(s.masks_b, 3)
                pe.wait_ge(s.ones_in, 1)
                pe.sem_inc(s.pv, 2)

                def beside(item, gi, par, cnt):
                    kind = item[0]
                    if kind in "KQM":
                        pe.wait_ge(s.T_out, cnt.t)
                        cnt.t += 1
                        f = item[-1]
                        if kind == "M":
                            pe.wait_ge(s.mparts, gi + 1)
                        else:
                            pe.wait_ge(s.qchain, 10 * gi + (5 if kind == "K" else 10))
                            pe.wait_ge(s.kparts, 6 * gi + (3 if kind == "K" else 6))
                        for k in range(8):
                            t = 8 * f + k
                            if kind == "K":
                                src, rows = Kt[:, t, :], ROWS
                            elif kind == "Q":
                                src, rows = Qt[:, t, item[1], :], ROWS
                            else:
                                src, rows = mpart[:, t, :, :].rearrange("p h a -> p (h a)"), 3 * GRP
                            last = nc.tensor.transpose(pTb[0:rows, k * P:(k + 1) * P], src, identb[:, :])
                        last.then_inc(s.T_mm, 1)
                        return
                    n = item[1]
                    h, qt, part = UNITS[n]
                    pe.wait_ge(s.unit_max, NU * gi + n + 1)
                    if qt == 0:
                        pe.wait_ge(s.T_out, cnt.t)
                    w = (qt + 1) * P
                    start, w = (0, min(w, 1024)) if part == 0 else (1024, w - 1024)
                    lhsT = QT[0:ROWS, par, h, qt * P:(qt + 1) * P]
                    masked = part == 1 or qt < 8
                    for a in range(0, w, 512):
                        n1 = min(512, w - a)
                        end = masked and a + n1 == w
                        last = nc.tensor.matmul(pM[:, a:a + n1], lhsT, KT[0:ROWS, par, start + a:start + a + n1],
                                                start=True, stop=not end)
                        if end:
                            last = nc.tensor.matmul(pM[:, w - P:w], identb[:, :], mask_qk[:, :], start=False, stop=True)
                    last.then_inc(s.unit_mm, 1)

                class Cnt:
                    def __init__(self, t):
                        self.t = t

                def pair(gi, par, n, pr):
                    c, kt = KSTEPS[n]
                    lo = max(0, kt - 4 * c) * P
                    idx = 2 * (NS_ * gi + n) + pr
                    pe.wait_ge(s.pair_exp, idx + 1)
                    for hh in range(2):
                        h = 2 * pr + hh
                        diag = kt >= 4 * c
                        last = nc.tensor.matmul(pS[:, pr, hh, lo:512], KT[0:ROWS + 3, par, kt * P:(kt + 1) * P],
                                                QT[0:ROWS + 3, par, h, 512 * c + lo:512 * c + 512], start=True,
                                                stop=not diag)
                        if diag:
                            last = nc.tensor.matmul(pS[:, pr, hh, lo:lo + P], identb[:, :], mask_kq[:, :], start=False,
                                                    stop=True)
                    last.then_inc(s.pair_mm, 1)

                def values(gi, par, n):
                    c, kt = KSTEPS[n]
                    lo = max(0, kt - 4 * c) * P
                    pe.wait_ge(s.pair_exp, 2 * (NS_ * gi + n) + 4)
                    if kt == 0:
                        pe.wait_ge(s.o_out, CH * gi + c + 1)
                    if n == 0:
                        pe.wait_ge(s.vparts, gi + 1)
                    for h in range(GRP):
                        last = nc.tensor.matmul(pO[32 * h:32 * h + 32, lo:512], VV[:, par, kt, :],
                                                prob[:, n % 2, h // 2, h % 2, lo:512], start=(kt == 0),
                                                stop=(kt == 4 * c + 3), tile_position=(0, 32 * h))
                    last.then_inc(s.pv, 1)

                def chunk_out(gi, c, cnt):
                    pe.wait_ge(s.o_out, CH * gi + c + 2)
                    pe.wait_ge(s.T_out, cnt.t)
                    cnt.t += 1
                    for k in range(4):
                        last = nc.tensor.transpose(pT[:, k * P:(k + 1) * P], oS[:, k * P:(k + 1) * P], ident[:, :])
                    last.then_inc(s.T_mm, 1)

                def one(gi, par, more):
                    cnt = Cnt(1 + NT + (NT + CH) * gi)
                    pe.wait_ge(s.mrow_in, 64 * gi + 64)
                    pair(gi, par, 0, 0)
                    pair(gi, par, 0, 1)
                    for n in range(NS_):
                        extra = [x for x in BESIDE[n]] if more else []
                        third = -(-len(extra) // 3)
                        for x in extra[:third]:
                            beside(x, gi + 1, 1 - par, cnt)
                        if n + 1 < NS_:
                            pair(gi, par, n + 1, 0)
                        for x in extra[third:2 * third]:
                            beside(x, gi + 1, 1 - par, cnt)
                        values(gi, par, n)
                        if n + 1 < NS_:
                            pair(gi, par, n + 1, 1)
                        for x in extra[2 * third:]:
                            beside(x, gi + 1, 1 - par, cnt)
                        if n and KSTEPS[n][1] == 0:
                            chunk_out(gi, KSTEPS[n][0] - 1, cnt)
                    chunk_out(gi, CH - 1, cnt)
                cnt = Cnt(1)
                for item in background():
                    beside(item, 0, 0, cnt)
                with pe.Fori(0, NG // 2 - 1) as i:
                    for k in range(2):
                        one(2 * i + k, k, True)
                one(NG - 2, 0, True)
                one(NG - 1, 1, False)

            @block.scalar
            def _(act):
                act.sem_inc(s.pair_exp, 2)
                act.wait_ge(s.vv_init, 1)
                with act.Fori(0, NG // 2) as i:
                    for k in range(2):
                        gi = 2 * i + k
                        for n in range(NS_):
                            c, kt = KSTEPS[n]
                            lo = max(0, kt - 4 * c) * P
                            act.wait_ge(s.pv, NS_ * gi + n + 1)
                            for pr in range(2):
                                act.wait_ge(s.pair_mm, 2 * (NS_ * gi + n) + pr + 1)
                                nc.scalar.activation(prob[:, n % 2, pr, :, lo:512], pS[:, pr, :, lo:512], ACT.Exp,
                                                     scale=SCALE).then_inc(s.pair_exp, 1)

            @block.vector
            def _(dve):
                dve.sem_inc(s.T_out, 1)
                dve.sem_inc(s.unit_max, 1)
                dve.sem_inc(s.o_out, 1)
                nc.vector.memset(KT[ROWS:ROWS + 3, :, :], 1.0).then_inc(s.ones_in, 1)
                ch = Chain(dve, s.mchain)
                ch.link(nc.vector.memset(mx[:, :, :, :], -3e38))

                def beside(item, gi, par, cnt):
                    kind = item[0]
                    if kind in "KQM":
                        f = item[-1]
                        if kind == "M" and f == 0:
                            dve.wait_ge(s.unit_max, NU * gi + NU + 1)
                            ch.at(6 * gi + 1)
                            ch.link(nc.vector.tensor_tensor(mrem[:, 1], mx[:, 0].rearrange("p h t -> p t h"),
                                                            mx[:, 1].rearrange("p h t -> p t h"), ALU.max))
                            ch.link(nc.vector.tensor_scalar(mrem[:, 0], mrem[:, 1], -1.0, None, ALU.mult))
                            ch.link(nc.vector.tensor_copy(mpart[:, :, :, 0], mrem[:, 0]))
                            ch.link(nc.vector.tensor_tensor(mrem[:, 1], mrem[:, 0], mpart[:, :, :, 0], ALU.subtract))
                            ch.link(nc.vector.tensor_copy(mpart[:, :, :, 1], mrem[:, 1]))
                            ch.link(nc.vector.tensor_tensor(mrem[:, 2], mrem[:, 1], mpart[:, :, :, 1], ALU.subtract))
                            nc.vector.tensor_copy(mpart[:, :, :, 2], mrem[:, 2]).then_inc(s.mparts, 1)
                        dve.wait_ge(s.T_mm, cnt.t)
                        cnt.t += 1
                        cols = slice(f * 1024, f * 1024 + 1024)
                        if kind == "K":
                            dst, rows = KT[0:ROWS, par, cols], ROWS
                        elif kind == "Q":
                            dst, rows = QT[0:ROWS, par, item[1], cols], ROWS
                        else:
                            dst, rows = mrow[:, cols], 3 * GRP
                            if f == 0:
                                if not (isinstance(gi, int) and gi == 0):
                                    dve.wait_ge(s.mrow_in, 64 * gi)
                        last = nc.vector.tensor_copy(dst, pTb[0:rows, :])
                        last.then_inc(s.T_out, 1)
                        return
                    n = item[1]
                    h, qt, part = UNITS[n]
                    dve.wait_ge(s.unit_mm, NU * gi + n + 1)
                    w = (qt + 1) * P
                    w = min(w, 1024) if part == 0 else w - 1024
                    nc.vector.reduce_max(mx[:, part, h, qt:qt + 1], pM[:, 0:w], AX.X).then_inc(s.unit_max, 1)

                def chunk(gi, c, cnt, after):
                    dve.wait_ge(s.pv, NS_ * gi + after + 2)
                    nc.vector.tensor_copy(oS[:, :], pO[:, :]).then_inc(s.o_out, 1)

                def chunk_put(gi, c, cnt):
                    t0, g = group(gi)
                    dve.wait_ge(s.T_mm, cnt.t)
                    cnt.t += 1
                    o = pT[:, :].rearrange("p (k h d) -> p k h d", k=4, h=GRP)
                    nc.vector.reciprocal(den[:, :, :], o[:, :, :, HD]).then_inc(s.den_out, 1)
                    dve.wait_ge(s.den_out, CH * gi + c + 1)
                    nc.vector.tensor_tensor(
                        QKV[:, bass.ds(t0 + 4 * c, 4), bass.ds(g * GRP * HD, GRP * HD)].rearrange("p k (h d) -> p k h d", d=HD),
                        o[:, :, :, 0:HD], den[:, :, :].unsqueeze(3).to_broadcast([P, 4, GRP, HD]),
                        ALU.mult).then_inc(s.T_out, 1)

                class Cnt:
                    def __init__(self, t):
                        self.t = t

                def one(gi, par, more):
                    cnt = Cnt(1 + NT + (NT + CH) * gi)
                    for n in range(NS_):
                        extra = [x for x in BESIDE[n]] if more else []
                        for x in extra:
                            beside(x, gi + 1, 1 - par, cnt)
                        if n and KSTEPS[n][1] == 0:
                            chunk_put(gi, KSTEPS[n][0] - 1, cnt)
                        if n + 1 < NS_ and KSTEPS[n + 1][1] == 0:
                            chunk(gi, KSTEPS[n][0], cnt, n + 1)
                    chunk(gi, CH - 1, cnt, NS_)
                    chunk_put(gi, CH - 1, cnt)
                cnt = Cnt(1)
                for item in background():
                    beside(item, 0, 0, cnt)
                with dve.Fori(0, NG // 2 - 1) as i:
                    for k in range(2):
                        one(2 * i + k, k, True)
                one(NG - 2, 0, True)
                one(NG - 1, 1, False)


CAP = B * L + P
MAXT = 2 * B * L // P + E
NTAB = MAXT + 2


def stage7(nc, sb, ps, sem, env, base_env):
    v, u = Names(env), base_env
    x1, ident, ones, QKV = u.x1, u.ident, u.ones, v.QKV
    G = 4
    with ExitStack() as ctx:
        stats = sb("stats7", [P, G, 6], F32, ctx)
        mv = sb("mv7", [P, G, 2], F32, ctx)
        rstd = sb("rstd7", [P, 4, G], F32, ctx)
        sq = sb("sq7", [P, G], F32, ctx)
        junk = sb("junk7", [P, G, H], F32, ctx)
        xl = sb("xl7", [P, G, H], F32, ctx)
        x2 = sb("x27", [P, G, H], F32, ctx)
        h2 = sb("h27", [P, G, H], F32, ctx)
        at = sb("at7", [P, 2, 2, H], F32, ctx)
        aT = sb("aT7", [P, 2, 2, C, P], F32, ctx)
        hT = sb("hT7", [P, 2, 2, C, P], F32, ctx)
        tri = sb("tri", [P, P], F32, ctx)
        iota_i = sb("iota_i7", [P, E], I32, ctx)
        iota8 = sb("iota8", [P, E], F32, ctx)
        iotap_i = sb("iotap_i", [P, 1], I32, ctx)
        iotap = sb("iotap", [P, 1], F32, ctx)
        lg = sb("lg", [P, G, E], F32, ctx)
        pr = sb("pr", [P, G, E], F32, ctx)
        ex = sb("ex7", [P, G, E], F32, ctx)
        red = sb("red7", [P, 4, G], F32, ctx)
        top = sb("top7", [P, G, 8], F32, ctx)
        topi = sb("topi7", [P, G, 8], U32, ctx)
        topf = sb("topf7", [P, G, 2], F32, ctx)
        hot = sb("hot7", [P, 2, G, E], F32, ctx)
        both = sb("both7", [P, G, E], F32, ctx)
        place = sb("place7", [P, G, E], F32, ctx)
        picked = sb("picked7", [P, 2, G, E], F32, ctx)
        slotf = sb("slotf7", [P, G, 2], F32, ctx)
        slot_now = sb("slot_now", [P, G, 2], I32, ctx)
        carry = sb("carry", [P, G + 1, E], F32, ctx)
        pT = ps("pT7", [P, 2, 2, C, P], F32, ctx)
        pX = ps("pX7", [P, 2, 512], F32, ctx)
        pL = ps("pL7", [P, 512], F32, ctx)
        pR = ps("pR7", [P, 512], F32, ctx)
        names = ("consts", "consts2", "tri_in", "stats", "mv", "eps1", "rstd1", "xl", "x2", "square", "eps2", "rstd2", "h",
                 "resid", "at_in", "aT_mm", "aT_out", "proj", "hT_mm", "hT_out", "logits", "ex", "chain", "both_in", "ranks",
                 "slots", "kept", "tab_chain", "tab_ready", "zero_in", "padded")
        s = Names({n: sem("r_" + n) for n in names})
        scattered = [sem(f"r_scattered{k}") for k in range(G)]
        NCH = 29
        PICKED = 17
        with nc.Block() as block:
            @block.gpsimd
            def _(pool):
                nc.gpsimd.iota(iota_i[:, :], pattern=[[1, E]], base=0, channel_multiplier=0).then_inc(s.consts, 1)
                nc.gpsimd.iota(iotap_i[:, :], pattern=[[0, 1]], base=0, channel_multiplier=1).then_inc(s.consts, 1)
                nc.gpsimd.memset(tri[:, :], 1.0).then_inc(s.consts, 1)
                nc.gpsimd.iota(v.jrow_i[:, :], pattern=[[1, NTAB]], base=0, channel_multiplier=0).then_inc(s.consts, 1)
                pool.wait_ge(s.consts, 4)
                nc.gpsimd.tensor_copy(v.jrow[:, :], v.jrow_i[:, :]).then_inc(s.consts2, 1)
                nc.gpsimd.tensor_copy(iota8[:, :], iota_i[:, :]).then_inc(s.consts2, 1)
                nc.gpsimd.tensor_copy(iotap[:, :], iotap_i[:, :]).then_inc(s.consts2, 1)
                nc.gpsimd.affine_select(out=tri[:, :], in_=tri[:, :], compare_op=ALU.is_gt, fill=0.0, base=0,
                                        pattern=[[1, P]], channel_multiplier=-1).then_inc(s.tri_in, 1)
                with pool.Fori(0, T // G) as i:
                    wait_apart(pool, s.mv, G * i + G)
                    nc.gpsimd.tensor_scalar(rstd[:, 0, :], mv[:, :, 1], 1e-5, None, ALU.add).then_inc(s.eps1, 1)
                    pool.wait_ge(s.eps1, i + 1)
                    nc.gpsimd.tensor_tensor(rstd[:, 1, :], rstd[:, 0, :], u.halfpow[:, :].to_broadcast([P, G]),
                                            ALU.pow).then_inc(s.rstd1, 1)
                    wait_apart(pool, s.square, G * i + G)
                    nc.gpsimd.tensor_scalar(rstd[:, 2, :], sq[:, :], 1.0 / H, 1e-5, ALU.mult, ALU.add).then_inc(s.eps2, 1)
                    pool.wait_ge(s.eps2, i + 1)
                    nc.gpsimd.tensor_tensor(rstd[:, 3, :], rstd[:, 2, :], u.halfpow[:, :].to_broadcast([P, G]),
                                            ALU.pow).then_inc(s.rstd2, 1)
                    nc.gpsimd.tensor_tensor(x1[:, bass.ds(G * i, G), :], x1[:, bass.ds(G * i, G), :], x2[:, :, :],
                                            ALU.add).then_inc(s.resid, 1)
                    pool.wait_ge(s.h, G * i + G)
                    wait_apart(pool, s.slots, i + 1)
                    for k in range(G):
                        for a in range(2):
                            nc.gpsimd.indirect_dma_start(
                                out=v.queue[:, :], out_offset=bass.IndirectOffsetOnAxis(ap=slot_now[:, k, a:a + 1], axis=0),
                                in_=h2[:, k, :], in_offset=None).then_inc(scattered[k], 16)
                    for k in range(G):
                        pool.wait_ge(scattered[k], 32 * i + 32)
                pool.wait_ge(s.tab_ready, 1)
                nc.gpsimd.memset(h2[:, 0, :], 0.0).then_inc(s.zero_in, 1)
                pool.wait_ge(s.zero_in, 1)
                for e in range(E):
                    nc.gpsimd.indirect_dma_start(
                        out=v.queue[:, :], out_offset=bass.IndirectOffsetOnAxis(ap=v.pad_rows[:, e:e + 1], axis=0),
                        in_=h2[:, 0, :], in_offset=None).then_inc(s.padded, 16)
                pool.wait_ge(s.padded, 16 * E)

            @block.tensor
            def _(pe):
                pe.wait_ge(s.tri_in, 1)
                pe.sem_inc(s.aT_mm, 2)
                pe.sem_inc(s.proj, 4)
                pe.sem_inc(s.hT_mm, 2)
                pe.sem_inc(s.logits, 1)
                with pe.Fori(0, T // G) as i:
                    for g in range(2):
                        pe.wait_ge(s.at_in, 2 * i + g + 1)
                        pe.wait_ge(s.hT_out, 2 * i + g + 1)
                        for k in range(2):
                            for c in range(C):
                                last = nc.tensor.transpose(pT[:, g, k, c, :], at[:, g, k, c * P:(c + 1) * P], ident[:, :])
                        last.then_inc(s.aT_mm, 1)
                    for g in range(2):
                        pe.wait_ge(s.aT_out, 2 * i + g + 1)
                        for k in range(2):
                            pe.wait_ge(s.x2, 4 * i + 2 * g + k + 1)
                            for c in range(C):
                                last = nc.tensor.matmul(pX[:, k, 0:H], aT[:, g, k, c, :], v.woT[:, c, :],
                                                        start=(c == 0), stop=(c == C - 1))
                            last.then_inc(s.proj, 1)
                    for g in range(2):
                        pe.wait_ge(s.h, G * i + 2 * g + 2)
                        for k in range(2):
                            for c in range(C):
                                last = nc.tensor.transpose(pT[:, g, k, c, :], h2[:, 2 * g + k, c * P:(c + 1) * P], ident[:, :])
                        last.then_inc(s.hT_mm, 1)
                    for g in range(2):
                        pe.wait_ge(s.hT_out, 2 * i + g + 3)
                        for k in range(2):
                            n = E * (2 * g + k)
                            for c in range(C):
                                last = nc.tensor.matmul(pL[:, n:n + E], hT[:, g, k, c, :], v.gwT[:, c, :],
                                                        start=(c == 0), stop=(c == C - 1))
                    last.then_inc(s.logits, 1)
                    pe.wait_ge(s.chain, NCH * i + PICKED)
                    b2 = both[:, :, :].rearrange("p k e -> p (k e)")
                    nc.tensor.matmul(pR[:, 0:G * E], tri[:, :], b2, start=True, stop=True)
                    nc.tensor.matmul(pR[:, G * E:2 * G * E], ones[:, :], b2, start=True, stop=True).then_inc(s.ranks, 1)

            @block.scalar
            def _(act):
                act.sem_inc(s.hT_out, 2)
                with act.Fori(0, T // G) as i:
                    for g in range(2):
                        act.wait_ge(s.aT_mm, 2 * i + g + 1)
                        nc.scalar.copy(at[:, g], QKV[:, bass.ds(G * i + 2 * g, 2), 0:H]).then_inc(s.at_in, 1)
                    for g in range(2):
                        act.wait_ge(s.aT_mm, 2 * i + g + 3)
                        act.wait_ge(s.proj, 4 * i + 2 * g + 2)
                        nc.scalar.copy(aT[:, g], pT[:, g]).then_inc(s.aT_out, 1)
                    for g in range(2):
                        act.wait_ge(s.hT_mm, 2 * i + g + 3)
                        act.wait_ge(s.logits, i + 1)
                        nc.scalar.copy(hT[:, g], pT[:, g]).then_inc(s.hT_out, 1)
                    act.wait_ge(s.chain, NCH * i + 2)
                    nc.scalar.activation(ex[:, :, :], pr[:, :, :], ACT.Exp).then_inc(s.ex, 1)

            @block.vector
            def _(dve):
                ch = Chain(dve, s.chain)
                dve.sem_inc(s.x2, 2)
                dve.wait_ge(s.consts2, 3)
                nc.vector.memset(carry[:, :, :], 0.0).then_inc(s.kept, 1)
                dve.wait_ge(s.kept, 1)

                def bc(ap):
                    return ap.unsqueeze(2).to_broadcast([P, G, E])
                with dve.Fori(0, T // G) as i:
                    ch.at(NCH * i)
                    for k in range(G):
                        nc.vector.bn_stats(stats[:, k, :], x1[:, G * i + k, :]).then_inc(s.stats, 1)
                    for k in range(G):
                        wait_apart(dve, s.stats, G * i + k + 1)
                        nc.vector.bn_aggr(mv[:, k, :], stats[:, k, :]).then_inc(s.mv, 1)
                    dve.wait_ge(s.mv, G * i + G)
                    dve.wait_ge(s.rstd1, i + 1)
                    for k in range(G):
                        nc.vector.tensor_scalar(xl[:, k, :], x1[:, G * i + k, :], mv[:, k, 0:1], rstd[:, 1, k:k + 1],
                                                ALU.subtract, ALU.mult).then_inc(s.xl, 1)
                    for k in range(G):
                        dve.wait_ge(s.xl, G * i + k + 1)
                        dve.wait_ge(s.proj, G * i + k + 5)
                        nc.vector.tensor_tensor(x2[:, k, :], xl[:, k, :], pX[:, k % 2, 0:H], ALU.add).then_inc(s.x2, 1)
                    for k in range(G):
                        dve.wait_ge(s.x2, G * i + k + 3)
                        nc.vector.tensor_tensor_reduce(junk[:, k, :], x2[:, k, :], x2[:, k, :], 1.0, 0.0, ALU.mult, ALU.add,
                                                       sq[:, k:k + 1]).then_inc(s.square, 1)
                    dve.wait_ge(s.rstd2, i + 1)
                    for k in range(G):
                        nc.vector.scalar_tensor_tensor(out=h2[:, k, :], in0=x2[:, k, :], scalar=rstd[:, 3, k:k + 1],
                                                       in1=v.ln2_b[:, :], op0=ALU.mult, op1=ALU.mult).then_inc(s.h, 1)
                    dve.wait_ge(s.logits, i + 2)
                    lgp = pL[:, 0:G * E].rearrange("p (k e) -> p k e", e=E)
                    ch.link(nc.vector.reduce_max(red[:, 0, :], lgp, AX.X))
                    nc.vector.tensor_tensor(pr[:, :, :], lgp, bc(red[:, 0, :]), ALU.subtract).then_inc(s.chain, 1)
                    ch.k += 1
                    dve.wait_ge(s.ex, i + 1)
                    ch.link(nc.vector.reduce_sum(red[:, 1, :], ex[:, :, :], AX.X))
                    ch.link(nc.vector.reciprocal(red[:, 2, :], red[:, 1, :]))
                    ch.link(nc.vector.tensor_tensor(lg[:, :, :], ex[:, :, :], bc(red[:, 2, :]), ALU.mult), apart=True)
                    for k in range(G):
                        ch.link(nc.vector.max(top[:, k, :], lg[:, k, :]), apart=True)
                        ch.link(nc.vector.max_index(topi[:, k, :], top[:, k, :], lg[:, k, :]), apart=True)
                    ch.link(nc.vector.tensor_copy(topf[:, :, :], topi[:, :, 0:2]))
                    for a in range(2):
                        ch.link(nc.vector.tensor_tensor(hot[:, a], iota8[:, :].unsqueeze(1).to_broadcast([P, G, E]),
                                                        bc(topf[:, :, a]), ALU.is_equal))
                    ch.link(nc.vector.tensor_tensor(both[:, :, :], hot[:, 0], hot[:, 1], ALU.add))
                    assert ch.k == PICKED
                    ch.link(nc.vector.tensor_tensor(red[:, 3, :], top[:, :, 0], top[:, :, 1], ALU.add))
                    ch.link(nc.vector.reciprocal(red[:, 3, :], red[:, 3, :]))
                    ch.link(nc.vector.tensor_tensor(v.weights[:, bass.ds(G * i, G), :], top[:, :, 0:2],
                                                    red[:, 3, :].unsqueeze(2).to_broadcast([P, G, 2]), ALU.mult))
                    dve.wait_ge(s.ranks, i + 1)
                    for k in range(G):
                        ch.link(nc.vector.tensor_tensor(carry[:, k + 1, :], carry[:, k, :],
                                                        pR[:, (G + k) * E:(G + k + 1) * E], ALU.add))
                    ch.link(nc.vector.tensor_tensor(place[:, :, :], carry[:, 0:G, :],
                                                    pR[:, 0:G * E].rearrange("p (k e) -> p k e", e=E), ALU.add))
                    ch.link(nc.vector.scalar_tensor_tensor(out=place[:, :, :],
                                                           in0=iota8[:, :].unsqueeze(1).to_broadcast([P, G, E]),
                                                           scalar=float(CAP), in1=place[:, :, :], op0=ALU.mult, op1=ALU.add))
                    ch.link(nc.vector.tensor_tensor(picked[:, :, :, :], hot[:, :, :, :],
                                                    place[:, :, :].unsqueeze(1).to_broadcast([P, 2, G, E]), ALU.mult))
                    ch.link(nc.vector.reduce_sum(slotf[:, :, :].rearrange("p k a -> p a k"), picked[:, :, :, :], AX.X))
                    ch.link(nc.vector.tensor_copy(carry[:, 0, :], carry[:, G, :]))
                    assert ch.k == NCH, ch.k
                    nc.vector.tensor_copy(v.rowsf[:, bass.ds(G * i, G), :], slotf[:, :, :]).then_inc(s.kept, 1)
                    nc.vector.tensor_copy(slot_now[:, :, :], slotf[:, :, :]).then_inc(s.slots, 1)
                    for k in range(G):
                        dve.wait_ge(scattered[k], 32 * i + 32)
                    dve.wait_ge(s.resid, i + 1)
                tc = Chain(dve, s.tab_chain)
                dve.wait_ge(s.kept, 1 + T // G)
                tables(nc, tc, v, s, carry, iota8, iotap)
                nc.vector.tensor_copy(v.pad_rows[:, :], v.padf[:, :]).then_inc(s.tab_ready, 1)
                dve.wait_ge(s.tab_ready, 1)


def tables(nc, tc, v, s, carry, iota8, iotap):
    count = carry[:, 0, :]
    tc.link(nc.vector.scalar_tensor_tensor(out=v.padf[:, :], in0=iota8[:, :], scalar=float(CAP), in1=count,
                                           op0=ALU.mult, op1=ALU.add))
    tc.link(nc.vector.tensor_scalar(v.padf[:, :], v.padf[:, :], iotap[:, :], None, ALU.add))
    tc.link(nc.vector.tensor_scalar(v.steps[:, :], v.jrow[:, 0:T], float(P), None, ALU.mult))
    tc.link(nc.vector.tensor_tensor(v.cmp[:, :, 0:T], v.steps[:, :].unsqueeze(1).to_broadcast([P, E, T]),
                                    count.unsqueeze(2).to_broadcast([P, E, T]), ALU.is_lt))
    tc.link(nc.vector.reduce_sum(v.ntile[:, :], v.cmp[:, :, 0:T], AX.X))
    tc.link(nc.vector.tensor_copy(v.ends[:, 0:1], v.ntile[:, 0:1]))
    for e in range(1, E):
        tc.link(nc.vector.tensor_tensor(v.ends[:, e:e + 1], v.ends[:, e - 1:e], v.ntile[:, e:e + 1], ALU.add))
    total = v.ends[:, E - 1:E]
    tc.link(nc.vector.tensor_scalar(v.lastt[:, :], total, -1.0, None, ALU.add))
    tc.link(nc.vector.tensor_scalar(v.jc[:, :], v.jrow[:, :], v.lastt[:, :], None, ALU.min))
    tc.link(nc.vector.tensor_tensor(v.cmp[:, :, :], v.jc[:, :].unsqueeze(1).to_broadcast([P, E, NTAB]),
                                    v.ends[:, :].unsqueeze(2).to_broadcast([P, E, NTAB]), ALU.is_ge))
    tc.link(nc.vector.reduce_sum(v.ej[:, :], v.cmp[:, :, :].rearrange("p e j -> p j e"), AX.X))
    tc.link(nc.vector.tensor_tensor(v.cmp[:, :, :], v.cmp[:, :, :], v.ntile[:, :].unsqueeze(2).to_broadcast([P, E, NTAB]),
                                    ALU.mult))
    tc.link(nc.vector.reduce_sum(v.before[:, :], v.cmp[:, :, :].rearrange("p e j -> p j e"), AX.X))
    tc.link(nc.vector.tensor_tensor(v.rowf[:, :], v.jc[:, :], v.before[:, :], ALU.subtract))
    tc.link(nc.vector.tensor_scalar(v.rowf[:, :], v.rowf[:, :], float(P), None, ALU.mult))
    tc.link(nc.vector.scalar_tensor_tensor(out=v.rowf[:, :], in0=v.ej[:, :], scalar=float(CAP), in1=v.rowf[:, :],
                                           op0=ALU.mult, op1=ALU.add))
    tc.link(nc.vector.tensor_copy(v.tile_expert[:, :], v.ej[:, :]))
    tc.link(nc.vector.tensor_copy(v.tile_in[:, :], v.rowf[:, :]))
    for e in range(1, E):
        tc.link(nc.vector.tensor_scalar(v.lastt[:, :], v.ntile[:, e - 1:e], -float(P), float(CAP), ALU.mult, ALU.add))
        tc.link(nc.vector.tensor_scalar(v.shift[:, :, :], v.rowsf[:, :, :], float(e * CAP), v.lastt[:, :], ALU.is_ge,
                                        ALU.mult))
        tc.link(nc.vector.tensor_tensor(v.shifts[:, :, :], v.shifts[:, :, :] if e > 1 else v.rowsf[:, :, :],
                                        v.shift[:, :, :], ALU.subtract))
    tc.link(nc.vector.tensor_copy(v.rows[:, :, :], v.shifts[:, :, :]))


def stage8(nc, sb, ps, sem, env, base_env):
    v, u = Names(env), base_env
    ident = u.ident
    NR = E * 2 * FFN // P
    NR2 = E * H // P
    with ExitStack() as ctx:
        w13T = sb("w13T", [P, C, E * 2 * FFN], F32, ctx)
        w2T = sb("w2T", [P, FFN // P, E * H], F32, ctx)
        with ExitStack() as c1:
            raw = sb("raw8", [P, 4, 512], F32, c1)
            pW = ps("pW8", [P, 4, 512], F32, c1)
            raw_in = [sem(f"m_raw_in{k}") for k in range(4)]
            wT_mm, wT_out = sem("m_wT_mm"), sem("m_wT_out")
            w13v = u.w13.rearrange("e (r a p) h -> p (e r) a h", a=2, p=P)
            w2v = u.w2.rearrange("e (r p) f -> p (e r) f", p=P)
            N1, N2 = NR // 2, NR2
            with nc.Block() as block:
                @block.sync
                def _(sp):
                    with sp.Fori(0, N1 // 4) as i:
                        for k in range(4):
                            sp.wait_ge(wT_mm, 4 * i + k + 1)
                            sp.dma_start(raw[:, k, :].rearrange("p (a h) -> p a h", a=2),
                                         w13v[:, 4 * i + k, :, :]).then_inc(raw_in[k], 16)
                    with sp.Fori(0, N2 // 4) as i:
                        for k in range(4):
                            sp.wait_ge(wT_mm, N1 + 4 * i + k + 1)
                            sp.dma_start(raw[:, k, :], w2v[:, 4 * i + k, :]).then_inc(raw_in[k], 16)

                @block.tensor
                def _(pe):
                    pe.sem_inc(wT_mm, 4)
                    with pe.Fori(0, (N1 + N2) // 4) as i:
                        for k in range(4):
                            pe.wait_ge(raw_in[k], 16 * i + 16)
                            pe.wait_ge(wT_out, 4 * i + k + 1)
                            for a in range(4):
                                last = nc.tensor.transpose(pW[:, k, a * P:(a + 1) * P], raw[:, k, a * P:(a + 1) * P],
                                                           ident[:, :])
                            last.then_inc(wT_mm, 1)

                @block.vector
                def _(dve):
                    dve.sem_inc(wT_out, 4)
                    with dve.Fori(0, N1 // 4) as i:
                        for k in range(4):
                            dve.wait_ge(wT_mm, 4 * i + k + 5)
                            nc.vector.tensor_copy(
                                w13T[:, :, bass.ds((4 * i + k) * 2 * P, 2 * P)].rearrange("p c (a n) -> p a c n", a=2),
                                pW[:, k, :].rearrange("p (a c n) -> p a c n", a=2, c=C)).then_inc(wT_out, 1)
                    with dve.Fori(0, N2 // 4) as i:
                        for k in range(4):
                            dve.wait_ge(wT_mm, N1 + 4 * i + k + 5)
                            nc.vector.tensor_copy(w2T[:, :, bass.ds((4 * i + k) * P, P)],
                                                  pW[:, k, :].rearrange("p (a n) -> p a n", a=4)).then_inc(wT_out, 1)
        with ExitStack() as c2:
            FC = FFN // P
            xq = sb("xq8", [P, 2, H], F32, c2)
            xqT = sb("xqT8", [P, 2, C, P], F32, c2)
            sil = sb("sil8", [P, 2, FFN], F32, c2)
            gg = sb("gg8", [P, 2, FFN], F32, c2)
            gT = sb("gT8", [P, 2, FC, P], F32, c2)
            y = sb("y8", [P, 2, H], F32, c2)
            pH = ps("pH8", [P, 2, 2, FFN], F32, c2)
            pX = ps("pX8", [P, C, P], F32, c2)
            pG = ps("pG8", [P, FC, P], F32, c2)
            pY = ps("pY8", [P, H], F32, c2)
            xq_in = [sem(f"m_xq_in{k}") for k in range(2)]
            y_put = [sem(f"m_y_put{k}") for k in range(2)]
            names = ("x_T", "x_out", "up", "sil", "gated", "g_T", "g_out", "down", "y_out")
            s = Names({n: sem("m_" + n) for n in names})
            with nc.Block() as block:
                @block.sync
                def _(sp):
                    def load(j, k, first=False):
                        row = sp.value_load(v.tile_in[0:1, bass.ds(j, 1)], min_val=0, max_val=E * CAP - P)
                        if not first:
                            sp.wait_ge(s.x_T, j - 1)
                        sp.dma_start(xq[:, k, :], v.queue[bass.ds(row, P), :]).then_inc(xq_in[k], 16)
                    load(0, 0, True)
                    load(1, 1, True)
                    with sp.Fori(0, MAXT // 2) as i:
                        for k in range(2):
                            j = 2 * i + k
                            load(j + 2, k)
                            sp.wait_ge(s.y_out, j + 2)
                            sp.dma_start(v.results[bass.ds(j * P, P), :], y[:, k, :]).then_inc(y_put[k], 16)
                            wait_apart(sp, y_put[k], 16 * i + 16)
                    for k in range(2):
                        sp.wait_ge(xq_in[k], 8 * (MAXT + 2))

                @block.tensor
                def _(pe):
                    def turn(j, k, i):
                        pe.wait_ge(xq_in[k], 16 * i + 16)
                        pe.wait_ge(s.x_out, j + 1)
                        for c in range(C):
                            last = nc.tensor.transpose(pX[:, c, :], xq[:, k, c * P:(c + 1) * P], ident[:, :])
                        last.then_inc(s.x_T, 1)

                    def up(j, k):
                        e = pe.value_load(v.tile_expert[0:1, bass.ds(j, 1)], min_val=0, max_val=E - 1)
                        pe.wait_ge(s.x_out, j + 2)
                        pe.wait_ge(s.gated, j + 1)
                        for a in range(2):
                            for c in range(C):
                                last = nc.tensor.matmul(pH[:, k, a, :], xqT[:, k, c, :],
                                                        w13T[:, c, bass.ds(e * (2 * FFN) + a * FFN, FFN)],
                                                        start=(c == 0), stop=(c == C - 1))
                        last.then_inc(s.up, 1)

                    def down(j, k):
                        e = pe.value_load(v.tile_expert[0:1, bass.ds(j, 1)], min_val=0, max_val=E - 1)
                        pe.wait_ge(s.gated, j + 3)
                        pe.wait_ge(s.g_out, j + 1)
                        for f in range(FC):
                            last = nc.tensor.transpose(pG[:, f, :], gg[:, k, f * P:(f + 1) * P], ident[:, :])
                        last.then_inc(s.g_T, 1)
                        pe.wait_ge(s.g_out, j + 2)
                        pe.wait_ge(s.y_out, j + 1)
                        for f in range(FC):
                            last = nc.tensor.matmul(pY[:, :], gT[:, k, f, :], w2T[:, f, bass.ds(e * H, H)],
                                                    start=(f == 0), stop=(f == FC - 1))
                        last.then_inc(s.down, 1)
                    turn(0, 0, 0)
                    up(0, 0)
                    turn(1, 1, 0)
                    with pe.Fori(0, MAXT // 2) as i:
                        for k in range(2):
                            j = 2 * i + k
                            up(j + 1, 1 - k)
                            turn(j + 2, k, i + 1)
                            down(j, k)

                @block.scalar
                def _(act):
                    act.sem_inc(s.x_out, 1)
                    act.sem_inc(s.y_out, 1)

                    def turned(j, k, first=False):
                        act.wait_ge(s.x_T, j + 1)
                        if not first:
                            act.wait_ge(s.up, j - 1)
                        nc.scalar.copy(xqT[:, k], pX[:, :, :]).then_inc(s.x_out, 1)
                    turned(0, 0, True)
                    turned(1, 1, True)
                    with act.Fori(0, MAXT // 2) as i:
                        for k in range(2):
                            j = 2 * i + k
                            act.wait_ge(s.up, j + 1)
                            act.wait_ge(s.gated, j + 1)
                            nc.scalar.activation(sil[:, k, :], pH[:, k, 0, :], ACT.Silu).then_inc(s.sil, 1)
                            turned(j + 2, k)
                            act.wait_ge(s.down, j + 1)
                            nc.scalar.copy(y[:, k, :], pY[:, :]).then_inc(s.y_out, 1)

                @block.vector
                def _(dve):
                    dve.sem_inc(s.gated, 2)
                    dve.sem_inc(s.g_out, 1)
                    with dve.Fori(0, MAXT // 2) as i:
                        for k in range(2):
                            j = 2 * i + k
                            dve.wait_ge(s.sil, j + 1)
                            nc.vector.tensor_tensor(gg[:, k, :], sil[:, k, :], pH[:, k, 1, :], ALU.mult).then_inc(s.gated, 1)
                            dve.wait_ge(s.g_T, j + 1)
                            nc.vector.tensor_copy(gT[:, k], pG[:, :, :]).then_inc(s.g_out, 1)


def stage9(nc, sb, ps, sem, env, base_env):
    v, u = Names(env), base_env
    G = 4
    with ExitStack() as ctx:
        rows_now = sb("rows_now", [P, G, 2], I32, ctx)
        yy = sb("yy9", [P, G, 2, H], F32, ctx)
        o = sb("o9", [P, G, H], F32, ctx)
        got = [sem(f"f_got{k}") for k in range(G)]
        put = [sem(f"f_put{k}") for k in range(G)]
        s = Names({n: sem("f_" + n) for n in ("rows", "half", "sum")})
        out_rows = u.out.rearrange("b (t p) h -> p (b t) h", p=P)
        with nc.Block() as block:
            @block.gpsimd
            def _(pool):
                with pool.Fori(0, T // G) as i:
                    for k in range(G):
                        nc.gpsimd.tensor_copy(rows_now[:, k, :], v.rows[:, G * i + k, :]).then_inc(s.rows, 1)
                    for k in range(G):
                        pool.wait_ge(s.rows, G * i + k + 1)
                        pool.wait_ge(s.half, G * i + k + 1)
                        wait_apart(pool, s.sum, G * i + k + 1)
                        for a in range(2):
                            nc.gpsimd.indirect_dma_start(
                                out=yy[:, k, a, :], out_offset=None, in_=v.results[:, :],
                                in_offset=bass.IndirectOffsetOnAxis(ap=rows_now[:, k, a:a + 1], axis=0)).then_inc(got[k], 16)
                    for k in range(G):
                        pool.wait_ge(got[k], 32 * i + 32)

            @block.vector
            def _(dve):
                dve.sem_inc(s.half, G)
                dve.sem_inc(s.sum, G)
                with dve.Fori(0, T // G) as i:
                    for k in range(G):
                        t = G * i + k
                        dve.wait_ge(got[k], 32 * i + 32)
                        nc.vector.scalar_tensor_tensor(out=yy[:, k, 0, :], in0=yy[:, k, 0, :],
                                                       scalar=v.weights[:, t, 0:1], in1=u.x1[:, t, :], op0=ALU.mult,
                                                       op1=ALU.add).then_inc(s.half, 1)
                    for k in range(G):
                        t = G * i + k
                        dve.wait_ge(s.half, t + G + 1)
                        nc.vector.scalar_tensor_tensor(out=u.x1[:, t, :], in0=yy[:, k, 1, :],
                                                       scalar=v.weights[:, t, 1:2], in1=yy[:, k, 0, :], op0=ALU.mult,
                                                       op1=ALU.add).then_inc(s.sum, 1)

            @block.sync
            def _(sp):
                with sp.Fori(0, T // G) as i:
                    for k in range(G):
                        sp.wait_ge(s.sum, G * i + k + 1 + G)
                        sp.dma_start(out_rows[:, G * i + k, :], u.x1[:, G * i + k, :]).then_inc(put[k], 16)
                    for k in range(G):
                        wait_apart(sp, put[k], 16 * i + 16)


_INS = ["attn_" + n for n in ("hidden_states", "Wq", "bq", "Wk", "bk", "Wv", "bv", "Wo", "bo", "Wg", "bg", "Wc", "bc", "Ws",
                              "bs")] + ["ffn_" + n for n in ("ln1_w", "ln2_w", "wqkv", "wo", "gate_w", "w13", "w2")]


def rotary_tables():
    inv = (1.0 / np.power(np.float32(10000.0), np.arange(0, HD, 2, dtype=np.float32) / np.float32(HD))).astype(np.float32)
    angle = np.arange(L, dtype=np.float32)[:, None] * inv[None, :]
    return np.cos(angle).astype(np.float32), np.sin(angle).astype(np.float32)


def kernel(**inputs):
    import concourse.bacc as _bacc
    from concourse.bass_utils import run_bass_kernel_spmd as _run

    nc = _bacc.Bacc("TRN2", target_bir_lowering=False, num_devices=1)
    arrays, args = {}, []
    for name in _INS:
        arrays[f"in_{name}_dram"] = np.ascontiguousarray(inputs["L0_" + name])
    arrays["in_cos_dram"], arrays["in_sin_dram"] = rotary_tables()
    for name, a in arrays.items():
        args.append(nc.dram_tensor(name, a.shape, mybir.dt.from_np(a.dtype), kind="ExternalInput").ap())
    args.append(nc.dram_tensor("out_0_dram", (B, L, H), F32, kind="ExternalOutput").ap())
    build(nc, *args)
    r = _run(nc, [arrays], core_ids=[0])
    return r.results[0]["out_0_dram"]
```

```python
from contextlib import ExitStack

import concourse.bass as bass
import numpy as np
from concourse import mybir

F32 = mybir.dt.float32
BF16 = mybir.dt.bfloat16
I32 = mybir.dt.int32
U32 = mybir.dt.uint32
ALU = mybir.AluOpType
ACT = mybir.ActivationFunctionType
AX = mybir.AxisListType

P = 128
B, L, H = 2, 2048, 256
C = H // P
T = B * L // P
TB = L // P
RATIO = 4
NBLK = L // RATIO
CT = NBLK // P
SEL = 128
WIN = 64
SCALE = 0.25
NH, NKV, HD = 16, 4, 16
GRP = NH // NKV
QKVW = (NH + 2 * NKV) * HD
E = 8
FFN = 512
NEG = -1e30


class Names(dict):

    def __getattr__(self, name):
        return self[name]


class Chain:

    def __init__(self, eng, sem, base=0):
        self.eng, self.sem, self.base, self.k = eng, sem, base, 0

    def at(self, base):
        self.base, self.k = base, 0

    def link(self, ins, apart=False):
        self.k += 1
        ins.then_inc(self.sem, 1)
        if apart:
            wait_apart(self.eng, self.sem, self.base + self.k)
        else:
            self.eng.wait_ge(self.sem, self.base + self.k)


PASSED = []


def wait_apart(eng, sem, value):
    eng.wait_ge(sem, value)
    eng.sem_inc(PASSED[0], 1)


def build(nc, x, Wq, bq, Wk, bk, Wv, bv, Wo, bo, Wg, bg, Wc, bc, Ws, bs,
          ln1_w, ln2_w, wqkv, wo, gate_w, w13, w2, cos_t, sin_t, out):
    with ExitStack() as whole:
        def sb(name, shape, dt=F32, ctx=whole):
            return ctx.enter_context(nc.sbuf_tensor(name, shape, dt))

        def ps(name, shape, dt=F32, ctx=whole):
            return ctx.enter_context(nc.psum_tensor(name, shape, dt))

        stage_sems = []

        def sem(name):
            stage_sems.append(nc.alloc_semaphore(name=name))
            return stage_sems[-1]

        def free_semaphores():
            nc.clear_and_free_semaphores(list(stage_sems))
            stage_sems.clear()
            nc.all_engine_barrier()

        PASSED[:] = [nc.alloc_semaphore(name="passed")]
        ident = sb("ident", [P, P])
        ones = sb("ones", [P, P])
        x1 = sb("x1", [P, T, H])
        halfpow = sb("halfpow", [P, 1])
        x_rows = x.rearrange("b (t p) h -> p (b t) h", p=P)

        with ExitStack() as layer1:
            def sb1(name, shape, dt=F32):
                return sb(name, shape, dt, layer1)
            base = sb1("base", [P, T, H])
            xnT = sb1("xnT", [P, C, B * L])
            wq_s, wk_s, wv_s = (sb1(n, [P, C, H]) for n in ("wq_s", "wk_s", "wv_s"))
            wo_s = sb1("wo_s", [P, 3 * C, H])
            wc_s = sb1("wc_s", [P, RATIO * C, H])
            wgs = sb1("wgs", [P, C, 4])
            bgs = sb1("bgs", [1, 4])
            bqk = sb1("bqk", [P, 3, C])
            bv_r = sb1("bv_r", [1, H])
            bo_b = sb1("bo_b", [P, H])
            GS = sb1("GS", [P, T, 4])

            stage1(nc, layer1, sb, ps, sem, locals())
            stage23(nc, layer1, sb, ps, sem, locals())
            stage4(nc, layer1, sb, ps, sem, locals())
            free_semaphores()
        stages_layer2(nc, whole, sb, ps, sem, locals())


def stage1(nc, layer, sb, ps, sem, env):
    v = Names(env)
    x_rows, x1, base, xnT, ident, ones, GS = v.x_rows, v.x1, v.base, v.xnT, v.ident, v.ones, v.GS
    G = 4
    with ExitStack() as ctx:
        stats = sb("stats", [P, 2, G, 6], F32, ctx)
        mv = sb("mv", [P, 2, G, 2], F32, ctx)
        rstd = sb("rstd", [P, 2, G], F32, ctx)
        xf = sb("xf", [P, G, H], F32, ctx)
        xTf = sb("xTf", [P, 2, 2, C, P], F32, ctx)
        pT = ps("pT", [P, 2, 2, C, P], F32, ctx)
        pG = ps("pG", [P, 512], F32, ctx)
        x_in = [sem(f"x_in{k}") for k in range(G)]
        w_in, small_in, const0, const1 = sem("w_in"), sem("small_in"), sem("const0"), sem("const1")
        stats_v, stats_done, var_eps, rstd_done, normed, base_copied = (sem(n) for n in
            ("stats_v", "stats_done", "var_eps", "rstd_done", "normed", "base_copied"))
        transposed, xT_done, xnT_copied, gates_mm, gates_out = (sem(n) for n in
            ("transposed", "xT_done", "xnT_copied", "gates_mm", "gates_out"))
        with nc.Block() as block:
            @block.sync
            def _(sp):
                def load(i, k):
                    sp.dma_start(x1[:, i * G + k, :], x_rows[:, i * G + k, :]).then_inc(x_in[k], 16)
                for k in range(G):
                    load(0, k)
                with sp.Fori(1, T // G) as i:
                    for k in range(G):
                        sp.wait_ge(x_in[k], 16 * i)
                        load(i, k)

            @block.scalar
            def _(act):
                act.dma_start(v.wgs[:, :, 0:3], v.Wg.rearrange("(c p) n -> p c n", p=P)).then_inc(small_in, 16)
                act.dma_start(v.wgs[:, :, 3:4], v.Ws.rearrange("(c p) n -> p c n", p=P), allow_slow_non_contiguous=True).then_inc(small_in, 16)
                act.dma_start(v.bgs[:, 0:3], v.bg.rearrange("(a n) -> a n", a=1)).then_inc(small_in, 16)
                act.dma_start(v.bgs[:, 3:4], v.bs.rearrange("(a n) -> a n", a=1)).then_inc(small_in, 16)
                for dst, src in ((v.wc_s, v.Wc), (v.wq_s, v.Wq), (v.wk_s, v.Wk), (v.wv_s, v.Wv), (v.wo_s, v.Wo)):
                    act.dma_start(dst[:, :, :], src.rearrange("(c p) n -> p c n", p=P)).then_inc(w_in, 16)
                for n, src in enumerate((v.bq, v.bk, v.bc)):
                    act.dma_start(v.bqk[:, n, :], src.rearrange("(c p) -> p c", p=P), allow_slow_non_contiguous=True).then_inc(w_in, 16)
                act.dma_start(v.bv_r[:, :], v.bv.rearrange("(a n) -> a n", a=1)).then_inc(w_in, 16)
                act.dma_start(v.bo_b[:, :], v.bo.partition_broadcast(P)).then_inc(w_in, 16)
                with act.Fori(0, T // G) as i:
                    for g in range(2):
                        act.wait_ge(transposed, 2 * i + g + 3)
                        act.wait_ge(gates_mm, 2 * i + g + 1)
                        act.wait_ge(xnT_copied, 2 * i + g + 1)
                        nc.scalar.copy(xTf[:, g], pT[:, g]).then_inc(xT_done, 1)
                act.wait_ge(w_in, 160)

            @block.gpsimd
            def _(pool):
                nc.gpsimd.memset(ident[:, :], 0.0).then_inc(const0, 1)
                nc.gpsimd.memset(ones[:, :], 1.0).then_inc(const0, 1)
                nc.gpsimd.memset(v.halfpow[:, :], -0.5).then_inc(const0, 1)
                pool.wait_ge(const0, 3)
                nc.gpsimd.affine_select(out=ident[:, :], in_=ident[:, :], compare_op=ALU.not_equal, fill=1.0,
                                        base=0, pattern=[[-1, P]], channel_multiplier=1).then_inc(const1, 1)
                pool.sem_inc(xnT_copied, 2)
                pool.sem_inc(base_copied, 1)
                with pool.Fori(0, T // G) as i:
                    wait_apart(pool, stats_done, G * i + G)
                    nc.gpsimd.tensor_scalar(rstd[:, 0, :], mv[:, 0, :, 1], 1e-5, None, ALU.add).then_inc(var_eps, 1)
                    pool.wait_ge(var_eps, i + 1)
                    nc.gpsimd.tensor_tensor(rstd[:, 1, :], rstd[:, 0, :], v.halfpow[:, :].to_broadcast([P, G]),
                                            ALU.pow).then_inc(rstd_done, 1)
                    wait_apart(pool, normed, G * i + G)
                    nc.gpsimd.tensor_copy(base[:, bass.ds(i * G, G), :], xf[:, :, :]).then_inc(base_copied, 1)
                    for g in range(2):
                        wait_apart(pool, xT_done, 2 * i + g + 1)
                        nc.gpsimd.tensor_copy(
                            xnT[:, :, bass.ds((i * G + 2 * g) * P, 2 * P)].rearrange("p c (t n) -> p c t n", t=2),
                            xTf[:, g].rearrange("p t c n -> p c t n")).then_inc(xnT_copied, 1)

            @block.vector
            def _(dve):
                with dve.Fori(0, T // G) as i:
                    for k in range(G):
                        dve.wait_ge(x_in[k], 16 * i + 16)
                        nc.vector.bn_stats(stats[:, 0, k, :], x1[:, i * G + k, :]).then_inc(stats_v, 1)
                    for k in range(G):
                        wait_apart(dve, stats_v, G * i + k + 1)
                        nc.vector.bn_aggr(mv[:, 0, k, :], stats[:, 0, k, :]).then_inc(stats_done, 1)
                    dve.wait_ge(rstd_done, i + 1)
                    dve.wait_ge(stats_done, G * i + G)
                    dve.wait_ge(transposed, 2 * i + 2)
                    dve.wait_ge(base_copied, i + 1)
                    for k in range(G):
                        nc.vector.tensor_scalar(xf[:, k, :], x1[:, i * G + k, :], mv[:, 0, k, 0:1],
                                                rstd[:, 1, k:k + 1], ALU.subtract, ALU.mult).then_inc(normed, 1)
                    dve.wait_ge(gates_mm, 2 * i + 4)
                    nc.vector.tensor_copy(GS[:, bass.ds(i * G, G), :],
                                          pG[:, 0:4 * G].rearrange("p (t n) -> p t n", n=4)).then_inc(gates_out, 1)

            @block.tensor
            def _(pe):
                pe.wait_ge(const1, 1)
                pe.wait_ge(small_in, 64)
                pe.sem_inc(transposed, 2)
                pe.sem_inc(gates_mm, 2)
                with pe.Fori(0, T // G) as i:
                    for g in range(2):
                        pe.wait_ge(normed, G * i + 2 * g + 2)
                        for k in range(2):
                            for c in range(C):
                                last = nc.tensor.transpose(pT[:, g, k, c, :],
                                                           xf[:, 2 * g + k, c * P:(c + 1) * P], ident[:, :])
                        last.then_inc(transposed, 1)
                    for g in range(2):
                        pe.wait_ge(xT_done, 2 * i + g + 1)
                        for k in range(2):
                            n = 4 * (2 * g + k)
                            nc.tensor.matmul(pG[:, n:n + 4], xTf[:, g, k, 0, :], v.wgs[:, 0, :], start=True, stop=False)
                            nc.tensor.matmul(pG[:, n:n + 4], xTf[:, g, k, 1, :], v.wgs[:, 1, :], start=False, stop=False)
                            last = nc.tensor.matmul(pG[:, n:n + 4], ones[0:1, :], v.bgs[:, :], start=False, stop=True)
                        last.then_inc(gates_mm, 1)


def stage23(nc, layer, sb, ps, sem, env):
    v = Names(env)
    base, xnT, ident, ones, GS = v.base, v.xnT, v.ident, v.ones, v.GS
    with ExitStack() as ctx:
        compT, qcT, kcT = (sb(n, [P, B, C, NBLK], F32, ctx) for n in ("compT", "qcT", "kcT"))
        Vc = sb("Vc", [P, B, CT, H], F32, ctx)
        PC = sb("PC", [P, TB, B], F32, ctx)
        with ExitStack() as c2:
            S32 = sb("S32", [T, P], F32, c2)
            srow = sb("srow", [B, L], F32, c2)
            work = sb("work", [B, L], F32, c2)
            above, equal, cum = work, sb("equal", [B, L], F32, c2), sb("cum", [B, L], F32, c2)
            ones_row = sb("ones_row", [B, L], F32, c2)
            best = sb("best", [B, 8], F32, c2)
            need = sb("need", [B, 2], F32, c2)
            eg = sb("eg", [P, T, 3], F32, c2)
            gsum = sb("gsum", [P, T], F32, c2)
            pJ = ps("pJ", [P, 2, 512], F32, c2)
            pS32 = ps("pS32", [T, P], F32, c2)
            pPC = ps("pPC", [P, TB, B], F32, c2)
            proj_mm, proj_out, s32_T, s32_out, srow_in, gate_exp, dve2, place_ready, place_T, place_out = (sem(n) for n in (
                "proj_mm", "proj_out", "s32_T", "s32_out", "srow_in", "gate_exp", "dve2", "place_ready", "place_T",
                "place_out"))
            with nc.Block() as block:
                @block.sync
                def _(sp):
                    sp.wait_ge(s32_out, 1)
                    for b in range(B):
                        sp.dma_start(srow[b:b + 1, :].rearrange("a (t n) -> a t n", n=P),
                                     S32[b * TB:(b + 1) * TB, :]).then_inc(srow_in, 16)
                    sp.wait_ge(srow_in, 16 * B)

                @block.tensor
                def _(pe):
                    nc.tensor.transpose(pS32[:, :], GS[:, :, 3], ident[:, :]).then_inc(s32_T, 1)
                    n = 0

                    def bank():
                        if n >= 2:
                            pe.wait_ge(proj_out, n - 1)
                        return pJ[:, n % 2]
                    for b in range(B):
                        for m in range(C):
                            o = bank()
                            for k in range(RATIO * C):
                                r, c = k // C, k % C
                                last = nc.tensor.matmul(o, v.wc_s[:, k, m * P:(m + 1) * P],
                                                        xnT[:, c, bass.ds(b * L + r, NBLK, RATIO)],
                                                        start=(k == 0), stop=(k == RATIO * C - 1))
                            last.then_inc(proj_mm, 1)
                            n += 1
                    for b in range(B):
                        pe.wait_ge(proj_out, 2 * b + 2)
                        for w in (v.wq_s, v.wk_s):
                            for m in range(C):
                                o = bank()
                                for c in range(C):
                                    last = nc.tensor.matmul(o, w[:, c, m * P:(m + 1) * P], compT[:, b, c, :],
                                                            start=(c == 0), stop=(c == C - 1))
                                last.then_inc(proj_mm, 1)
                                n += 1
                    for b in range(B):
                        for i in range(CT):
                            o = bank()[:, 0:H]
                            for c in range(C):
                                nc.tensor.matmul(o, compT[:, b, c, i * P:(i + 1) * P], v.wv_s[:, c, :],
                                                 start=(c == 0), stop=False)
                            nc.tensor.matmul(o, ones[0:1, :], v.bv_r[:, :], start=False, stop=True).then_inc(proj_mm, 1)
                            n += 1
                    pe.wait_ge(place_ready, 1)
                    for t in range(TB):
                        last = nc.tensor.transpose(pPC[:, t, :], srow[:, t * P:(t + 1) * P], ident[0:B, 0:B])
                    last.then_inc(place_T, 1)

                @block.scalar
                def _(act):
                    nc.scalar.activation(eg[:, :, :], GS[:, :, 0:3], ACT.Exp, scale=-1.0).then_inc(gate_exp, 1)
                    n = 0
                    for b in range(B):
                        for m in range(C):
                            act.wait_ge(proj_mm, n + 1)
                            nc.scalar.activation(compT[:, b, m, :], pJ[:, n % 2], ACT.Identity,
                                                 bias=v.bqk[:, 2, m:m + 1]).then_inc(proj_out, 1)
                            n += 1
                    for b in range(B):
                        for w, dst in ((0, qcT), (1, kcT)):
                            for m in range(C):
                                act.wait_ge(proj_mm, n + 1)
                                nc.scalar.activation(dst[:, b, m, :], pJ[:, n % 2], ACT.Identity,
                                                     bias=v.bqk[:, w, m:m + 1]).then_inc(proj_out, 1)
                                n += 1
                    for b in range(B):
                        for i in range(CT):
                            act.wait_ge(proj_mm, n + 1)
                            nc.scalar.copy(Vc[:, b, i, :], pJ[:, n % 2, 0:H]).then_inc(proj_out, 1)
                            n += 1

                @block.vector
                def _(dve):
                    ch = Chain(dve, dve2)
                    dve.wait_ge(s32_T, 1)
                    nc.vector.tensor_copy(S32[:, :], pS32[:, :]).then_inc(s32_out, 1)
                    dve.wait_ge(gate_exp, 1)
                    ch.link(nc.vector.tensor_scalar(eg[:, :, :], eg[:, :, :], 1.0, None, ALU.add))
                    ch.link(nc.vector.reciprocal(eg[:, :, :], eg[:, :, :]))
                    ch.link(nc.vector.reduce_sum(gsum[:, :], eg[:, :, :], AX.X))
                    ch.link(nc.vector.tensor_scalar(gsum[:, :], gsum[:, :], 1e-6, None, ALU.add))
                    ch.link(nc.vector.reciprocal(gsum[:, :], gsum[:, :]))
                    ch.link(nc.vector.tensor_tensor(GS[:, :, 0:3], eg[:, :, :],
                                                    gsum[:, :].unsqueeze(2).to_broadcast([P, T, 3]), ALU.mult))
                    ch.link(nc.vector.memset(ones_row[:, :], 1.0))
                    dve.wait_ge(srow_in, 16 * B)
                    ch.link(nc.vector.tensor_copy(work[:, :], srow[:, :]))
                    done = ch.k
                    with dve.Fori(0, SEL // 8) as i:
                        ch.at(2 * i + done)
                        ch.link(nc.vector.max(best[:, :], work[:, :]), apart=True)
                        ch.link(nc.vector.match_replace(work[:, :], best[:, :], work[:, :], -3e38), apart=True)
                    ch.at(done + 2 * (SEL // 8))
                    least = best[:, 7:8]
                    ch.link(nc.vector.tensor_scalar(above[:, :], srow[:, :], least, 0.0, ALU.is_gt, ALU.add,
                                                    accum_out=need[:, 0:1]))
                    ch.link(nc.vector.tensor_scalar(equal[:, :], srow[:, :], least, None, ALU.is_equal))
                    ch.link(nc.vector.tensor_scalar(need[:, 1:2], need[:, 0:1], -1.0, float(SEL), ALU.mult, ALU.add))
                    ch.link(nc.vector.tensor_tensor_scan(cum[:, :], ones_row[:, :], equal[:, :], 0.0, ALU.mult, ALU.add))
                    ch.link(nc.vector.scalar_tensor_tensor(out=equal[:, :], in0=cum[:, :], scalar=need[:, 1:2],
                                                           in1=equal[:, :], op0=ALU.is_le, op1=ALU.mult))
                    ch.link(nc.vector.tensor_tensor(above[:, :], above[:, :], equal[:, :], ALU.add))
                    ch.link(nc.vector.tensor_tensor_scan(cum[:, :], ones_row[:, :], above[:, :], 0.0, ALU.mult, ALU.add))
                    nc.vector.tensor_tensor(srow[:, :], cum[:, :], above[:, :], ALU.mult).then_inc(place_ready, 1)
                    dve.wait_ge(place_T, 1)
                    nc.vector.tensor_scalar(PC[:, :, :], pPC[:, :, :], -1.0, None, ALU.add).then_inc(place_out, 1)
                    dve.wait_ge(place_out, 1)

        with ExitStack() as c3:
            iota_i = sb("iota_i", [P, P], I32, c3)
            iota_f = sb("iota_f", [P, P], F32, c3)
            OH = sb("OH", [P, B, TB, P], F32, c3)
            selT = sb("selT", [P, B, C, SEL], F32, c3)
            qksT = sb("qksT", [P, B, 2, C, SEL], F32, c3)
            Vs = sb("Vs", [P, B, H], F32, c3)
            nmax = sb("nmax", [P, 2, 2], F32, c3)
            rs = sb("rs", [P, 2, 2], F32, c3)
            prob = sb("prob", [P, 2, 512], F32, c3)
            probT = sb("probT", [P, 2, 4, P], F32, c3)
            ctxT = sb("ctxT", [P, 2, C, P], F32, c3)
            pS = ps("pS3", [P, 2, 512], F32, c3)
            pPT = ps("pPT3", [P, 4, P], F32, c3)
            pC = ps("pC3", [P, C, P], F32, c3)
            pO = ps("pO3", [P, H], F32, c3)
            pX = ps("pX3", [P, 512], F32, c3)
            pV = ps("pV3", [P, H], F32, c3)
            iota_in, iota_done, onehot, sel_mm, sel_out, selqk_mm, selqk_out, selv_mm, selv_out, bo_in = (sem(n) for n in (
                "iota_in", "iota_done", "onehot", "sel_mm", "sel_out", "selqk_mm", "selqk_out", "selv_mm", "selv_out",
                "bo_in"))
            scores, rowmax, negmax, expd, rowsum, share, weighed, probT_mm, probT_out, ctx_mm, ctx_out, out_mm, added = (
                sem("a_" + n) for n in ("scores", "rowmax", "negmax", "expd", "rowsum", "share", "weighed", "probT_mm",
                                        "probT_out", "ctx_mm", "ctx_out", "out_mm", "added"))
            tiles = [(b, i, CT, 0) for b in range(B) for i in range(CT)] + [(b, 0, 1, 1) for b in range(B)]
            N = len(tiles)
            with nc.Block() as block:
                @block.gpsimd
                def _(pool):
                    nc.gpsimd.iota(iota_i[:, :], pattern=[[1, P]], base=0, channel_multiplier=0).then_inc(iota_in, 1)
                    pool.wait_ge(iota_in, 1)
                    nc.gpsimd.tensor_copy(iota_f[:, :], iota_i[:, :]).then_inc(iota_done, 1)
                    pool.wait_ge(sel_mm, B)
                    for t in list(range(0, TB * B, CT)):
                        last = nc.gpsimd.tensor_tensor(base[:, t:t + CT, :], base[:, t:t + CT, :],
                                                       v.bo_b[:, :].unsqueeze(1).to_broadcast([P, CT, H]), ALU.add)
                        last.then_inc(bo_in, 1)

                @block.tensor
                def _(pe):
                    for b in range(B):
                        pe.wait_ge(onehot, TB * (b + 1))
                        if b:
                            pe.wait_ge(sel_out, b)
                        for c in range(C):
                            for t in range(TB):
                                last = nc.tensor.matmul(pX[:, c * P:(c + 1) * P], base[:, b * TB + t, c * P:(c + 1) * P],
                                                        OH[:, b, t, :], start=(t == 0), stop=(t == TB - 1))
                        last.then_inc(sel_mm, 1)
                    for b in range(B):
                        pe.wait_ge(sel_out, b + 1 if b == 0 else B)
                        if b == 0:
                            pe.wait_ge(sel_out, B)
                        else:
                            pe.wait_ge(selqk_out, 2 * C * b)
                            pe.wait_ge(selv_out, b)
                        for w, W in ((0, v.wq_s), (1, v.wk_s)):
                            for m in range(C):
                                for c in range(C):
                                    last = nc.tensor.matmul(pX[:, (w * C + m) * P:(w * C + m + 1) * P],
                                                            W[:, c, m * P:(m + 1) * P], selT[:, b, c, :],
                                                            start=(c == 0), stop=(c == C - 1))
                        last.then_inc(selqk_mm, 1)
                        for c in range(C):
                            nc.tensor.matmul(pV[:, :], selT[:, b, c, :], v.wv_s[:, c, :], start=(c == 0), stop=False)
                        nc.tensor.matmul(pV[:, :], ones[0:1, :], v.bv_r[:, :], start=False, stop=True).then_inc(selv_mm, 1)

                    def tile_scores(n):
                        b, i, kt, sel = tiles[n]
                        if n >= 2:
                            pe.wait_ge(expd, n - 1)
                        if sel:
                            pe.wait_ge(selqk_out, 2 * C * (b + 1))
                        for c in range(C):
                            q = qksT[:, b, 0, c, :] if sel else qcT[:, b, c, i * P:(i + 1) * P]
                            k = qksT[:, b, 1, c, :] if sel else kcT[:, b, c, :]
                            last = nc.tensor.matmul(pS[:, n % 2, 0:kt * P], q, k, start=(c == 0), stop=(c == C - 1))
                        last.then_inc(scores, 1)

                    def tile_transposes(n):
                        pe.wait_ge(weighed, n + 1)
                        if n >= 1:
                            pe.wait_ge(probT_out, n)
                        for k in range(tiles[n][2]):
                            last = nc.tensor.transpose(pPT[:, k, :], prob[:, n % 2, k * P:(k + 1) * P], ident[:, :])
                        last.then_inc(probT_mm, 1)

                    def tile_context(n):
                        b, i, kt, sel = tiles[n]
                        pe.wait_ge(probT_out, n + 1)
                        if n >= 1:
                            pe.wait_ge(ctx_out, n)
                        if sel:
                            pe.wait_ge(selv_out, b + 1)
                        for m in range(C):
                            for k in range(kt):
                                val = Vs[:, b, m * P:(m + 1) * P] if sel else Vc[:, b, k, m * P:(m + 1) * P]
                                last = nc.tensor.matmul(pC[:, m, :], val, probT[:, n % 2, k, :], start=(k == 0),
                                                        stop=(k == kt - 1))
                        last.then_inc(ctx_mm, 1)

                    def tile_output(n):
                        sel = tiles[n][3]
                        pe.wait_ge(ctx_out, n + 1)
                        if n >= 1:
                            pe.wait_ge(added, n)
                        for m in range(C):
                            last = nc.tensor.matmul(pO[:, :], ctxT[:, n % 2, m, :], v.wo_s[:, sel * C + m, :],
                                                    start=(m == 0), stop=(m == C - 1))
                        last.then_inc(out_mm, 1)
                    tile_scores(0)
                    for n in range(N):
                        if n + 1 < N:
                            tile_scores(n + 1)
                        tile_transposes(n)
                        if n >= 1:
                            tile_output(n - 1)
                        tile_context(n)
                    tile_output(N - 1)

                @block.scalar
                def _(act):
                    for b in range(B):
                        act.wait_ge(sel_mm, b + 1)
                        nc.scalar.copy(selT[:, b], pX[:, 0:C * P].rearrange("p (c n) -> p c n", n=P)).then_inc(sel_out, 1)
                    for b in range(B):
                        act.wait_ge(selqk_mm, b + 1)
                        for w in range(2):
                            for m in range(C):
                                nc.scalar.activation(qksT[:, b, w, m, :], pX[:, (w * C + m) * P:(w * C + m + 1) * P],
                                                     ACT.Identity, bias=v.bqk[:, w, m:m + 1]).then_inc(selqk_out, 1)
                        act.wait_ge(selv_mm, b + 1)
                        nc.scalar.copy(Vs[:, b, :], pV[:, :]).then_inc(selv_out, 1)

                    def tile_exp(n):
                        w = tiles[n][2] * P
                        act.wait_ge(negmax, n + 1)
                        if n >= 2:
                            act.wait_ge(probT_mm, n - 1)
                        nc.scalar.activation(prob[:, n % 2, 0:w], pS[:, n % 2, 0:w], ACT.Exp, scale=SCALE,
                                             bias=nmax[:, n % 2, 1:2], accum_out=rs[:, n % 2, 0:1]).then_inc(expd, 1)

                    def tile_ctx(n):
                        act.wait_ge(ctx_mm, n + 1)
                        if n >= 2:
                            act.wait_ge(out_mm, n - 1)
                        nc.scalar.copy(ctxT[:, n % 2], pC[:, :, :]).then_inc(ctx_out, 1)
                    tile_exp(0)
                    for n in range(N):
                        if n + 1 < N:
                            tile_exp(n + 1)
                        tile_ctx(n)

                @block.vector
                def _(dve):
                    dve.wait_ge(iota_done, 1)
                    for b in range(B):
                        for t in range(TB):
                            nc.vector.tensor_scalar(OH[:, b, t, :], iota_f[:, :], PC[:, t, b:b + 1], None,
                                                    ALU.is_equal).then_inc(onehot, 1)

                    def tile_max(n):
                        w = tiles[n][2] * P
                        dve.wait_ge(scores, n + 1)
                        nc.vector.reduce_max(nmax[:, n % 2, 0:1], pS[:, n % 2, 0:w], AX.X).then_inc(rowmax, 1)
                        dve.wait_ge(rowmax, n + 1)
                        nc.vector.tensor_scalar(nmax[:, n % 2, 1:2], nmax[:, n % 2, 0:1], -SCALE, None,
                                                ALU.mult).then_inc(negmax, 1)

                    def tile_share(n):
                        b, i, kt, sel = tiles[n]
                        w = kt * P
                        dve.wait_ge(expd, n + 1)
                        nc.vector.reciprocal(rs[:, n % 2, 1:2], rs[:, n % 2, 0:1]).then_inc(rowsum, 1)
                        dve.wait_ge(rowsum, n + 1)
                        nc.vector.tensor_scalar(prob[:, n % 2, 0:w], prob[:, n % 2, 0:w], rs[:, n % 2, 1:2],
                                                GS[:, b * TB + i, sel:sel + 1], ALU.mult, ALU.mult).then_inc(weighed, 1)
                        dve.wait_ge(probT_mm, n + 1)
                        if n >= 2:
                            dve.wait_ge(ctx_mm, n - 1)
                        nc.vector.tensor_copy(probT[:, n % 2, 0:kt, :], pPT[:, 0:kt, :]).then_inc(probT_out, 1)

                    def tile_add(n):
                        b, i, _, _ = tiles[n]
                        t = b * TB + i
                        dve.wait_ge(out_mm, n + 1)
                        dve.wait_ge(bo_in, t // CT + 1)
                        if n:
                            dve.wait_ge(added, n)
                        nc.vector.tensor_tensor(base[:, t, :], base[:, t, :], pO[:, :], ALU.add).then_inc(added, 1)
                    tile_max(0)
                    for n in range(N):
                        if n + 1 < N:
                            tile_max(n + 1)
                        tile_share(n)
                        if n >= 1:
                            tile_add(n - 1)
                    tile_add(N - 1)


def stage4(nc, layer, sb, ps, sem, env):
    v = Names(env)
    base, xnT, ident, ones, GS, x1 = v.base, v.xnT, v.ident, v.ones, v.GS, v.x1
    HALF = WIN // 2
    with ExitStack() as ctx:
        xs = sb("xs4", [P, 2, C, 2, WIN], F32, ctx)
        qkT = sb("qkT4", [P, 2, 2, C, P], F32, ctx)
        V = sb("V4", [P, 2, H], F32, ctx)
        nmax = sb("nmax4", [P, 2, 2], F32, ctx)
        rs = sb("rs4", [P, 2, 2], F32, ctx)
        prob = sb("prob4", [P, 2, WIN], F32, ctx)
        block_p = sb("block_p4", [P, 2, P], F32, ctx)
        probT = sb("probT4", [P, 2, P], F32, ctx)
        ctxT = sb("ctxT4", [P, 2, C, P], F32, ctx)
        z = sb("z4", [P, 2, H], F32, ctx)
        stats = sb("stats4", [P, 2, 6], F32, ctx)
        mv = sb("mv4", [P, 2, 2], F32, ctx)
        rstd = sb("rstd4", [P, 2, 3], F32, ctx)
        pQK = ps("pQK4", [P, 2, 2, C, P], F32, ctx)
        pV = ps("pV4", [P, H], F32, ctx)
        pS = ps("pS4", [P, 512], F32, ctx)
        pPT = ps("pPT4", [P, 512], F32, ctx)
        pC = ps("pC4", [P, C, P], F32, ctx)
        pO = ps("pO4", [P, H], F32, ctx)
        names = ("xs_in", "qk_mm", "qk_out", "v_mm", "v_out", "scores", "rowmax", "negmax", "expd", "rowsum", "weighed",
                 "probT_mm", "probT_out", "ctx_mm", "ctx_out", "out_mm", "z_sum", "z_stats", "z_mv", "z_rstd", "pow_in",
                 "z_norm", "x1_out", "zero4")
        s = Names({n: sem("w_" + n) for n in names})

        def pipelined(eng, step, body=2):
            for t in (0, 1):
                step(t, t, t)
            with eng.Fori(1, T // 2) as i:
                for k in range(2):
                    step(2 * i + k, k, 2)

        with nc.Block() as block:
            @block.gpsimd
            def _(pool):
                nc.gpsimd.memset(block_p[:, :, :], 0.0).then_inc(s.zero4, 1)

                def take(t, off, k, late):
                    if late:
                        pool.wait_ge(s.qk_mm, t - 1)
                        wait_apart(pool, s.v_mm, t - 1)
                    for w in range(2):
                        nc.gpsimd.tensor_copy(xs[:, k, :, w, :], xnT[:, :, bass.ds(off + w * HALF, WIN)]).then_inc(s.xs_in, 1)

                def root(t, k, late):
                    wait_apart(pool, s.z_mv, t + 1)
                    nc.gpsimd.tensor_scalar(rstd[:, k, 0:1], mv[:, k, 1:2], 0.25, 1e-6, ALU.mult, ALU.add).then_inc(s.pow_in, 1)
                    pool.wait_ge(s.pow_in, t + 1)
                    if late:
                        pool.wait_ge(s.x1_out, t - 1)
                    nc.gpsimd.tensor_tensor(rstd[:, k, 1:2], rstd[:, k, 0:1], v.halfpow[:, :], ALU.pow).then_inc(s.z_rstd, 1)
                take(0, 0, 0, False)
                take(1, WIN, 1, False)
                take(2, 2 * WIN, 0, True)
                root(0, 0, False)
                take(3, 3 * WIN, 1, True)
                root(1, 1, False)
                with pool.Fori(2, TB // 2) as i:
                    for k in range(2):
                        take(2 * i + k, i * 2 * WIN + k * WIN, k, True)
                        root(2 * i - 2 + k, k, True)
                with pool.Fori(0, TB // 2) as i:
                    for k in range(2):
                        take(TB + 2 * i + k, L + i * 2 * WIN + k * WIN, k, True)
                        root(TB - 2 + 2 * i + k, k, True)
                for t in (T - 2, T - 1):
                    root(t, t % 2, True)

            @block.tensor
            def _(pe):
                def project(t, k, first):
                    pe.wait_ge(s.xs_in, 2 * t + 2)
                    if first >= 2:
                        pe.wait_ge(s.qk_out, 4 * t - 4)
                    x_k = xs[:, k].rearrange("p c w n -> p c (w n)")
                    for w, W in ((0, v.wq_s), (1, v.wk_s)):
                        for m in range(C):
                            for c in range(C):
                                last = nc.tensor.matmul(pQK[:, k, w, m, :], W[:, c, m * P:(m + 1) * P], x_k[:, c, :],
                                                        start=(c == 0), stop=(c == C - 1))
                    last.then_inc(s.qk_mm, 1)
                    if first:
                        pe.wait_ge(s.v_out, t)
                    for c in range(C):
                        nc.tensor.matmul(pV[:, :], x_k[:, c, :], v.wv_s[:, c, :], start=(c == 0), stop=False)
                    nc.tensor.matmul(pV[:, :], ones[0:1, :], v.bv_r[:, :], start=False, stop=True).then_inc(s.v_mm, 1)

                def tile_scores(t, k, first):
                    pe.wait_ge(s.qk_out, 4 * t + 4)
                    if first:
                        pe.wait_ge(s.expd, t)
                    for w in range(2):
                        for c in range(C):
                            last = nc.tensor.matmul(pS[w * WIN:(w + 1) * WIN, 0:WIN],
                                                    qkT[:, k, 0, c, w * WIN:(w + 1) * WIN],
                                                    qkT[:, k, 1, c, w * WIN:(w + 1) * WIN],
                                                    start=(c == 0), stop=(c == C - 1))
                    last.then_inc(s.scores, 1)

                def tile_transposes(t, k, first):
                    pe.wait_ge(s.weighed, 2 * t + 2)
                    if first:
                        pe.wait_ge(s.probT_out, t)
                    nc.tensor.transpose(pPT[:, 0:P], block_p[:, k, :], ident[:, :]).then_inc(s.probT_mm, 1)

                def tile_context(t, k, first):
                    pe.wait_ge(s.probT_out, t + 1)
                    pe.wait_ge(s.v_out, t + 1)
                    if first:
                        pe.wait_ge(s.ctx_out, t)
                    for m in range(C):
                        last = nc.tensor.matmul(pC[:, m, :], V[:, k, m * P:(m + 1) * P], probT[:, k, :],
                                                start=True, stop=True)
                    last.then_inc(s.ctx_mm, 1)

                def tile_output(t, k, first):
                    pe.wait_ge(s.ctx_out, t + 1)
                    if first:
                        pe.wait_ge(s.z_sum, t)
                    for m in range(C):
                        last = nc.tensor.matmul(pO[:, :], ctxT[:, k, m, :], v.wo_s[:, 2 * C + m, :],
                                                start=(m == 0), stop=(m == C - 1))
                    last.then_inc(s.out_mm, 1)

                def step(t, k, first, before=True, after=True):
                    tile_scores(t, k, first)
                    if after:
                        project(t + 1, 1 - k, 2 if first == 2 else first + 1)
                    tile_transposes(t, k, first)
                    if before:
                        tile_output(t - 1, 1 - k, first if first == 2 else 0)
                    tile_context(t, k, first)
                project(0, 0, 0)
                step(0, 0, 0, before=False)
                step(1, 1, 1)
                with pe.Fori(1, T // 2 - 1) as i:
                    for k in range(2):
                        step(2 * i + k, k, 2)
                step(T - 2, 0, 2)
                step(T - 1, 1, 2, after=False)
                tile_output(T - 1, 1, 2)

            @block.scalar
            def _(act):
                def step(t, k, first):
                    act.wait_ge(s.qk_mm, t + 1)
                    if first >= 2:
                        act.wait_ge(s.scores, t - 1)
                    for w in range(2):
                        for m in range(C):
                            nc.scalar.activation(qkT[:, k, w, m, :], pQK[:, k, w, m, :], ACT.Identity,
                                                 bias=v.bqk[:, w, m:m + 1]).then_inc(s.qk_out, 1)
                    act.wait_ge(s.v_mm, t + 1)
                    if first >= 2:
                        act.wait_ge(s.ctx_mm, t - 1)
                    nc.scalar.copy(V[:, k, :], pV[:, :]).then_inc(s.v_out, 1)

                def soft(t, k, first):
                    act.wait_ge(s.negmax, t + 1)
                    if first >= 2:
                        act.wait_ge(s.weighed, 2 * t - 2)
                    nc.scalar.activation(prob[:, k, :], pS[:, 0:WIN], ACT.Exp, scale=SCALE,
                                         bias=nmax[:, k, 1:2], accum_out=rs[:, k, 0:1]).then_inc(s.expd, 1)

                def context(t, k, first):
                    act.wait_ge(s.ctx_mm, t + 1)
                    if first >= 2:
                        act.wait_ge(s.out_mm, t - 1)
                    nc.scalar.copy(ctxT[:, k], pC[:, :, :]).then_inc(s.ctx_out, 1)

                def turn(t, k, first, after=True):
                    soft(t, k, first)
                    if after:
                        step(t + 1, 1 - k, 2 if first >= 1 else 0)
                    context(t, k, first)
                step(0, 0, 0)
                turn(0, 0, 0)
                turn(1, 1, 1)
                with act.Fori(1, T // 2 - 1) as i:
                    for k in range(2):
                        turn(2 * i + k, k, 2)
                turn(T - 2, 0, 2)
                turn(T - 1, 1, 2, after=False)

            @block.vector
            def _(dve):
                dve.wait_ge(s.zero4, 1)

                def soft(t, k, first):
                    dve.wait_ge(s.scores, t + 1)
                    nc.vector.reduce_max(nmax[:, k, 0:1], pS[:, 0:WIN], AX.X).then_inc(s.rowmax, 1)
                    dve.wait_ge(s.rowmax, t + 1)
                    nc.vector.tensor_scalar(nmax[:, k, 1:2], nmax[:, k, 0:1], -SCALE, None, ALU.mult).then_inc(s.negmax, 1)

                def weigh(t, k, first):
                    dve.wait_ge(s.expd, t + 1)
                    nc.vector.reciprocal(rs[:, k, 1:2], rs[:, k, 0:1]).then_inc(s.rowsum, 1)
                    dve.wait_ge(s.rowsum, t + 1)
                    for w in range(2):
                        r = slice(w * WIN, (w + 1) * WIN)
                        nc.vector.tensor_scalar(block_p[r, k, w * WIN:(w + 1) * WIN], prob[r, k, :], rs[r, k, 1:2],
                                                GS[r, t, 2:3], ALU.mult, ALU.mult).then_inc(s.weighed, 1)
                    dve.wait_ge(s.probT_mm, t + 1)
                    if first >= 2:
                        dve.wait_ge(s.ctx_mm, t - 1)
                    nc.vector.tensor_copy(probT[:, k, :], pPT[:, 0:P]).then_inc(s.probT_out, 1)

                def finish(t, k, first):
                    dve.wait_ge(s.out_mm, t + 1)
                    nc.vector.tensor_tensor(z[:, k, :], base[:, t, :], pO[:, :], ALU.add).then_inc(s.z_sum, 1)
                    dve.wait_ge(s.z_sum, t + 1)
                    nc.vector.bn_stats(stats[:, k, :], z[:, k, :]).then_inc(s.z_stats, 1)
                    wait_apart(dve, s.z_stats, t + 1)
                    nc.vector.bn_aggr(mv[:, k, :], stats[:, k, :]).then_inc(s.z_mv, 1)

                def norm(t, k, first):
                    dve.wait_ge(s.z_rstd, t + 1)
                    nc.vector.tensor_scalar(z[:, k, :], z[:, k, :], mv[:, k, 0:1], 0.5, ALU.subtract,
                                            ALU.mult).then_inc(s.z_norm, 1)
                    dve.wait_ge(s.z_norm, t + 1)
                    nc.vector.scalar_tensor_tensor(out=x1[:, t, :], in0=z[:, k, :], scalar=rstd[:, k, 1:2],
                                                   in1=x1[:, t, :], op0=ALU.mult, op1=ALU.add).then_inc(s.x1_out, 1)

                def turn(t, k, first):
                    soft(t, k, first)
                    if first >= 2:
                        norm(t - 2, k, first)
                    weigh(t, k, first)
                    if first:
                        finish(t - 1, 1 - k, first)
                pipelined(dve, turn)
                norm(T - 2, 0, 2)
                finish(T - 1, 1, 2)
                norm(T - 1, 1, 2)


def stages_layer2(nc, whole, sb, ps, sem, env):
    v = Names(env)
    with ExitStack() as late:
        ln2_b = sb("ln2_b", [P, H], F32, late)
        woT = sb("woT", [P, C, H], F32, late)
        gwT = sb("gwT", [P, C, E], F32, late)
        weights = sb("weights", [P, T, 2], F32, late)
        rows = sb("rows", [P, T, 2], I32, late)
        rowsf, shift, shifts = (sb(n, [P, T, 2], F32, late) for n in ("rowsf", "shift", "shifts"))
        pad_rows = sb("pad_rows", [P, E], I32, late)
        jrow_i = sb("jrow_i", [P, NTAB], I32, late)
        jrow, jc, ej, before, rowf = (sb(n, [P, NTAB], F32, late) for n in ("jrow", "jc", "ej", "before", "rowf"))
        cmp = sb("cmp", [P, E, NTAB], F32, late)
        steps = sb("steps", [P, T], F32, late)
        padf, ntile, ends = (sb(n, [P, E], F32, late) for n in ("padf", "ntile", "ends"))
        lastt = sb("lastt", [P, 1], F32, late)
        tile_expert, tile_in = (sb(n, [P, NTAB], I32, late) for n in ("tile_expert", "tile_in"))
        queue = nc.dram_tensor("queue", [E * CAP, H], F32).ap()
        results = nc.dram_tensor("results", [MAXT * P, H], F32).ap()
        with ExitStack() as att:
            QKV = sb("QKV", [P, T, QKVW], F32, att)
            stage5(nc, sb, ps, sem, locals(), v)
            stage6(nc, sb, ps, sem, locals(), v)
            v.free_semaphores()
            stage7(nc, sb, ps, sem, locals(), v)
        stage8(nc, sb, ps, sem, locals(), v)
        stage9(nc, sb, ps, sem, locals(), v)


def stage5(nc, sb, ps, sem, env, base_env):
    v, u = Names(env), base_env
    x1, ident, ones = u.x1, u.ident, u.ones
    G = 4
    with ExitStack() as ctx:
        ln1_b = sb("ln1_b", [P, H], F32, ctx)
        wqkvT = sb("wqkvT", [P, C, QKVW], F32, ctx)
        raw = sb("raw5", [P, 6, H], F32, ctx)
        cosb = sb("cosb", [P, TB, HD // 2], F32, ctx)
        sinb = sb("sinb", [P, TB, HD // 2], F32, ctx)
        stats = sb("stats5", [P, G, 6], F32, ctx)
        mv = sb("mv5", [P, G, 2], F32, ctx)
        rstd = sb("rstd5", [P, 4, G], F32, ctx)
        sq = sb("sq5", [P, G], F32, ctx)
        junk = sb("junk5", [P, G, H], F32, ctx)
        xl = sb("xl5", [P, G, H], F32, ctx)
        h = sb("h5", [P, G, H], F32, ctx)
        hT = sb("hT5", [P, 2, 2, C, P], F32, ctx)
        qk = sb("qk5", [P, 2, 320], F32, ctx)
        byc = sb("byc5", [P, 2, 320], F32, ctx)
        bys = sb("bys5", [P, 2, 320], F32, ctx)
        pT = ps("pT5", [P, 2, 2, C, P], F32, ctx)
        pQ = ps("pQ5", [P, 2, 512], F32, ctx)
        names = ("raw_in", "small_in", "wT_mm", "wT_out", "stats", "mv", "eps1", "rstd1", "xl", "square", "eps2", "eps3",
                 "rstd2", "h", "hT_mm", "hT_out", "qkv_mm", "qk_out", "v_out", "turned", "byc", "bys")
        s = Names({n: sem("q_" + n) for n in names})
        nwT = (QKVW // P + C) * C + C
        with nc.Block() as block:
            @block.sync
            def _(sp):
                sp.dma_start(raw[:, 0:3, :], u.wqkv.rearrange("(t p) h -> p t h", p=P)).then_inc(s.raw_in, 16)
                sp.dma_start(raw[:, 3:5, :], u.wo.rearrange("(t p) h -> p t h", p=P)).then_inc(s.raw_in, 16)
                sp.dma_start(raw[0:E, 5, :], u.gate_w).then_inc(s.raw_in, 16)
                sp.dma_start(ln1_b[:, :], u.ln1_w.partition_broadcast(P)).then_inc(s.small_in, 16)
                sp.dma_start(v.ln2_b[:, :], u.ln2_w.partition_broadcast(P)).then_inc(s.small_in, 16)
                sp.dma_start(cosb[:, :, :], u.cos_t.rearrange("(t p) n -> p t n", p=P)).then_inc(s.small_in, 16)
                sp.dma_start(sinb[:, :, :], u.sin_t.rearrange("(t p) n -> p t n", p=P)).then_inc(s.small_in, 16)

            @block.tensor
            def _(pe):
                pe.wait_ge(s.raw_in, 48)
                for n in range(6):
                    rows = E if n == 5 else P
                    for c in range(C):
                        k = 2 * n + c
                        if k >= 2:
                            pe.wait_ge(s.wT_out, k - 1)
                        nc.tensor.transpose(pT[:, k % 2, 0, 0, 0:rows], raw[0:rows, n, c * P:(c + 1) * P],
                                            ident[0:rows, 0:rows]).then_inc(s.wT_mm, 1)
                pe.wait_ge(s.wT_out, 12)
                pe.sem_inc(s.hT_mm, 2)
                pe.sem_inc(s.qkv_mm, 2)
                with pe.Fori(0, T // G) as i:
                    for g in range(2):
                        pe.wait_ge(s.h, G * i + 2 * g + 2)
                        for k in range(2):
                            for c in range(C):
                                last = nc.tensor.transpose(pT[:, g, k, c, :], h[:, 2 * g + k, c * P:(c + 1) * P], ident[:, :])
                        last.then_inc(s.hT_mm, 1)
                    for g in range(2):
                        pe.wait_ge(s.hT_out, 2 * i + g + 1)
                        for k in range(2):
                            pe.wait_ge(s.v_out, 4 * i + 2 * g + k + 1)
                            pe.wait_ge(s.qk_out, 4 * i + 2 * g + k + 1)
                            for c in range(C):
                                last = nc.tensor.matmul(pQ[:, k, 0:QKVW], hT[:, g, k, c, :], wqkvT[:, c, :],
                                                        start=(c == 0), stop=(c == C - 1))
                            last.then_inc(s.qkv_mm, 1)

            @block.scalar
            def _(act):
                act.sem_inc(s.v_out, 2)
                act.sem_inc(s.qk_out, 2)
                with act.Fori(0, T // G) as i:
                    for g in range(2):
                        act.wait_ge(s.hT_mm, 2 * i + g + 3)
                        act.wait_ge(s.qkv_mm, 4 * i + 2 * g + 2)
                        nc.scalar.copy(hT[:, g], pT[:, g]).then_inc(s.hT_out, 1)
                    for g in range(2):
                        for k in range(2):
                            t = 4 * i + 2 * g + k
                            act.wait_ge(s.qkv_mm, t + 3)
                            act.wait_ge(s.turned, t + 1)
                            nc.scalar.copy(qk[:, k, :], pQ[:, k, 0:320]).then_inc(s.qk_out, 1)
                            nc.scalar.copy(v.QKV[:, t, 320:QKVW], pQ[:, k, 320:QKVW]).then_inc(s.v_out, 1)

            @block.gpsimd
            def _(pool):
                pool.sem_inc(s.turned, 2)
                with pool.Fori(0, T // G) as i:
                    wait_apart(pool, s.mv, G * i + G)
                    nc.gpsimd.tensor_scalar(rstd[:, 0, :], mv[:, :, 1], 1e-5, None, ALU.add).then_inc(s.eps1, 1)
                    pool.wait_ge(s.eps1, i + 1)
                    nc.gpsimd.tensor_tensor(rstd[:, 1, :], rstd[:, 0, :], u.halfpow[:, :].to_broadcast([P, G]),
                                            ALU.pow).then_inc(s.rstd1, 1)
                    wait_apart(pool, s.square, G * i + G)
                    nc.gpsimd.tensor_scalar(rstd[:, 2, :], sq[:, :], 1.0 / H, 1e-5, ALU.mult, ALU.add).then_inc(s.eps2, 1)
                    pool.wait_ge(s.eps2, i + 1)
                    nc.gpsimd.tensor_tensor(rstd[:, 3, :], rstd[:, 2, :], u.halfpow[:, :].to_broadcast([P, G]),
                                            ALU.pow).then_inc(s.rstd2, 1)
                    for k in range(G):
                        t = G * i + k
                        pos = G * (i % (TB // G)) + k
                        pool.wait_ge(s.qk_out, t + 3)
                        src = qk[:, k % 2, :].rearrange("p (n d) -> p n d", d=8)
                        for name, dst, table in (("byc", byc, cosb), ("bys", bys, sinb)):
                            nc.gpsimd.tensor_tensor(dst[:, k % 2, :].rearrange("p (n d) -> p n d", d=8), src,
                                                    table[:, pos, :].unsqueeze(1).to_broadcast([P, 40, 8]),
                                                    ALU.mult).then_inc(s.byc if name == "byc" else s.bys, 1)
                        pool.wait_ge(s.byc, t + 1)
                        pool.wait_ge(s.bys, t + 1)
                        o = v.QKV[:, t, 0:320].rearrange("p (n a d) -> p n a d", a=2, d=8)
                        yc = byc[:, k % 2, :].rearrange("p (n a d) -> p n a d", a=2, d=8)
                        ys = bys[:, k % 2, :].rearrange("p (n a d) -> p n a d", a=2, d=8)
                        nc.gpsimd.tensor_tensor(o[:, :, 0, :], yc[:, :, 0, :], ys[:, :, 1, :], ALU.subtract)
                        nc.gpsimd.tensor_tensor(o[:, :, 1, :], yc[:, :, 1, :], ys[:, :, 0, :], ALU.add).then_inc(s.turned, 1)

            @block.vector
            def _(dve):
                k = 0
                for n in range(6):
                    for c in range(C):
                        dve.wait_ge(s.wT_mm, k + 1)
                        rows = E if n == 5 else P
                        dst = (wqkvT[:, c, n * P:(n + 1) * P] if n < 3 else v.woT[:, c, (n - 3) * P:(n - 2) * P]
                               if n < 5 else v.gwT[:, c, :])
                        nc.vector.tensor_copy(dst, pT[:, k % 2, 0, 0, 0:rows]).then_inc(s.wT_out, 1)
                        k += 1
                dve.wait_ge(s.small_in, 64)
                with dve.Fori(0, T // G) as i:
                    for k in range(G):
                        nc.vector.bn_stats(stats[:, k, :], x1[:, G * i + k, :]).then_inc(s.stats, 1)
                    for k in range(G):
                        wait_apart(dve, s.stats, G * i + k + 1)
                        nc.vector.bn_aggr(mv[:, k, :], stats[:, k, :]).then_inc(s.mv, 1)
                    dve.wait_ge(s.mv, G * i + G)
                    dve.wait_ge(s.rstd1, i + 1)
                    for k in range(G):
                        nc.vector.tensor_scalar(xl[:, k, :], x1[:, G * i + k, :], mv[:, k, 0:1], rstd[:, 1, k:k + 1],
                                                ALU.subtract, ALU.mult).then_inc(s.xl, 1)
                    for k in range(G):
                        dve.wait_ge(s.xl, G * i + k + 1)
                        nc.vector.tensor_tensor_reduce(junk[:, k, :], xl[:, k, :], xl[:, k, :], 1.0, 0.0, ALU.mult, ALU.add,
                                                       sq[:, k:k + 1]).then_inc(s.square, 1)
                    dve.wait_ge(s.rstd2, i + 1)
                    dve.wait_ge(s.hT_mm, 2 * i + 2)
                    for k in range(G):
                        nc.vector.scalar_tensor_tensor(out=h[:, k, :], in0=xl[:, k, :], scalar=rstd[:, 3, k:k + 1],
                                                       in1=ln1_b[:, :], op0=ALU.mult, op1=ALU.mult).then_inc(s.h, 1)


PARTS_Q = (0, 0, 1, 1, 0, 2)
PARTS_K = (0, 1, 0, 1, 2, 0)
NPART = len(PARTS_Q)
ROWS = NPART * HD
CH = L // 512


def key_order(c):
    if c == 0:
        return list(range(4))
    return [kt for n in range(4) for kt in list(range(n * c, n * c + c)) + [4 * c + n]]


KSTEPS = [(c, kt) for c in range(CH) for kt in key_order(c)]
UNITS = [(h, qt, part) for h in range(GRP) for qt in range(TB) for part in range(qt // 4 + 1)]


def background():
    items = []
    for h in range(GRP):
        units = [("U", n) for n, unit in enumerate(UNITS) if unit[0] == h]
        first = sum(1 for unit in UNITS if unit[0] == 0 and unit[1] < TB // 2)
        if h == 0:
            items += [("K", 0), ("Q", 0, 0)] + units[:first] + [("K", 1), ("Q", 0, 1)]
            units = units[first:]
            turns = [("Q", 1, 0), ("Q", 1, 1)]
        else:
            turns = [("Q", k, f) for k in range(2, GRP) for f in range(2)] if h == 1 else []
        every = len(units) // (len(turns) + 1)
        for n, unit in enumerate(units):
            if turns and n and n % every == 0:
                items.append(turns.pop(0))
            items.append(unit)
        items += turns
    return items + [("M", 0), ("M", 1)]


def interleave():
    items = background()
    width = [min(512, P * (UNITS[x[1]][1] + 1) - 512 * UNITS[x[1]][2]) + 64 if x[0] == "U" else 600 for x in items]
    step = [512 - max(0, kt - 4 * c) * P + 64 for c, kt in KSTEPS]
    out, at = [], 0
    for n in range(len(KSTEPS)):
        share = min(1.0, sum(step[:n + 1]) / (0.98 * sum(step)))
        upto = at
        while upto < len(items) and sum(width[:upto + 1]) <= share * sum(width) + 1e-6:
            upto += 1
        out.append(items[at:upto])
        at = upto
    assert at == len(items)
    return out


class Uses:

    def __init__(self, passes):
        kq = 2 + 2 * GRP
        if isinstance(passes, int) and passes == 0:
            self.t, self.a, self.d = 0, 1, 1
        else:
            self.t, self.a, self.d = (kq + 2) + (kq + 2 + CH) * (passes - 1), 1 + kq * passes, 3 + (2 + CH) * (passes - 1)

    def use(self, by):
        self.t += 1
        if by == "a":
            self.a += 1
        else:
            self.d += 1


class Ring:
    BANKS = 3

    def __init__(self):
        self.at, self.last = -1, [None] * self.BANKS

    def take(self, item):
        self.at = (self.at + 1) % self.BANKS
        before, self.last[self.at] = self.last[self.at], item
        return self.at, before


def stage6(nc, sb, ps, sem, env, base_env):
    v, u = Names(env), base_env
    QKV, ident = v.QKV, u.ident
    NG = B * NKV
    NU, NS_ = len(UNITS), len(KSTEPS)
    BESIDE = interleave()
    EARLY = 2
    U0 = sum(1 for unit in UNITS if unit[0] == 0)
    with ExitStack() as ctx:
        identb = sb("identb", [P, P], BF16, ctx)
        maskf = sb("maskf", [P, P], F32, ctx)
        mask_qk = sb("mask_qk", [P, P], BF16, ctx)
        mask_kq = sb("mask_kq", [P, P], BF16, ctx)
        Qt = sb("Qt", [P, TB, GRP, ROWS], BF16, ctx)
        Kt = sb("Kt", [P, TB, ROWS], BF16, ctx)
        rem = sb("rem", [P, 2, TB, GRP * HD], F32, ctx)
        KT = sb("KT", [P, 2, L], BF16, ctx)
        QT = sb("QT", [P, 2, GRP, L], BF16, ctx)
        VV = sb("VV", [P, 2, TB, 32], F32, ctx)
        prob = sb("prob6", [P, 3, 2, 2, 512], F32, ctx)
        mx = sb("mx", [P, GRP, TB, CH], F32, ctx)
        mrem = sb("mrem", [P, 3, TB, GRP], F32, ctx)
        mpart = sb("mpart", [P, TB, GRP, 3], BF16, ctx)
        mrow = sb("mrow", [GRP * 3, L], BF16, ctx)
        oS = sb("oS", [P, 512], F32, ctx)
        den = sb("den", [P, 4, GRP], F32, ctx)
        pS = ps("pS6", [P, 2, 2, 512], F32, ctx)
        pO = ps("pO6", [P, 512], F32, ctx)
        pM = ps("pM6", [P, Ring.BANKS, 512], F32, ctx)
        pMb = [pM[:, k, :].bitcast(BF16) for k in range(Ring.BANKS)]
        names = ("zero", "masks", "masks_b", "maskT", "maskT_out", "qparts", "kparts", "vparts", "T_mm", "T_out", "TA_out", "unit_mm", "unit_max",
                 "mparts", "mrow_in", "pair_mm", "pair_exp", "pv", "o_out", "den_out", "o_put", "vv_init", "ones_in",
                 "qchain", "mchain")
        s = Names({n: sem("c_" + n) for n in names})

        def group(gi):
            b, g = gi // NKV, gi % NKV
            return b * TB, g

        with nc.Block() as block:
            @block.sync
            def _(sp):
                def send(gi, par, maxima_out):
                    sp.wait_ge(s.T_out, maxima_out)
                    for h in range(GRP):
                        sp.dma_start(QT[ROWS:ROWS + 3, par, h, :], mrow[3 * h:3 * h + 3, :]).then_inc(s.mrow_in, 16)
                sp.wait_ge(s.ones_in, 1)
                send(0, 0, 1 + 2)
                send(1, 1, 1 + 2 + (2 + CH - 1))
                with sp.Fori(1, NG // 2) as i:
                    for k in range(2):
                        gi = 2 * i + k
                        send(gi, k, (2 + CH) * gi + 2)
                sp.wait_ge(s.mrow_in, 64 * NG)

            @block.gpsimd
            def _(pool):
                nc.gpsimd.memset(maskf[:, :], 0.0).then_inc(s.zero, 1)
                nc.gpsimd.memset(VV[:, :, :, :], 0.0).then_inc(s.zero, 1)
                nc.gpsimd.tensor_copy(identb[:, :], ident[:, :]).then_inc(s.masks_b, 1)
                pool.wait_ge(s.zero, 2)
                nc.gpsimd.affine_select(out=maskf[:, :], in_=maskf[:, :], compare_op=ALU.is_ge, fill=NEG, base=0,
                                        pattern=[[-1, P]], channel_multiplier=1).then_inc(s.masks, 1)
                nc.gpsimd.memset(VV[:, :, :, HD:HD + 1], 1.0).then_inc(s.vv_init, 1)
                pool.wait_ge(s.masks, 1)
                nc.gpsimd.tensor_copy(mask_qk[:, :], maskf[:, :]).then_inc(s.masks_b, 1)
                pool.wait_ge(s.masks_b, 2)
                nc.gpsimd.memset(maskf[:, :], 0.0).then_inc(s.zero, 1)
                pool.wait_ge(s.zero, 3)
                nc.gpsimd.affine_select(out=maskf[:, :], in_=maskf[:, :], compare_op=ALU.is_ge, fill=NEG, base=0,
                                        pattern=[[1, P]], channel_multiplier=-1).then_inc(s.masks, 1)
                pool.wait_ge(s.masks, 2)
                nc.gpsimd.tensor_copy(mask_kq[:, :], maskf[:, :]).then_inc(s.masks_b, 1)
                pool.wait_ge(s.vv_init, 1)
                ch = Chain(pool, s.qchain)

                def split(src, parts, slots, rem_ap, per):
                    for part in range(3):
                        at = [n for n in range(NPART) if slots[n] == part]
                        now = src if part == 0 else rem_ap[part - 1]
                        ch.link(nc.gpsimd.tensor_copy(parts(at[0]), now), apart=True)
                        for n in at[1:]:
                            last = nc.gpsimd.tensor_copy(parts(n), parts(at[0]))
                            if part == 2:
                                return last
                            last.then_inc(s.kparts, 1)
                        if part < 2:
                            ch.link(nc.gpsimd.tensor_tensor(rem_ap[part], now, parts(at[0]), ALU.subtract), apart=True)

                def prepare(gi, par, later=False):
                    t0, g = group(gi)
                    tiles = bass.ds(t0, TB)
                    ch.at(10 * gi)
                    q = QKV[:, tiles, bass.ds(g * GRP * HD, GRP * HD)].rearrange("p t (h d) -> p t h d", d=HD)
                    k = QKV[:, tiles, bass.ds(NH * HD + g * HD, HD)]
                    split(k, lambda n: Kt[:, :, n * HD:(n + 1) * HD], PARTS_K,
                          [rem[:, r, :, 0:HD] for r in range(2)], 0)
                    r4 = [rem[:, r].rearrange("p t (h d) -> p t h d", d=HD) for r in range(2)]
                    split(q, lambda n: Qt[:, :, :, n * HD:(n + 1) * HD], PARTS_Q, r4, 0)
                    assert ch.k == 10
                    if later:
                        wait_apart(pool, s.pv, NS_ * (gi - 1) + 2)
                    nc.gpsimd.tensor_copy(VV[:, par, :, 0:HD],
                                          QKV[:, tiles, bass.ds((NH + NKV) * HD + g * HD, HD)]).then_inc(s.vparts, 1)
                prepare(0, 0)
                pool.wait_ge(s.unit_mm, 2 * U0 + 1)
                prepare(1, 1)
                with pool.Fori(1, NG // 2) as i:
                    for k in range(2):
                        gi = 2 * i + k
                        pool.wait_ge(s.unit_mm, NU * (gi - 1) + 2 * U0 + 1)
                        prepare(gi, k, later=True)

            @block.tensor
            def _(pe):
                pe.wait_ge(s.masks_b, 3)
                pe.wait_ge(s.ones_in, 1)
                pe.sem_inc(s.pv, 2)

                def take(ring, item):
                    bank, before = ring.take(item)
                    if before is not None:
                        pe.wait_ge(*before)
                    return bank

                def beside(item, gi, par, cnt, ring):
                    kind = item[0]
                    if kind in "KQM":
                        cnt.use("a" if kind in "KQ" else "d")
                        bank = take(ring, (s.TA_out, cnt.a) if kind in "KQ" else (s.T_out, cnt.d))
                        f = item[-1]
                        if kind == "M":
                            pe.wait_ge(s.mparts, gi + 1)
                        else:
                            pe.wait_ge(s.qchain, 10 * gi + (5 if kind == "K" else 10))
                            pe.wait_ge(s.kparts, 6 * gi + (3 if kind == "K" else 6))
                        for k in range(8):
                            t = 8 * f + k
                            if kind == "K":
                                src, rows = Kt[:, t, :], ROWS
                            elif kind == "Q":
                                src, rows = Qt[:, t, item[1], :], ROWS
                            else:
                                src, rows = mpart[:, t, :, :].rearrange("p h a -> p (h a)"), 3 * GRP
                            last = nc.tensor.transpose(pMb[bank][0:rows, k * P:(k + 1) * P], src, identb[:, :])
                        last.then_inc(s.T_mm, 1)
                        return
                    n = item[1]
                    h, qt, part = UNITS[n]
                    bank = take(ring, (s.unit_max, NU * gi + n + 1))
                    if qt == 0 or (h == 0 and qt == TB // 2):
                        pe.wait_ge(s.TA_out, cnt.a)
                    w = min(512, (qt + 1) * P - 512 * part)
                    last = nc.tensor.matmul(pM[:, bank, 0:w], QT[0:ROWS, par, h, qt * P:(qt + 1) * P],
                                            KT[0:ROWS, par, 512 * part:512 * part + w], start=True, stop=part < qt // 4)
                    if part == qt // 4:
                        last = nc.tensor.matmul(pM[:, bank, w - P:w], identb[:, :], mask_qk[:, :], start=False, stop=True)
                    last.then_inc(s.unit_mm, 1)

                def pair(gi, par, n, pr, between):
                    c, kt = KSTEPS[n]
                    lo = max(0, kt - 4 * c) * P
                    idx = 2 * (NS_ * gi + n) + pr
                    pe.wait_ge(s.pair_exp, idx + 1)
                    for hh in range(2):
                        h = 2 * pr + hh
                        diag = kt >= 4 * c
                        last = nc.tensor.matmul(pS[:, pr, hh, lo:512], KT[0:ROWS + 3, par, kt * P:(kt + 1) * P],
                                                QT[0:ROWS + 3, par, h, 512 * c + lo:512 * c + 512], start=True,
                                                stop=not diag)
                        if diag:
                            last = nc.tensor.matmul(pS[:, pr, hh, lo:lo + P], identb[:, :], mask_kq[:, :], start=False,
                                                    stop=True)
                        if hh == 0:
                            between()
                    last.then_inc(s.pair_mm, 1)

                def values(gi, par, n):
                    c, kt = KSTEPS[n]
                    lo = max(0, kt - 4 * c) * P
                    pe.wait_ge(s.pair_exp, 2 * (NS_ * gi + n) + 4)
                    if kt == 0:
                        pe.wait_ge(s.o_out, CH * gi + c + 1)
                    if n == 0:
                        pe.wait_ge(s.vparts, gi + 1)
                    for h in range(GRP):
                        last = nc.tensor.matmul(pO[32 * h:32 * h + 32, lo:512], VV[:, par, kt, :],
                                                prob[:, n % 3, h // 2, h % 2, lo:512], start=(kt == 0),
                                                stop=(kt == 4 * c + 3), tile_position=(0, 32 * h))
                    last.then_inc(s.pv, 1)

                def chunk_out(gi, c, cnt, ring):
                    pe.wait_ge(s.o_out, CH * gi + c + 2)
                    cnt.use("d")
                    bank = take(ring, (s.T_out, cnt.d))
                    for k in range(4):
                        last = nc.tensor.transpose(pM[:, bank, k * P:(k + 1) * P], oS[:, k * P:(k + 1) * P], ident[:, :])
                    last.then_inc(s.T_mm, 1)

                def one(gi, par, more):
                    cnt, ring = Uses(gi + 1), Ring()
                    pe.wait_ge(s.T_out, cnt.d)
                    for x in BESIDE[0][:EARLY] if more else []:
                        beside(x, gi + 1, 1 - par, cnt, ring)
                    pe.wait_ge(s.mrow_in, 64 * gi + 64)
                    pair(gi, par, 0, 0, lambda: None)
                    pair(gi, par, 0, 1, lambda: None)
                    for n in range(NS_):
                        extra = BESIDE[n][0 if n else EARLY:] if more else []

                        def some(place):
                            for x in extra[place * len(extra) // 5:(place + 1) * len(extra) // 5]:
                                beside(x, gi + 1, 1 - par, cnt, ring)
                        some(0)
                        if n + 1 < NS_:
                            pair(gi, par, n + 1, 0, lambda: some(1))
                        else:
                            some(1)
                        some(2)
                        if n:
                            values(gi, par, n - 1)
                        some(3)
                        if n + 1 < NS_:
                            pair(gi, par, n + 1, 1, lambda: some(4))
                        else:
                            some(4)
                        if n > 1 and KSTEPS[n - 1][1] == 0:
                            chunk_out(gi, KSTEPS[n][0] - 1, cnt, ring)
                    values(gi, par, NS_ - 1)
                    chunk_out(gi, CH - 1, cnt, ring)
                cnt, ring = Uses(0), Ring()
                for item in background():
                    beside(item, 0, 0, cnt, ring)
                with pe.Fori(0, NG // 2 - 1) as i:
                    for k in range(2):
                        one(2 * i + k, k, True)
                one(NG - 2, 0, True)
                one(NG - 1, 1, False)

            @block.scalar
            def _(act):
                act.sem_inc(s.pair_exp, 2)
                act.sem_inc(s.TA_out, 1)
                act.wait_ge(s.vv_init, 1)

                def beside(item, par, cnt, ring):
                    bank, _before = ring.take(item)
                    if item[0] == "U":
                        return
                    cnt.use("a" if item[0] in "KQ" else "d")
                    if item[0] == "M":
                        return
                    act.wait_ge(s.T_mm, cnt.t)
                    cols = slice(item[-1] * 1024, item[-1] * 1024 + 1024)
                    dst = KT[0:ROWS, par, cols] if item[0] == "K" else QT[0:ROWS, par, item[1], cols]
                    nc.scalar.copy(dst, pMb[bank][0:ROWS, :]).then_inc(s.TA_out, 1)

                def one(gi, par, more):
                    cnt, ring = Uses(gi + 1), Ring()
                    for x in BESIDE[0][:EARLY] if more else []:
                        beside(x, 1 - par, cnt, ring)
                    for n in range(NS_):
                        c, kt = KSTEPS[n]
                        lo = max(0, kt - 4 * c) * P
                        act.wait_ge(s.pv, NS_ * gi + 2 + max(0, n - 2))
                        for pr in range(2):
                            act.wait_ge(s.pair_mm, 2 * (NS_ * gi + n) + pr + 1)
                            nc.scalar.activation(prob[:, n % 3, pr, :, lo:512], pS[:, pr, :, lo:512], ACT.Exp,
                                                 scale=SCALE).then_inc(s.pair_exp, 1)
                        for x in BESIDE[n][0 if n else EARLY:] if more else []:
                            beside(x, 1 - par, cnt, ring)
                        if n > 1 and KSTEPS[n - 1][1] == 0:
                            cnt.use("d")
                            ring.take("context")
                cnt, ring = Uses(0), Ring()
                for item in background():
                    beside(item, 0, cnt, ring)
                with act.Fori(0, NG // 2 - 1) as i:
                    for k in range(2):
                        one(2 * i + k, k, True)
                one(NG - 2, 0, True)
                one(NG - 1, 1, False)

            @block.vector
            def _(dve):
                dve.sem_inc(s.T_out, 1)
                dve.sem_inc(s.o_out, 1)
                nc.vector.memset(KT[ROWS:ROWS + 3, :, :], 1.0).then_inc(s.ones_in, 1)
                ch = Chain(dve, s.mchain)
                ch.link(nc.vector.memset(mx[:, :, :, :], -3e38))

                def beside(item, gi, par, cnt, ring):
                    kind = item[0]
                    bank, _before = ring.take(item)
                    if kind in "KQM":
                        f = item[-1]
                        if kind == "M" and f == 0:
                            dve.wait_ge(s.unit_max, NU * gi + NU)
                            ch.at(6 * gi + 1)
                            ch.link(nc.vector.reduce_max(mrem[:, 1].rearrange("p t h -> p h t"), mx[:, :, :, :], AX.X))
                            ch.link(nc.vector.tensor_scalar(mrem[:, 0], mrem[:, 1], -1.0, None, ALU.mult))
                            ch.link(nc.vector.tensor_copy(mpart[:, :, :, 0], mrem[:, 0]))
                            ch.link(nc.vector.tensor_tensor(mrem[:, 1], mrem[:, 0], mpart[:, :, :, 0], ALU.subtract))
                            ch.link(nc.vector.tensor_copy(mpart[:, :, :, 1], mrem[:, 1]))
                            ch.link(nc.vector.tensor_tensor(mrem[:, 2], mrem[:, 1], mpart[:, :, :, 1], ALU.subtract))
                            nc.vector.tensor_copy(mpart[:, :, :, 2], mrem[:, 2]).then_inc(s.mparts, 1)
                        cnt.use("a" if kind in "KQ" else "d")
                        if kind in "KQ":
                            return
                        dve.wait_ge(s.T_mm, cnt.t)
                        if f == 0 and not (isinstance(gi, int) and gi == 0):
                            dve.wait_ge(s.mrow_in, 64 * gi)
                        nc.vector.tensor_copy(mrow[:, f * 1024:f * 1024 + 1024], pMb[bank][0:3 * GRP, :]).then_inc(s.T_out, 1)
                        return
                    n = item[1]
                    h, qt, part = UNITS[n]
                    dve.wait_ge(s.unit_mm, NU * gi + n + 1)
                    w = min(512, (qt + 1) * P - 512 * part)
                    nc.vector.reduce_max(mx[:, h, qt, part:part + 1], pM[:, bank, 0:w], AX.X).then_inc(s.unit_max, 1)

                def chunk(gi, c, cnt, after):
                    dve.wait_ge(s.pv, NS_ * gi + after + 2)
                    nc.vector.tensor_copy(oS[:, :], pO[:, :]).then_inc(s.o_out, 1)

                def chunk_put(gi, c, cnt, ring):
                    t0, g = group(gi)
                    cnt.use("d")
                    bank, _before = ring.take("context")
                    dve.wait_ge(s.T_mm, cnt.t)
                    o = pM[:, bank, :].rearrange("p (k h d) -> p k h d", k=4, h=GRP)
                    nc.vector.reciprocal(den[:, :, :], o[:, :, :, HD]).then_inc(s.den_out, 1)
                    dve.wait_ge(s.den_out, CH * gi + c + 1)
                    nc.vector.tensor_tensor(
                        QKV[:, bass.ds(t0 + 4 * c, 4), bass.ds(g * GRP * HD, GRP * HD)].rearrange("p k (h d) -> p k h d", d=HD),
                        o[:, :, :, 0:HD], den[:, :, :].unsqueeze(3).to_broadcast([P, 4, GRP, HD]),
                        ALU.mult).then_inc(s.T_out, 1)

                def one(gi, par, more):
                    cnt, ring = Uses(gi + 1), Ring()
                    for n in range(NS_):
                        for x in BESIDE[n] if more else []:
                            beside(x, gi + 1, 1 - par, cnt, ring)
                        if n > 1 and KSTEPS[n - 1][1] == 0:
                            chunk_put(gi, KSTEPS[n][0] - 1, cnt, ring)
                        if n and KSTEPS[n][1] == 0:
                            chunk(gi, KSTEPS[n - 1][0], cnt, n)
                    chunk(gi, CH - 1, cnt, NS_)
                    chunk_put(gi, CH - 1, cnt, ring)
                cnt, ring = Uses(0), Ring()
                for item in background():
                    beside(item, 0, 0, cnt, ring)
                with dve.Fori(0, NG // 2 - 1) as i:
                    for k in range(2):
                        one(2 * i + k, k, True)
                one(NG - 2, 0, True)
                one(NG - 1, 1, False)


CAP = B * L + P
MAXT = 2 * B * L // P + E
NTAB = MAXT + 2


def stage7(nc, sb, ps, sem, env, base_env):
    v, u = Names(env), base_env
    x1, ident, ones, QKV = u.x1, u.ident, u.ones, v.QKV
    G = 4
    with ExitStack() as ctx:
        stats = sb("stats7", [P, G, 6], F32, ctx)
        mv = sb("mv7", [P, G, 2], F32, ctx)
        rstd = sb("rstd7", [P, 4, G], F32, ctx)
        sq = sb("sq7", [P, G], F32, ctx)
        junk = sb("junk7", [P, G, H], F32, ctx)
        xl = sb("xl7", [P, G, H], F32, ctx)
        x2 = sb("x27", [P, G, H], F32, ctx)
        h2 = sb("h27", [P, G, H], F32, ctx)
        at = sb("at7", [P, 2, 2, H], F32, ctx)
        aT = sb("aT7", [P, 2, 2, C, P], F32, ctx)
        hT = sb("hT7", [P, 2, 2, C, P], F32, ctx)
        tri = sb("tri", [P, P], F32, ctx)
        iota_i = sb("iota_i7", [P, E], I32, ctx)
        iota8 = sb("iota8", [P, E], F32, ctx)
        iotap_i = sb("iotap_i", [P, 1], I32, ctx)
        iotap = sb("iotap", [P, 1], F32, ctx)
        lg = sb("lg", [P, G, E], F32, ctx)
        pr = sb("pr", [P, G, E], F32, ctx)
        ex = sb("ex7", [P, G, E], F32, ctx)
        red = sb("red7", [P, 4, G], F32, ctx)
        top = sb("top7", [P, G, 8], F32, ctx)
        topi = sb("topi7", [P, G, 8], U32, ctx)
        topf = sb("topf7", [P, G, 2], F32, ctx)
        hot = sb("hot7", [P, 2, G, E], F32, ctx)
        both = sb("both7", [P, G, E], F32, ctx)
        place = sb("place7", [P, G, E], F32, ctx)
        picked = sb("picked7", [P, 2, G, E], F32, ctx)
        slotf = sb("slotf7", [P, G, 2], F32, ctx)
        slot_now = sb("slot_now", [P, G, 2], I32, ctx)
        carry = sb("carry", [P, G + 1, E], F32, ctx)
        pT = ps("pT7", [P, 2, 2, C, P], F32, ctx)
        pX = ps("pX7", [P, 2, 512], F32, ctx)
        pL = ps("pL7", [P, 512], F32, ctx)
        pR = ps("pR7", [P, 512], F32, ctx)
        names = ("consts", "consts2", "tri_in", "stats", "mv", "eps1", "rstd1", "xl", "x2", "square", "eps2", "rstd2", "h",
                 "resid", "at_in", "aT_mm", "aT_out", "proj", "hT_mm", "hT_out", "logits", "ex", "chain", "both_in", "ranks",
                 "slots", "kept", "tab_chain", "tab_ready", "zero_in", "padded")
        s = Names({n: sem("r_" + n) for n in names})
        scattered = [sem(f"r_scattered{k}") for k in range(G)]
        NCH = 29
        PICKED = 17
        with nc.Block() as block:
            @block.gpsimd
            def _(pool):
                nc.gpsimd.iota(iota_i[:, :], pattern=[[1, E]], base=0, channel_multiplier=0).then_inc(s.consts, 1)
                nc.gpsimd.iota(iotap_i[:, :], pattern=[[0, 1]], base=0, channel_multiplier=1).then_inc(s.consts, 1)
                nc.gpsimd.memset(tri[:, :], 1.0).then_inc(s.consts, 1)
                nc.gpsimd.iota(v.jrow_i[:, :], pattern=[[1, NTAB]], base=0, channel_multiplier=0).then_inc(s.consts, 1)
                pool.wait_ge(s.consts, 4)
                nc.gpsimd.tensor_copy(v.jrow[:, :], v.jrow_i[:, :]).then_inc(s.consts2, 1)
                nc.gpsimd.tensor_copy(iota8[:, :], iota_i[:, :]).then_inc(s.consts2, 1)
                nc.gpsimd.tensor_copy(iotap[:, :], iotap_i[:, :]).then_inc(s.consts2, 1)
                nc.gpsimd.affine_select(out=tri[:, :], in_=tri[:, :], compare_op=ALU.is_gt, fill=0.0, base=0,
                                        pattern=[[1, P]], channel_multiplier=-1).then_inc(s.tri_in, 1)
                with pool.Fori(0, T // G) as i:
                    wait_apart(pool, s.mv, G * i + G)
                    nc.gpsimd.tensor_scalar(rstd[:, 0, :], mv[:, :, 1], 1e-5, None, ALU.add).then_inc(s.eps1, 1)
                    pool.wait_ge(s.eps1, i + 1)
                    nc.gpsimd.tensor_tensor(rstd[:, 1, :], rstd[:, 0, :], u.halfpow[:, :].to_broadcast([P, G]),
                                            ALU.pow).then_inc(s.rstd1, 1)
                    wait_apart(pool, s.square, G * i + G)
                    nc.gpsimd.tensor_scalar(rstd[:, 2, :], sq[:, :], 1.0 / H, 1e-5, ALU.mult, ALU.add).then_inc(s.eps2, 1)
                    pool.wait_ge(s.eps2, i + 1)
                    nc.gpsimd.tensor_tensor(rstd[:, 3, :], rstd[:, 2, :], u.halfpow[:, :].to_broadcast([P, G]),
                                            ALU.pow).then_inc(s.rstd2, 1)
                    nc.gpsimd.tensor_tensor(x1[:, bass.ds(G * i, G), :], x1[:, bass.ds(G * i, G), :], x2[:, :, :],
                                            ALU.add).then_inc(s.resid, 1)
                    pool.wait_ge(s.h, G * i + G)
                    wait_apart(pool, s.slots, i + 1)
                    for k in range(G):
                        for a in range(2):
                            nc.gpsimd.indirect_dma_start(
                                out=v.queue[:, :], out_offset=bass.IndirectOffsetOnAxis(ap=slot_now[:, k, a:a + 1], axis=0),
                                in_=h2[:, k, :], in_offset=None).then_inc(scattered[k], 16)
                    for k in range(G):
                        pool.wait_ge(scattered[k], 32 * i + 32)
                pool.wait_ge(s.tab_ready, 1)
                nc.gpsimd.memset(h2[:, 0, :], 0.0).then_inc(s.zero_in, 1)
                pool.wait_ge(s.zero_in, 1)
                for e in range(E):
                    nc.gpsimd.indirect_dma_start(
                        out=v.queue[:, :], out_offset=bass.IndirectOffsetOnAxis(ap=v.pad_rows[:, e:e + 1], axis=0),
                        in_=h2[:, 0, :], in_offset=None).then_inc(s.padded, 16)
                pool.wait_ge(s.padded, 16 * E)

            @block.tensor
            def _(pe):
                pe.wait_ge(s.tri_in, 1)
                pe.sem_inc(s.aT_mm, 2)
                pe.sem_inc(s.proj, 4)
                pe.sem_inc(s.hT_mm, 2)
                pe.sem_inc(s.logits, 1)
                with pe.Fori(0, T // G) as i:
                    for g in range(2):
                        pe.wait_ge(s.at_in, 2 * i + g + 1)
                        pe.wait_ge(s.hT_out, 2 * i + g + 1)
                        for k in range(2):
                            for c in range(C):
                                last = nc.tensor.transpose(pT[:, g, k, c, :], at[:, g, k, c * P:(c + 1) * P], ident[:, :])
                        last.then_inc(s.aT_mm, 1)
                    for g in range(2):
                        pe.wait_ge(s.aT_out, 2 * i + g + 1)
                        for k in range(2):
                            pe.wait_ge(s.x2, 4 * i + 2 * g + k + 1)
                            for c in range(C):
                                last = nc.tensor.matmul(pX[:, k, 0:H], aT[:, g, k, c, :], v.woT[:, c, :],
                                                        start=(c == 0), stop=(c == C - 1))
                            last.then_inc(s.proj, 1)
                    for g in range(2):
                        pe.wait_ge(s.h, G * i + 2 * g + 2)
                        for k in range(2):
                            for c in range(C):
                                last = nc.tensor.transpose(pT[:, g, k, c, :], h2[:, 2 * g + k, c * P:(c + 1) * P], ident[:, :])
                        last.then_inc(s.hT_mm, 1)
                    for g in range(2):
                        pe.wait_ge(s.hT_out, 2 * i + g + 3)
                        for k in range(2):
                            n = E * (2 * g + k)
                            for c in range(C):
                                last = nc.tensor.matmul(pL[:, n:n + E], hT[:, g, k, c, :], v.gwT[:, c, :],
                                                        start=(c == 0), stop=(c == C - 1))
                    last.then_inc(s.logits, 1)
                    pe.wait_ge(s.chain, NCH * i + PICKED)
                    b2 = both[:, :, :].rearrange("p k e -> p (k e)")
                    nc.tensor.matmul(pR[:, 0:G * E], tri[:, :], b2, start=True, stop=True)
                    nc.tensor.matmul(pR[:, G * E:2 * G * E], ones[:, :], b2, start=True, stop=True).then_inc(s.ranks, 1)

            @block.scalar
            def _(act):
                act.sem_inc(s.hT_out, 2)
                with act.Fori(0, T // G) as i:
                    for g in range(2):
                        act.wait_ge(s.aT_mm, 2 * i + g + 1)
                        nc.scalar.copy(at[:, g], QKV[:, bass.ds(G * i + 2 * g, 2), 0:H]).then_inc(s.at_in, 1)
                    for g in range(2):
                        act.wait_ge(s.aT_mm, 2 * i + g + 3)
                        act.wait_ge(s.proj, 4 * i + 2 * g + 2)
                        nc.scalar.copy(aT[:, g], pT[:, g]).then_inc(s.aT_out, 1)
                    for g in range(2):
                        act.wait_ge(s.hT_mm, 2 * i + g + 3)
                        act.wait_ge(s.logits, i + 1)
                        nc.scalar.copy(hT[:, g], pT[:, g]).then_inc(s.hT_out, 1)
                    act.wait_ge(s.chain, NCH * i + 2)
                    nc.scalar.activation(ex[:, :, :], pr[:, :, :], ACT.Exp).then_inc(s.ex, 1)

            @block.vector
            def _(dve):
                ch = Chain(dve, s.chain)
                dve.sem_inc(s.x2, 2)
                dve.wait_ge(s.consts2, 3)
                nc.vector.memset(carry[:, :, :], 0.0).then_inc(s.kept, 1)
                dve.wait_ge(s.kept, 1)

                def bc(ap):
                    return ap.unsqueeze(2).to_broadcast([P, G, E])
                with dve.Fori(0, T // G) as i:
                    ch.at(NCH * i)
                    for k in range(G):
                        nc.vector.bn_stats(stats[:, k, :], x1[:, G * i + k, :]).then_inc(s.stats, 1)
                    for k in range(G):
                        wait_apart(dve, s.stats, G * i + k + 1)
                        nc.vector.bn_aggr(mv[:, k, :], stats[:, k, :]).then_inc(s.mv, 1)
                    dve.wait_ge(s.mv, G * i + G)
                    dve.wait_ge(s.rstd1, i + 1)
                    for k in range(G):
                        nc.vector.tensor_scalar(xl[:, k, :], x1[:, G * i + k, :], mv[:, k, 0:1], rstd[:, 1, k:k + 1],
                                                ALU.subtract, ALU.mult).then_inc(s.xl, 1)
                    for k in range(G):
                        dve.wait_ge(s.xl, G * i + k + 1)
                        dve.wait_ge(s.proj, G * i + k + 5)
                        nc.vector.tensor_tensor(x2[:, k, :], xl[:, k, :], pX[:, k % 2, 0:H], ALU.add).then_inc(s.x2, 1)
                    for k in range(G):
                        dve.wait_ge(s.x2, G * i + k + 3)
                        nc.vector.tensor_tensor_reduce(junk[:, k, :], x2[:, k, :], x2[:, k, :], 1.0, 0.0, ALU.mult, ALU.add,
                                                       sq[:, k:k + 1]).then_inc(s.square, 1)
                    dve.wait_ge(s.rstd2, i + 1)
                    for k in range(G):
                        nc.vector.scalar_tensor_tensor(out=h2[:, k, :], in0=x2[:, k, :], scalar=rstd[:, 3, k:k + 1],
                                                       in1=v.ln2_b[:, :], op0=ALU.mult, op1=ALU.mult).then_inc(s.h, 1)
                    dve.wait_ge(s.logits, i + 2)
                    lgp = pL[:, 0:G * E].rearrange("p (k e) -> p k e", e=E)
                    ch.link(nc.vector.reduce_max(red[:, 0, :], lgp, AX.X))
                    nc.vector.tensor_tensor(pr[:, :, :], lgp, bc(red[:, 0, :]), ALU.subtract).then_inc(s.chain, 1)
                    ch.k += 1
                    dve.wait_ge(s.ex, i + 1)
                    ch.link(nc.vector.reduce_sum(red[:, 1, :], ex[:, :, :], AX.X))
                    ch.link(nc.vector.reciprocal(red[:, 2, :], red[:, 1, :]))
                    ch.link(nc.vector.tensor_tensor(lg[:, :, :], ex[:, :, :], bc(red[:, 2, :]), ALU.mult), apart=True)
                    for k in range(G):
                        ch.link(nc.vector.max(top[:, k, :], lg[:, k, :]), apart=True)
                        ch.link(nc.vector.max_index(topi[:, k, :], top[:, k, :], lg[:, k, :]), apart=True)
                    ch.link(nc.vector.tensor_copy(topf[:, :, :], topi[:, :, 0:2]))
                    for a in range(2):
                        ch.link(nc.vector.tensor_tensor(hot[:, a], iota8[:, :].unsqueeze(1).to_broadcast([P, G, E]),
                                                        bc(topf[:, :, a]), ALU.is_equal))
                    ch.link(nc.vector.tensor_tensor(both[:, :, :], hot[:, 0], hot[:, 1], ALU.add))
                    assert ch.k == PICKED
                    ch.link(nc.vector.tensor_tensor(red[:, 3, :], top[:, :, 0], top[:, :, 1], ALU.add))
                    ch.link(nc.vector.reciprocal(red[:, 3, :], red[:, 3, :]))
                    ch.link(nc.vector.tensor_tensor(v.weights[:, bass.ds(G * i, G), :], top[:, :, 0:2],
                                                    red[:, 3, :].unsqueeze(2).to_broadcast([P, G, 2]), ALU.mult))
                    dve.wait_ge(s.ranks, i + 1)
                    for k in range(G):
                        ch.link(nc.vector.tensor_tensor(carry[:, k + 1, :], carry[:, k, :],
                                                        pR[:, (G + k) * E:(G + k + 1) * E], ALU.add))
                    ch.link(nc.vector.tensor_tensor(place[:, :, :], carry[:, 0:G, :],
                                                    pR[:, 0:G * E].rearrange("p (k e) -> p k e", e=E), ALU.add))
                    ch.link(nc.vector.scalar_tensor_tensor(out=place[:, :, :],
                                                           in0=iota8[:, :].unsqueeze(1).to_broadcast([P, G, E]),
                                                           scalar=float(CAP), in1=place[:, :, :], op0=ALU.mult, op1=ALU.add))
                    ch.link(nc.vector.tensor_tensor(picked[:, :, :, :], hot[:, :, :, :],
                                                    place[:, :, :].unsqueeze(1).to_broadcast([P, 2, G, E]), ALU.mult))
                    ch.link(nc.vector.reduce_sum(slotf[:, :, :].rearrange("p k a -> p a k"), picked[:, :, :, :], AX.X))
                    ch.link(nc.vector.tensor_copy(carry[:, 0, :], carry[:, G, :]))
                    assert ch.k == NCH, ch.k
                    nc.vector.tensor_copy(v.rowsf[:, bass.ds(G * i, G), :], slotf[:, :, :]).then_inc(s.kept, 1)
                    nc.vector.tensor_copy(slot_now[:, :, :], slotf[:, :, :]).then_inc(s.slots, 1)
                    for k in range(G):
                        dve.wait_ge(scattered[k], 32 * i + 32)
                    dve.wait_ge(s.resid, i + 1)
                tc = Chain(dve, s.tab_chain)
                dve.wait_ge(s.kept, 1 + T // G)
                tables(nc, tc, v, s, carry, iota8, iotap)
                nc.vector.tensor_copy(v.pad_rows[:, :], v.padf[:, :]).then_inc(s.tab_ready, 1)
                dve.wait_ge(s.tab_ready, 1)


def tables(nc, tc, v, s, carry, iota8, iotap):
    count = carry[:, 0, :]
    tc.link(nc.vector.scalar_tensor_tensor(out=v.padf[:, :], in0=iota8[:, :], scalar=float(CAP), in1=count,
                                           op0=ALU.mult, op1=ALU.add))
    tc.link(nc.vector.tensor_scalar(v.padf[:, :], v.padf[:, :], iotap[:, :], None, ALU.add))
    tc.link(nc.vector.tensor_scalar(v.steps[:, :], v.jrow[:, 0:T], float(P), None, ALU.mult))
    tc.link(nc.vector.tensor_tensor(v.cmp[:, :, 0:T], v.steps[:, :].unsqueeze(1).to_broadcast([P, E, T]),
                                    count.unsqueeze(2).to_broadcast([P, E, T]), ALU.is_lt))
    tc.link(nc.vector.reduce_sum(v.ntile[:, :], v.cmp[:, :, 0:T], AX.X))
    tc.link(nc.vector.tensor_copy(v.ends[:, 0:1], v.ntile[:, 0:1]))
    for e in range(1, E):
        tc.link(nc.vector.tensor_tensor(v.ends[:, e:e + 1], v.ends[:, e - 1:e], v.ntile[:, e:e + 1], ALU.add))
    total = v.ends[:, E - 1:E]
    tc.link(nc.vector.tensor_scalar(v.lastt[:, :], total, -1.0, None, ALU.add))
    tc.link(nc.vector.tensor_scalar(v.jc[:, :], v.jrow[:, :], v.lastt[:, :], None, ALU.min))
    tc.link(nc.vector.tensor_tensor(v.cmp[:, :, :], v.jc[:, :].unsqueeze(1).to_broadcast([P, E, NTAB]),
                                    v.ends[:, :].unsqueeze(2).to_broadcast([P, E, NTAB]), ALU.is_ge))
    tc.link(nc.vector.reduce_sum(v.ej[:, :], v.cmp[:, :, :].rearrange("p e j -> p j e"), AX.X))
    tc.link(nc.vector.tensor_tensor(v.cmp[:, :, :], v.cmp[:, :, :], v.ntile[:, :].unsqueeze(2).to_broadcast([P, E, NTAB]),
                                    ALU.mult))
    tc.link(nc.vector.reduce_sum(v.before[:, :], v.cmp[:, :, :].rearrange("p e j -> p j e"), AX.X))
    tc.link(nc.vector.tensor_tensor(v.rowf[:, :], v.jc[:, :], v.before[:, :], ALU.subtract))
    tc.link(nc.vector.tensor_scalar(v.rowf[:, :], v.rowf[:, :], float(P), None, ALU.mult))
    tc.link(nc.vector.scalar_tensor_tensor(out=v.rowf[:, :], in0=v.ej[:, :], scalar=float(CAP), in1=v.rowf[:, :],
                                           op0=ALU.mult, op1=ALU.add))
    tc.link(nc.vector.tensor_copy(v.tile_expert[:, :], v.ej[:, :]))
    tc.link(nc.vector.tensor_copy(v.tile_in[:, :], v.rowf[:, :]))
    for e in range(1, E):
        tc.link(nc.vector.tensor_scalar(v.lastt[:, :], v.ntile[:, e - 1:e], -float(P), float(CAP), ALU.mult, ALU.add))
        tc.link(nc.vector.tensor_scalar(v.shift[:, :, :], v.rowsf[:, :, :], float(e * CAP), v.lastt[:, :], ALU.is_ge,
                                        ALU.mult))
        tc.link(nc.vector.tensor_tensor(v.shifts[:, :, :], v.shifts[:, :, :] if e > 1 else v.rowsf[:, :, :],
                                        v.shift[:, :, :], ALU.subtract))
    tc.link(nc.vector.tensor_copy(v.rows[:, :, :], v.shifts[:, :, :]))


def stage8(nc, sb, ps, sem, env, base_env):
    v, u = Names(env), base_env
    ident = u.ident
    NR = E * 2 * FFN // P
    NR2 = E * H // P
    with ExitStack() as ctx:
        w13T = sb("w13T", [P, C, E * 2 * FFN], F32, ctx)
        w2T = sb("w2T", [P, FFN // P, E * H], F32, ctx)
        with ExitStack() as c1:
            raw = sb("raw8", [P, 4, 512], F32, c1)
            pW = ps("pW8", [P, 4, 512], F32, c1)
            raw_in = [sem(f"m_raw_in{k}") for k in range(4)]
            wT_mm, wT_out = sem("m_wT_mm"), sem("m_wT_out")
            w13v = u.w13.rearrange("e (r a p) h -> p (e r) a h", a=2, p=P)
            w2v = u.w2.rearrange("e (r p) f -> p (e r) f", p=P)
            N1, N2 = NR // 2, NR2
            with nc.Block() as block:
                @block.sync
                def _(sp):
                    with sp.Fori(0, N1 // 4) as i:
                        for k in range(4):
                            sp.wait_ge(wT_mm, 4 * i + k + 1)
                            sp.dma_start(raw[:, k, :].rearrange("p (a h) -> p a h", a=2),
                                         w13v[:, 4 * i + k, :, :]).then_inc(raw_in[k], 16)
                    with sp.Fori(0, N2 // 4) as i:
                        for k in range(4):
                            sp.wait_ge(wT_mm, N1 + 4 * i + k + 1)
                            sp.dma_start(raw[:, k, :], w2v[:, 4 * i + k, :]).then_inc(raw_in[k], 16)

                @block.tensor
                def _(pe):
                    pe.sem_inc(wT_mm, 4)
                    with pe.Fori(0, (N1 + N2) // 4) as i:
                        for k in range(4):
                            pe.wait_ge(raw_in[k], 16 * i + 16)
                            pe.wait_ge(wT_out, 4 * i + k + 1)
                            for a in range(4):
                                last = nc.tensor.transpose(pW[:, k, a * P:(a + 1) * P], raw[:, k, a * P:(a + 1) * P],
                                                           ident[:, :])
                            last.then_inc(wT_mm, 1)

                @block.vector
                def _(dve):
                    dve.sem_inc(wT_out, 4)
                    with dve.Fori(0, N1 // 4) as i:
                        for k in range(4):
                            dve.wait_ge(wT_mm, 4 * i + k + 5)
                            nc.vector.tensor_copy(
                                w13T[:, :, bass.ds((4 * i + k) * 2 * P, 2 * P)].rearrange("p c (a n) -> p a c n", a=2),
                                pW[:, k, :].rearrange("p (a c n) -> p a c n", a=2, c=C)).then_inc(wT_out, 1)
                    with dve.Fori(0, N2 // 4) as i:
                        for k in range(4):
                            dve.wait_ge(wT_mm, N1 + 4 * i + k + 5)
                            nc.vector.tensor_copy(w2T[:, :, bass.ds((4 * i + k) * P, P)],
                                                  pW[:, k, :].rearrange("p (a n) -> p a n", a=4)).then_inc(wT_out, 1)
        with ExitStack() as c2:
            FC = FFN // P
            R = 4
            LAST = MAXT - 1
            xq = sb("xq8", [P, R, H], F32, c2)
            xqT = sb("xqT8", [P, 2, C, P], F32, c2)
            sil = sb("sil8", [P, 2, FFN], F32, c2)
            gg = sb("gg8", [P, 2, FFN], F32, c2)
            gT = sb("gT8", [P, 2, FC, P], F32, c2)
            y = sb("y8", [P, R, H], F32, c2)
            pH = ps("pH8", [P, 2, 2, FFN], F32, c2)
            pX = ps("pX8", [P, C, P], F32, c2)
            pG = ps("pG8", [P, FC, P], F32, c2)
            pY = ps("pY8", [P, H], F32, c2)
            xq_in = [sem(f"m_xq_in{k}") for k in range(R)]
            y_put = [sem(f"m_y_put{k}") for k in range(R)]
            names = ("x_T", "x_out", "up", "sil", "gated", "g_T", "g_out", "down", "y_out")
            s = Names({n: sem("m_" + n) for n in names})
            assert (MAXT - R) % R == 0

            def steps(eng, step):
                with eng.Fori(0, MAXT // R - 1) as i:
                    for k in range(R):
                        step(R * i + k + 1, (k + 1) % R, i + (k + 1) // R)
                for j in range(MAXT - R + 1, MAXT):
                    step(j, j % R, j // R)

            with nc.Block() as block:
                @block.sync
                def _(sp):
                    def load(j, k):
                        row = sp.value_load(v.tile_in[0:1, bass.ds(j, 1)], min_val=0, max_val=E * CAP - P)
                        sp.dma_start(xq[:, k, :], v.queue[bass.ds(row, P), :]).then_inc(xq_in[k], 16)

                    def put(j, k):
                        sp.wait_ge(s.y_out, j + 2)
                        sp.dma_start(v.results[bass.ds(j * P, P), :], y[:, k, :]).then_inc(y_put[k], 16)
                    for k in range(R):
                        load(k, k)
                    with sp.Fori(0, MAXT // R - 1) as i:
                        for k in range(R):
                            wait_apart(sp, s.x_T, R * i + k + 1)
                            load(R * i + k + R, k)
                            put(R * i + k, k)
                    for k in range(R):
                        put(MAXT - R + k, k)
                    for k in range(R):
                        sp.wait_ge(y_put[k], 16 * (MAXT // R) + 16)

                @block.tensor
                def _(pe):
                    def turn(j, k, i):
                        pe.wait_ge(xq_in[k], 16 * i + 16)
                        pe.wait_ge(s.x_out, j + 1)
                        for c in range(C):
                            last = nc.tensor.transpose(pX[:, c, :], xq[:, k, c * P:(c + 1) * P], ident[:, :])
                        last.then_inc(s.x_T, 1)

                    def up(j, k):
                        e = pe.value_load(v.tile_expert[0:1, bass.ds(j, 1)], min_val=0, max_val=E - 1)
                        pe.wait_ge(s.x_out, j + 2)
                        pe.wait_ge(s.gated, j + 1)
                        for a in range(2):
                            for c in range(C):
                                last = nc.tensor.matmul(pH[:, k % 2, a, :], xqT[:, k % 2, c, :],
                                                        w13T[:, c, bass.ds(e * (2 * FFN) + a * FFN, FFN)],
                                                        start=(c == 0), stop=(c == C - 1))
                        last.then_inc(s.up, 1)

                    def turn_gated(j, k):
                        pe.wait_ge(s.gated, j + 3)
                        pe.wait_ge(s.g_out, j + 1)
                        for f in range(FC):
                            last = nc.tensor.transpose(pG[:, f, :], gg[:, k % 2, f * P:(f + 1) * P], ident[:, :])
                        last.then_inc(s.g_T, 1)

                    def down(j, k):
                        e = pe.value_load(v.tile_expert[0:1, bass.ds(j, 1)], min_val=0, max_val=E - 1)
                        pe.wait_ge(s.g_out, j + 2)
                        pe.wait_ge(s.y_out, j + 1)
                        for f in range(FC):
                            last = nc.tensor.matmul(pY[:, :], gT[:, k % 2, f, :], w2T[:, f, bass.ds(e * H, H)],
                                                    start=(f == 0), stop=(f == FC - 1))
                        last.then_inc(s.down, 1)

                    def step(j, k, i):
                        if not isinstance(j, int) or j < LAST:
                            up(j + 1, k + 1)
                        turn_gated(j, k)
                        if not isinstance(j, int) or j + 1 < LAST:
                            turn(j + 2, (k + 2) % R, i + (k + 2) // R)
                        down(j - 1, k + 1)
                    turn(0, 0, 0)
                    up(0, 0)
                    turn(1, 1, 0)
                    up(1, 1)
                    turn_gated(0, 0)
                    turn(2, 2, 0)
                    steps(pe, step)
                    down(LAST, LAST % R)

                @block.scalar
                def _(act):
                    act.sem_inc(s.x_out, 1)
                    act.sem_inc(s.y_out, 1)

                    def turned(j, k, first=False):
                        act.wait_ge(s.x_T, j + 1)
                        if not first:
                            act.wait_ge(s.up, j - 1)
                        nc.scalar.copy(xqT[:, k % 2], pX[:, :, :]).then_inc(s.x_out, 1)

                    def silu(j, k):
                        act.wait_ge(s.up, j + 1)
                        act.wait_ge(s.gated, j + 1)
                        nc.scalar.activation(sil[:, k % 2, :], pH[:, k % 2, 0, :], ACT.Silu).then_inc(s.sil, 1)

                    def result(j, k, i):
                        act.wait_ge(s.down, j + 1)
                        act.wait_ge(y_put[k], 16 * i + 16)
                        nc.scalar.copy(y[:, k, :], pY[:, :]).then_inc(s.y_out, 1)

                    def step(j, k, i):
                        if not isinstance(j, int) or j < LAST:
                            silu(j + 1, k + 1)
                        if not isinstance(j, int) or j + 1 < LAST:
                            turned(j + 2, k)
                        result(j - 1, (k - 1) % R, i + (k - 1) // R)
                    for k in range(R):
                        act.sem_inc(y_put[k], 16)
                    turned(0, 0, True)
                    turned(1, 1, True)
                    silu(0, 0)
                    silu(1, 1)
                    turned(2, 2)
                    steps(act, step)
                    result(LAST, LAST % R, LAST // R)

                @block.vector
                def _(dve):
                    dve.sem_inc(s.gated, 2)
                    dve.sem_inc(s.g_out, 1)

                    def gate(j, k):
                        dve.wait_ge(s.sil, j + 1)
                        nc.vector.tensor_tensor(gg[:, k % 2, :], sil[:, k % 2, :], pH[:, k % 2, 1, :],
                                                ALU.mult).then_inc(s.gated, 1)

                    def turned(j, k):
                        dve.wait_ge(s.g_T, j + 1)
                        nc.vector.tensor_copy(gT[:, k % 2], pG[:, :, :]).then_inc(s.g_out, 1)

                    def step(j, k, i):
                        turned(j, k)
                        if not isinstance(j, int) or j < LAST:
                            gate(j + 1, k + 1)
                    gate(0, 0)
                    gate(1, 1)
                    turned(0, 0)
                    steps(dve, step)


def stage9(nc, sb, ps, sem, env, base_env):
    v, u = Names(env), base_env
    G = 4
    with ExitStack() as ctx:
        rows_now = sb("rows_now", [P, G, 2], I32, ctx)
        yy = sb("yy9", [P, G, 2, H], F32, ctx)
        o = sb("o9", [P, G, H], F32, ctx)
        got = [sem(f"f_got{k}") for k in range(G)]
        put = [sem(f"f_put{k}") for k in range(G)]
        s = Names({n: sem("f_" + n) for n in ("rows", "half", "sum")})
        out_rows = u.out.rearrange("b (t p) h -> p (b t) h", p=P)
        with nc.Block() as block:
            @block.gpsimd
            def _(pool):
                with pool.Fori(0, T // G) as i:
                    for k in range(G):
                        nc.gpsimd.tensor_copy(rows_now[:, k, :], v.rows[:, G * i + k, :]).then_inc(s.rows, 1)
                    for k in range(G):
                        pool.wait_ge(s.rows, G * i + k + 1)
                        pool.wait_ge(s.half, G * i + k + 1)
                        wait_apart(pool, s.sum, G * i + k + 1)
                        for a in range(2):
                            nc.gpsimd.indirect_dma_start(
                                out=yy[:, k, a, :], out_offset=None, in_=v.results[:, :],
                                in_offset=bass.IndirectOffsetOnAxis(ap=rows_now[:, k, a:a + 1], axis=0)).then_inc(got[k], 16)
                    for k in range(G):
                        pool.wait_ge(got[k], 32 * i + 32)

            @block.vector
            def _(dve):
                dve.sem_inc(s.half, G)
                dve.sem_inc(s.sum, G)
                with dve.Fori(0, T // G) as i:
                    for k in range(G):
                        t = G * i + k
                        dve.wait_ge(got[k], 32 * i + 32)
                        nc.vector.scalar_tensor_tensor(out=yy[:, k, 0, :], in0=yy[:, k, 0, :],
                                                       scalar=v.weights[:, t, 0:1], in1=u.x1[:, t, :], op0=ALU.mult,
                                                       op1=ALU.add).then_inc(s.half, 1)
                    for k in range(G):
                        t = G * i + k
                        dve.wait_ge(s.half, t + G + 1)
                        nc.vector.scalar_tensor_tensor(out=u.x1[:, t, :], in0=yy[:, k, 1, :],
                                                       scalar=v.weights[:, t, 1:2], in1=yy[:, k, 0, :], op0=ALU.mult,
                                                       op1=ALU.add).then_inc(s.sum, 1)

            @block.sync
            def _(sp):
                with sp.Fori(0, T // G) as i:
                    for k in range(G):
                        sp.wait_ge(s.sum, G * i + k + 1 + G)
                        sp.dma_start(out_rows[:, G * i + k, :], u.x1[:, G * i + k, :]).then_inc(put[k], 16)
                    for k in range(G):
                        wait_apart(sp, put[k], 16 * i + 16)


_INS = ["attn_" + n for n in ("hidden_states", "Wq", "bq", "Wk", "bk", "Wv", "bv", "Wo", "bo", "Wg", "bg", "Wc", "bc", "Ws",
                              "bs")] + ["ffn_" + n for n in ("ln1_w", "ln2_w", "wqkv", "wo", "gate_w", "w13", "w2")]


def rotary_tables():
    inv = (1.0 / np.power(np.float32(10000.0), np.arange(0, HD, 2, dtype=np.float32) / np.float32(HD))).astype(np.float32)
    angle = np.arange(L, dtype=np.float32)[:, None] * inv[None, :]
    return np.cos(angle).astype(np.float32), np.sin(angle).astype(np.float32)


def kernel(**inputs):
    import concourse.bacc as _bacc
    from concourse.bass_utils import run_bass_kernel_spmd as _run

    nc = _bacc.Bacc("TRN2", target_bir_lowering=False, num_devices=1)
    arrays, args = {}, []
    for name in _INS:
        arrays[f"in_{name}_dram"] = np.ascontiguousarray(inputs["L0_" + name])
    arrays["in_cos_dram"], arrays["in_sin_dram"] = rotary_tables()
    for name, a in arrays.items():
        args.append(nc.dram_tensor(name, a.shape, mybir.dt.from_np(a.dtype), kind="ExternalInput").ap())
    args.append(nc.dram_tensor("out_0_dram", (B, L, H), F32, kind="ExternalOutput").ap())
    build(nc, *args)
    r = _run(nc, [arrays], core_ids=[0])
    return r.results[0]["out_0_dram"]
```

```python
from contextlib import ExitStack

import concourse.bass as bass
import numpy as np
from concourse import mybir

F32 = mybir.dt.float32
BF16 = mybir.dt.bfloat16
I32 = mybir.dt.int32
U32 = mybir.dt.uint32
ALU = mybir.AluOpType
ACT = mybir.ActivationFunctionType
AX = mybir.AxisListType

P = 128
B, L, H = 2, 2048, 256
C = H // P
T = B * L // P
TB = L // P
RATIO = 4
NBLK = L // RATIO
CT = NBLK // P
SEL = 128
WIN = 64
SCALE = 0.25
NH, NKV, HD = 16, 4, 16
GRP = NH // NKV
QKVW = (NH + 2 * NKV) * HD
E = 8
FFN = 512
NEG = -1e30


class Names(dict):

    def __getattr__(self, name):
        return self[name]


class Chain:

    def __init__(self, eng, sem, base=0):
        self.eng, self.sem, self.base, self.k = eng, sem, base, 0

    def at(self, base):
        self.base, self.k = base, 0

    def link(self, ins, apart=False):
        self.k += 1
        ins.then_inc(self.sem, 1)
        if apart:
            wait_apart(self.eng, self.sem, self.base + self.k)
        else:
            self.eng.wait_ge(self.sem, self.base + self.k)


PASSED = []


def wait_apart(eng, sem, value):
    eng.wait_ge(sem, value)
    eng.sem_inc(PASSED[0], 1)


def build(nc, x, Wq, bq, Wk, bk, Wv, bv, Wo, bo, Wg, bg, Wc, bc, Ws, bs,
          ln1_w, ln2_w, wqkv, wo, gate_w, w13, w2, cos_t, sin_t, out):
    with ExitStack() as whole:
        def sb(name, shape, dt=F32, ctx=whole):
            return ctx.enter_context(nc.sbuf_tensor(name, shape, dt))

        def ps(name, shape, dt=F32, ctx=whole):
            return ctx.enter_context(nc.psum_tensor(name, shape, dt))

        stage_sems = []

        def sem(name):
            stage_sems.append(nc.alloc_semaphore(name=name))
            return stage_sems[-1]

        def free_semaphores():
            nc.clear_and_free_semaphores(list(stage_sems))
            stage_sems.clear()
            nc.all_engine_barrier()

        PASSED[:] = [nc.alloc_semaphore(name="passed")]
        ident = sb("ident", [P, P])
        ones = sb("ones", [P, P])
        x1 = sb("x1", [P, T, H])
        halfpow = sb("halfpow", [P, 1])
        x_rows = x.rearrange("b (t p) h -> p (b t) h", p=P)

        with ExitStack() as layer1:
            def sb1(name, shape, dt=F32):
                return sb(name, shape, dt, layer1)
            base = sb1("base", [P, T, H])
            xnT = sb1("xnT", [P, C, B * L])
            wq_s, wk_s, wv_s = (sb1(n, [P, C, H]) for n in ("wq_s", "wk_s", "wv_s"))
            wo_s = sb1("wo_s", [P, 3 * C, H])
            wc_s = sb1("wc_s", [P, RATIO * C, H])
            wgs = sb1("wgs", [P, C, 4])
            bgs = sb1("bgs", [1, 4])
            bqk = sb1("bqk", [P, 3, C])
            bv_r = sb1("bv_r", [1, H])
            bo_b = sb1("bo_b", [P, H])
            GS = sb1("GS", [P, T, 4])

            stage1(nc, layer1, sb, ps, sem, locals())
            stage23(nc, layer1, sb, ps, sem, locals())
            stage4(nc, layer1, sb, ps, sem, locals())
            free_semaphores()
        stages_layer2(nc, whole, sb, ps, sem, locals())


def stage1(nc, layer, sb, ps, sem, env):
    v = Names(env)
    x_rows, x1, base, xnT, ident, ones, GS = v.x_rows, v.x1, v.base, v.xnT, v.ident, v.ones, v.GS
    G = 4
    with ExitStack() as ctx:
        stats = sb("stats", [P, 2, G, 6], F32, ctx)
        mv = sb("mv", [P, 2, G, 2], F32, ctx)
        rstd = sb("rstd", [P, 2, G], F32, ctx)
        xf = sb("xf", [P, G, H], F32, ctx)
        xTf = sb("xTf", [P, 2, 2, C, P], F32, ctx)
        pT = ps("pT", [P, 2, 2, C, P], F32, ctx)
        pG = ps("pG", [P, 512], F32, ctx)
        x_in = [sem(f"x_in{k}") for k in range(G)]
        w_in, small_in, const0, const1 = sem("w_in"), sem("small_in"), sem("const0"), sem("const1")
        stats_v, stats_done, var_eps, rstd_done, normed, base_copied = (sem(n) for n in
            ("stats_v", "stats_done", "var_eps", "rstd_done", "normed", "base_copied"))
        transposed, xT_done, xnT_copied, gates_mm, gates_out = (sem(n) for n in
            ("transposed", "xT_done", "xnT_copied", "gates_mm", "gates_out"))
        with nc.Block() as block:
            @block.sync
            def _(sp):
                def load(i, k):
                    sp.dma_start(x1[:, i * G + k, :], x_rows[:, i * G + k, :]).then_inc(x_in[k], 16)
                for k in range(G):
                    load(0, k)
                with sp.Fori(1, T // G) as i:
                    for k in range(G):
                        sp.wait_ge(x_in[k], 16 * i)
                        load(i, k)

            @block.scalar
            def _(act):
                act.dma_start(v.wgs[:, :, 0:3], v.Wg.rearrange("(c p) n -> p c n", p=P)).then_inc(small_in, 16)
                act.dma_start(v.wgs[:, :, 3:4], v.Ws.rearrange("(c p) n -> p c n", p=P), allow_slow_non_contiguous=True).then_inc(small_in, 16)
                act.dma_start(v.bgs[:, 0:3], v.bg.rearrange("(a n) -> a n", a=1)).then_inc(small_in, 16)
                act.dma_start(v.bgs[:, 3:4], v.bs.rearrange("(a n) -> a n", a=1)).then_inc(small_in, 16)
                for dst, src in ((v.wc_s, v.Wc), (v.wq_s, v.Wq), (v.wk_s, v.Wk), (v.wv_s, v.Wv), (v.wo_s, v.Wo)):
                    act.dma_start(dst[:, :, :], src.rearrange("(c p) n -> p c n", p=P)).then_inc(w_in, 16)
                for n, src in enumerate((v.bq, v.bk, v.bc)):
                    act.dma_start(v.bqk[:, n, :], src.rearrange("(c p) -> p c", p=P), allow_slow_non_contiguous=True).then_inc(w_in, 16)
                act.dma_start(v.bv_r[:, :], v.bv.rearrange("(a n) -> a n", a=1)).then_inc(w_in, 16)
                act.dma_start(v.bo_b[:, :], v.bo.partition_broadcast(P)).then_inc(w_in, 16)
                act.sem_inc(xnT_copied, 2)
                with act.Fori(0, T // G) as i:
                    for g in range(2):
                        act.wait_ge(transposed, 2 * i + g + 3)
                        act.wait_ge(gates_mm, 2 * i + g + 1)
                        act.wait_ge(xnT_copied, 2 * i + g + 1)
                        nc.scalar.copy(xTf[:, g], pT[:, g]).then_inc(xT_done, 1)
                        wait_apart(act, xT_done, 2 * i + g + 1)
                        nc.scalar.copy(
                            xnT[:, :, bass.ds((i * G + 2 * g) * P, 2 * P)].rearrange("p c (t n) -> p c t n", t=2),
                            xTf[:, g].rearrange("p t c n -> p c t n")).then_inc(xnT_copied, 1)
                act.wait_ge(w_in, 160)

            @block.gpsimd
            def _(pool):
                nc.gpsimd.memset(ident[:, :], 0.0).then_inc(const0, 1)
                nc.gpsimd.memset(ones[:, :], 1.0).then_inc(const0, 1)
                nc.gpsimd.memset(v.halfpow[:, :], -0.5).then_inc(const0, 1)
                pool.wait_ge(const0, 3)
                nc.gpsimd.affine_select(out=ident[:, :], in_=ident[:, :], compare_op=ALU.not_equal, fill=1.0,
                                        base=0, pattern=[[-1, P]], channel_multiplier=1).then_inc(const1, 1)
                pool.sem_inc(base_copied, 1)
                with pool.Fori(0, T // G) as i:
                    wait_apart(pool, stats_done, G * i + G)
                    nc.gpsimd.tensor_scalar(rstd[:, 0, :], mv[:, 0, :, 1], 1e-5, None, ALU.add).then_inc(var_eps, 1)
                    pool.wait_ge(var_eps, i + 1)
                    nc.gpsimd.tensor_tensor(rstd[:, 1, :], rstd[:, 0, :], v.halfpow[:, :].to_broadcast([P, G]),
                                            ALU.pow).then_inc(rstd_done, 1)
                    wait_apart(pool, normed, G * i + G)
                    nc.gpsimd.tensor_copy(base[:, bass.ds(i * G, G), :], xf[:, :, :]).then_inc(base_copied, 1)

            @block.vector
            def _(dve):
                def gates(i):
                    dve.wait_ge(gates_mm, 2 * i + 4)
                    nc.vector.tensor_copy(GS[:, bass.ds(i * G, G), :],
                                          pG[:, 0:4 * G].rearrange("p (t n) -> p t n", n=4)).then_inc(gates_out, 1)

                def step(i, first=False):
                    for k in range(G):
                        dve.wait_ge(x_in[k], 16 * i + 16)
                        nc.vector.bn_stats(stats[:, 0, k, :], x1[:, i * G + k, :]).then_inc(stats_v, 1)
                    for k in range(G):
                        wait_apart(dve, stats_v, G * i + k + 1)
                        nc.vector.bn_aggr(mv[:, 0, k, :], stats[:, 0, k, :]).then_inc(stats_done, 1)
                    if not first:
                        gates(i - 1)
                    dve.wait_ge(rstd_done, i + 1)
                    dve.wait_ge(stats_done, G * i + G)
                    dve.wait_ge(transposed, 2 * i + 2)
                    dve.wait_ge(base_copied, i + 1)
                    for k in range(G):
                        nc.vector.tensor_scalar(xf[:, k, :], x1[:, i * G + k, :], mv[:, 0, k, 0:1],
                                                rstd[:, 1, k:k + 1], ALU.subtract, ALU.mult).then_inc(normed, 1)
                step(0, first=True)
                with dve.Fori(1, T // G) as i:
                    step(i)
                gates(T // G - 1)

            @block.tensor
            def _(pe):
                pe.wait_ge(const1, 1)
                pe.wait_ge(small_in, 64)
                pe.sem_inc(transposed, 2)
                pe.sem_inc(gates_mm, 2)
                with pe.Fori(0, T // G) as i:
                    for g in range(2):
                        pe.wait_ge(normed, G * i + 2 * g + 2)
                        for k in range(2):
                            for c in range(C):
                                last = nc.tensor.transpose(pT[:, g, k, c, :],
                                                           xf[:, 2 * g + k, c * P:(c + 1) * P], ident[:, :])
                        last.then_inc(transposed, 1)
                    for g in range(2):
                        pe.wait_ge(xT_done, 2 * i + g + 1)
                        for k in range(2):
                            n = 4 * (2 * g + k)
                            nc.tensor.matmul(pG[:, n:n + 4], xTf[:, g, k, 0, :], v.wgs[:, 0, :], start=True, stop=False)
                            nc.tensor.matmul(pG[:, n:n + 4], xTf[:, g, k, 1, :], v.wgs[:, 1, :], start=False, stop=False)
                            last = nc.tensor.matmul(pG[:, n:n + 4], ones[0:1, :], v.bgs[:, :], start=False, stop=True)
                        last.then_inc(gates_mm, 1)


def stage23(nc, layer, sb, ps, sem, env):
    v = Names(env)
    base, xnT, ident, ones, GS = v.base, v.xnT, v.ident, v.ones, v.GS
    with ExitStack() as ctx:
        compT, qcT, kcT = (sb(n, [P, B, C, NBLK], F32, ctx) for n in ("compT", "qcT", "kcT"))
        Vc = sb("Vc", [P, B, CT, H], F32, ctx)
        PC = sb("PC", [P, TB, B], F32, ctx)
        with ExitStack() as c2:
            S32 = sb("S32", [T, P], F32, c2)
            srow = sb("srow", [B, L], F32, c2)
            work = sb("work", [B, L], F32, c2)
            above, equal, cum = work, sb("equal", [B, L], F32, c2), sb("cum", [B, L], F32, c2)
            ones_row = sb("ones_row", [B, L], F32, c2)
            best = sb("best", [B, 8], F32, c2)
            need = sb("need", [B, 2], F32, c2)
            eg = sb("eg", [P, T, 3], F32, c2)
            gsum = sb("gsum", [P, T], F32, c2)
            pJ = ps("pJ", [P, 2, 512], F32, c2)
            pS32 = ps("pS32", [T, P], F32, c2)
            pPC = ps("pPC", [P, TB, B], F32, c2)
            proj_mm, proj_out, s32_T, s32_out, srow_in, gate_exp, dve2, place_ready, place_T, place_out = (sem(n) for n in (
                "proj_mm", "proj_out", "s32_T", "s32_out", "srow_in", "gate_exp", "dve2", "place_ready", "place_T",
                "place_out"))
            with nc.Block() as block:
                @block.sync
                def _(sp):
                    sp.wait_ge(s32_out, 1)
                    for b in range(B):
                        sp.dma_start(srow[b:b + 1, :].rearrange("a (t n) -> a t n", n=P),
                                     S32[b * TB:(b + 1) * TB, :]).then_inc(srow_in, 16)
                    sp.wait_ge(srow_in, 16 * B)

                @block.tensor
                def _(pe):
                    nc.tensor.transpose(pS32[:, :], GS[:, :, 3], ident[:, :]).then_inc(s32_T, 1)
                    n = 0

                    def bank():
                        if n >= 2:
                            pe.wait_ge(proj_out, n - 1)
                        return pJ[:, n % 2]
                    for b in range(B):
                        for m in range(C):
                            o = bank()
                            for k in range(RATIO * C):
                                r, c = k // C, k % C
                                last = nc.tensor.matmul(o, v.wc_s[:, k, m * P:(m + 1) * P],
                                                        xnT[:, c, bass.ds(b * L + r, NBLK, RATIO)],
                                                        start=(k == 0), stop=(k == RATIO * C - 1))
                            last.then_inc(proj_mm, 1)
                            n += 1
                    for b in range(B):
                        pe.wait_ge(proj_out, 2 * b + 2)
                        for w in (v.wq_s, v.wk_s):
                            for m in range(C):
                                o = bank()
                                for c in range(C):
                                    last = nc.tensor.matmul(o, w[:, c, m * P:(m + 1) * P], compT[:, b, c, :],
                                                            start=(c == 0), stop=(c == C - 1))
                                last.then_inc(proj_mm, 1)
                                n += 1
                    for b in range(B):
                        for i in range(CT):
                            o = bank()[:, 0:H]
                            for c in range(C):
                                nc.tensor.matmul(o, compT[:, b, c, i * P:(i + 1) * P], v.wv_s[:, c, :],
                                                 start=(c == 0), stop=False)
                            nc.tensor.matmul(o, ones[0:1, :], v.bv_r[:, :], start=False, stop=True).then_inc(proj_mm, 1)
                            n += 1
                    pe.wait_ge(place_ready, 1)
                    for t in range(TB):
                        last = nc.tensor.transpose(pPC[:, t, :], srow[:, t * P:(t + 1) * P], ident[0:B, 0:B])
                    last.then_inc(place_T, 1)

                @block.scalar
                def _(act):
                    nc.scalar.activation(eg[:, :, :], GS[:, :, 0:3], ACT.Exp, scale=-1.0).then_inc(gate_exp, 1)
                    n = 0
                    for b in range(B):
                        for m in range(C):
                            act.wait_ge(proj_mm, n + 1)
                            nc.scalar.activation(compT[:, b, m, :], pJ[:, n % 2], ACT.Identity,
                                                 bias=v.bqk[:, 2, m:m + 1]).then_inc(proj_out, 1)
                            n += 1
                    for b in range(B):
                        for w, dst in ((0, qcT), (1, kcT)):
                            for m in range(C):
                                act.wait_ge(proj_mm, n + 1)
                                nc.scalar.activation(dst[:, b, m, :], pJ[:, n % 2], ACT.Identity,
                                                     bias=v.bqk[:, w, m:m + 1]).then_inc(proj_out, 1)
                                n += 1
                    for b in range(B):
                        for i in range(CT):
                            act.wait_ge(proj_mm, n + 1)
                            nc.scalar.copy(Vc[:, b, i, :], pJ[:, n % 2, 0:H]).then_inc(proj_out, 1)
                            n += 1

                @block.vector
                def _(dve):
                    ch = Chain(dve, dve2)
                    dve.wait_ge(s32_T, 1)
                    nc.vector.tensor_copy(S32[:, :], pS32[:, :]).then_inc(s32_out, 1)
                    dve.wait_ge(gate_exp, 1)
                    ch.link(nc.vector.tensor_scalar(eg[:, :, :], eg[:, :, :], 1.0, None, ALU.add))
                    ch.link(nc.vector.reciprocal(eg[:, :, :], eg[:, :, :]))
                    ch.link(nc.vector.reduce_sum(gsum[:, :], eg[:, :, :], AX.X))
                    ch.link(nc.vector.tensor_scalar(gsum[:, :], gsum[:, :], 1e-6, None, ALU.add))
                    ch.link(nc.vector.reciprocal(gsum[:, :], gsum[:, :]))
                    ch.link(nc.vector.tensor_tensor(GS[:, :, 0:3], eg[:, :, :],
                                                    gsum[:, :].unsqueeze(2).to_broadcast([P, T, 3]), ALU.mult))
                    ch.link(nc.vector.memset(ones_row[:, :], 1.0))
                    dve.wait_ge(srow_in, 16 * B)
                    ch.link(nc.vector.tensor_copy(work[:, :], srow[:, :]))
                    done = ch.k
                    with dve.Fori(0, SEL // 8) as i:
                        ch.at(2 * i + done)
                        ch.link(nc.vector.max(best[:, :], work[:, :]), apart=True)
                        ch.link(nc.vector.match_replace(work[:, :], best[:, :], work[:, :], -3e38), apart=True)
                    ch.at(done + 2 * (SEL // 8))
                    least = best[:, 7:8]
                    ch.link(nc.vector.tensor_scalar(above[:, :], srow[:, :], least, 0.0, ALU.is_gt, ALU.add,
                                                    accum_out=need[:, 0:1]))
                    ch.link(nc.vector.tensor_scalar(equal[:, :], srow[:, :], least, None, ALU.is_equal))
                    ch.link(nc.vector.tensor_scalar(need[:, 1:2], need[:, 0:1], -1.0, float(SEL), ALU.mult, ALU.add))
                    ch.link(nc.vector.tensor_tensor_scan(cum[:, :], ones_row[:, :], equal[:, :], 0.0, ALU.mult, ALU.add))
                    ch.link(nc.vector.scalar_tensor_tensor(out=equal[:, :], in0=cum[:, :], scalar=need[:, 1:2],
                                                           in1=equal[:, :], op0=ALU.is_le, op1=ALU.mult))
                    ch.link(nc.vector.tensor_tensor(above[:, :], above[:, :], equal[:, :], ALU.add))
                    ch.link(nc.vector.tensor_tensor_scan(cum[:, :], ones_row[:, :], above[:, :], 0.0, ALU.mult, ALU.add))
                    nc.vector.tensor_tensor(srow[:, :], cum[:, :], above[:, :], ALU.mult).then_inc(place_ready, 1)
                    dve.wait_ge(place_T, 1)
                    nc.vector.tensor_scalar(PC[:, :, :], pPC[:, :, :], -1.0, None, ALU.add).then_inc(place_out, 1)
                    dve.wait_ge(place_out, 1)

        with ExitStack() as c3:
            iota_i = sb("iota_i", [P, P], I32, c3)
            iota_f = sb("iota_f", [P, P], F32, c3)
            OH = sb("OH", [P, B, TB, P], F32, c3)
            selT = sb("selT", [P, B, C, SEL], F32, c3)
            qksT = sb("qksT", [P, B, 2, C, SEL], F32, c3)
            Vs = sb("Vs", [P, B, H], F32, c3)
            nmax = sb("nmax", [P, 2, 2], F32, c3)
            rs = sb("rs", [P, 2, 2], F32, c3)
            prob = sb("prob", [P, 2, 512], F32, c3)
            probT = sb("probT", [P, 2, 4, P], F32, c3)
            ctxT = sb("ctxT", [P, 2, C, P], F32, c3)
            pS = ps("pS3", [P, 2, 512], F32, c3)
            pPT = ps("pPT3", [P, 4, P], F32, c3)
            pC = ps("pC3", [P, C, P], F32, c3)
            pO = ps("pO3", [P, H], F32, c3)
            pX = ps("pX3", [P, 512], F32, c3)
            pV = ps("pV3", [P, H], F32, c3)
            iota_in, iota_done, onehot, sel_mm, sel_out, selqk_mm, selqk_out, selv_mm, selv_out, bo_in = (sem(n) for n in (
                "iota_in", "iota_done", "onehot", "sel_mm", "sel_out", "selqk_mm", "selqk_out", "selv_mm", "selv_out",
                "bo_in"))
            scores, rowmax, negmax, expd, rowsum, share, weighed, probT_mm, probT_out, ctx_mm, ctx_out, out_mm, added = (
                sem("a_" + n) for n in ("scores", "rowmax", "negmax", "expd", "rowsum", "share", "weighed", "probT_mm",
                                        "probT_out", "ctx_mm", "ctx_out", "out_mm", "added"))
            tiles = [(b, i, CT, 0) for b in range(B) for i in range(CT)] + [(b, 0, 1, 1) for b in range(B)]
            N = len(tiles)
            with nc.Block() as block:
                @block.gpsimd
                def _(pool):
                    nc.gpsimd.iota(iota_i[:, :], pattern=[[1, P]], base=0, channel_multiplier=0).then_inc(iota_in, 1)
                    pool.wait_ge(iota_in, 1)
                    nc.gpsimd.tensor_copy(iota_f[:, :], iota_i[:, :]).then_inc(iota_done, 1)
                    pool.wait_ge(sel_mm, B)
                    for t in list(range(0, TB * B, CT)):
                        last = nc.gpsimd.tensor_tensor(base[:, t:t + CT, :], base[:, t:t + CT, :],
                                                       v.bo_b[:, :].unsqueeze(1).to_broadcast([P, CT, H]), ALU.add)
                        last.then_inc(bo_in, 1)

                @block.tensor
                def _(pe):
                    for b in range(B):
                        pe.wait_ge(onehot, TB * (b + 1))
                        if b:
                            pe.wait_ge(sel_out, b)
                        for c in range(C):
                            for t in range(TB):
                                last = nc.tensor.matmul(pX[:, c * P:(c + 1) * P], base[:, b * TB + t, c * P:(c + 1) * P],
                                                        OH[:, b, t, :], start=(t == 0), stop=(t == TB - 1))
                        last.then_inc(sel_mm, 1)
                    for b in range(B):
                        pe.wait_ge(sel_out, b + 1 if b == 0 else B)
                        if b == 0:
                            pe.wait_ge(sel_out, B)
                        else:
                            pe.wait_ge(selqk_out, 2 * C * b)
                            pe.wait_ge(selv_out, b)
                        for w, W in ((0, v.wq_s), (1, v.wk_s)):
                            for m in range(C):
                                for c in range(C):
                                    last = nc.tensor.matmul(pX[:, (w * C + m) * P:(w * C + m + 1) * P],
                                                            W[:, c, m * P:(m + 1) * P], selT[:, b, c, :],
                                                            start=(c == 0), stop=(c == C - 1))
                        last.then_inc(selqk_mm, 1)
                        for c in range(C):
                            nc.tensor.matmul(pV[:, :], selT[:, b, c, :], v.wv_s[:, c, :], start=(c == 0), stop=False)
                        nc.tensor.matmul(pV[:, :], ones[0:1, :], v.bv_r[:, :], start=False, stop=True).then_inc(selv_mm, 1)

                    def tile_scores(n):
                        b, i, kt, sel = tiles[n]
                        if n >= 2:
                            pe.wait_ge(expd, n - 1)
                        if sel:
                            pe.wait_ge(selqk_out, 2 * C * (b + 1))
                        for c in range(C):
                            q = qksT[:, b, 0, c, :] if sel else qcT[:, b, c, i * P:(i + 1) * P]
                            k = qksT[:, b, 1, c, :] if sel else kcT[:, b, c, :]
                            last = nc.tensor.matmul(pS[:, n % 2, 0:kt * P], q, k, start=(c == 0), stop=(c == C - 1))
                        last.then_inc(scores, 1)

                    def tile_transposes(n):
                        pe.wait_ge(weighed, n + 1)
                        if n >= 1:
                            pe.wait_ge(probT_out, n)
                        for k in range(tiles[n][2]):
                            last = nc.tensor.transpose(pPT[:, k, :], prob[:, n % 2, k * P:(k + 1) * P], ident[:, :])
                        last.then_inc(probT_mm, 1)

                    def tile_context(n):
                        b, i, kt, sel = tiles[n]
                        pe.wait_ge(probT_out, n + 1)
                        if n >= 1:
                            pe.wait_ge(ctx_out, n)
                        if sel:
                            pe.wait_ge(selv_out, b + 1)
                        for m in range(C):
                            for k in range(kt):
                                val = Vs[:, b, m * P:(m + 1) * P] if sel else Vc[:, b, k, m * P:(m + 1) * P]
                                last = nc.tensor.matmul(pC[:, m, :], val, probT[:, n % 2, k, :], start=(k == 0),
                                                        stop=(k == kt - 1))
                        last.then_inc(ctx_mm, 1)

                    def tile_output(n):
                        sel = tiles[n][3]
                        pe.wait_ge(ctx_out, n + 1)
                        if n >= 1:
                            pe.wait_ge(added, n)
                        for m in range(C):
                            last = nc.tensor.matmul(pO[:, :], ctxT[:, n % 2, m, :], v.wo_s[:, sel * C + m, :],
                                                    start=(m == 0), stop=(m == C - 1))
                        last.then_inc(out_mm, 1)
                    tile_scores(0)
                    for n in range(N):
                        if n + 1 < N:
                            tile_scores(n + 1)
                        tile_transposes(n)
                        if n >= 1:
                            tile_output(n - 1)
                        tile_context(n)
                    tile_output(N - 1)

                @block.scalar
                def _(act):
                    for b in range(B):
                        act.wait_ge(sel_mm, b + 1)
                        nc.scalar.copy(selT[:, b], pX[:, 0:C * P].rearrange("p (c n) -> p c n", n=P)).then_inc(sel_out, 1)
                    for b in range(B):
                        act.wait_ge(selqk_mm, b + 1)
                        for w in range(2):
                            for m in range(C):
                                nc.scalar.activation(qksT[:, b, w, m, :], pX[:, (w * C + m) * P:(w * C + m + 1) * P],
                                                     ACT.Identity, bias=v.bqk[:, w, m:m + 1]).then_inc(selqk_out, 1)
                        act.wait_ge(selv_mm, b + 1)
                        nc.scalar.copy(Vs[:, b, :], pV[:, :]).then_inc(selv_out, 1)

                    def tile_exp(n):
                        w = tiles[n][2] * P
                        act.wait_ge(negmax, n + 1)
                        if n >= 2:
                            act.wait_ge(probT_mm, n - 1)
                        nc.scalar.activation(prob[:, n % 2, 0:w], pS[:, n % 2, 0:w], ACT.Exp, scale=SCALE,
                                             bias=nmax[:, n % 2, 1:2], accum_out=rs[:, n % 2, 0:1]).then_inc(expd, 1)

                    def tile_ctx(n):
                        act.wait_ge(ctx_mm, n + 1)
                        if n >= 2:
                            act.wait_ge(out_mm, n - 1)
                        nc.scalar.copy(ctxT[:, n % 2], pC[:, :, :]).then_inc(ctx_out, 1)
                    tile_exp(0)
                    for n in range(N):
                        if n + 1 < N:
                            tile_exp(n + 1)
                        tile_ctx(n)

                @block.vector
                def _(dve):
                    dve.wait_ge(iota_done, 1)
                    for b in range(B):
                        for t in range(TB):
                            nc.vector.tensor_scalar(OH[:, b, t, :], iota_f[:, :], PC[:, t, b:b + 1], None,
                                                    ALU.is_equal).then_inc(onehot, 1)

                    def tile_max(n):
                        w = tiles[n][2] * P
                        dve.wait_ge(scores, n + 1)
                        nc.vector.reduce_max(nmax[:, n % 2, 0:1], pS[:, n % 2, 0:w], AX.X).then_inc(rowmax, 1)
                        dve.wait_ge(rowmax, n + 1)
                        nc.vector.tensor_scalar(nmax[:, n % 2, 1:2], nmax[:, n % 2, 0:1], -SCALE, None,
                                                ALU.mult).then_inc(negmax, 1)

                    def tile_share(n):
                        b, i, kt, sel = tiles[n]
                        w = kt * P
                        dve.wait_ge(expd, n + 1)
                        nc.vector.reciprocal(rs[:, n % 2, 1:2], rs[:, n % 2, 0:1]).then_inc(rowsum, 1)
                        dve.wait_ge(rowsum, n + 1)
                        nc.vector.tensor_scalar(prob[:, n % 2, 0:w], prob[:, n % 2, 0:w], rs[:, n % 2, 1:2],
                                                GS[:, b * TB + i, sel:sel + 1], ALU.mult, ALU.mult).then_inc(weighed, 1)
                        dve.wait_ge(probT_mm, n + 1)
                        if n >= 2:
                            dve.wait_ge(ctx_mm, n - 1)
                        nc.vector.tensor_copy(probT[:, n % 2, 0:kt, :], pPT[:, 0:kt, :]).then_inc(probT_out, 1)

                    def tile_add(n):
                        b, i, _, _ = tiles[n]
                        t = b * TB + i
                        dve.wait_ge(out_mm, n + 1)
                        dve.wait_ge(bo_in, t // CT + 1)
                        if n:
                            dve.wait_ge(added, n)
                        nc.vector.tensor_tensor(base[:, t, :], base[:, t, :], pO[:, :], ALU.add).then_inc(added, 1)
                    tile_max(0)
                    for n in range(N):
                        if n + 1 < N:
                            tile_max(n + 1)
                        tile_share(n)
                        if n >= 1:
                            tile_add(n - 1)
                    tile_add(N - 1)


def stage4(nc, layer, sb, ps, sem, env):
    v = Names(env)
    base, xnT, ident, ones, GS, x1 = v.base, v.xnT, v.ident, v.ones, v.GS, v.x1
    HALF = WIN // 2
    with ExitStack() as ctx:
        xs = sb("xs4", [P, 2, C, 2, WIN], F32, ctx)
        qkT = sb("qkT4", [P, 2, 2, C, P], F32, ctx)
        V = sb("V4", [P, 2, H], F32, ctx)
        nmax = sb("nmax4", [P, 2, 2], F32, ctx)
        rs = sb("rs4", [P, 2, 2], F32, ctx)
        prob = sb("prob4", [P, 2, WIN], F32, ctx)
        block_p = sb("block_p4", [P, 2, P], F32, ctx)
        probT = sb("probT4", [P, 2, P], F32, ctx)
        ctxT = sb("ctxT4", [P, 2, C, P], F32, ctx)
        z = sb("z4", [P, 2, H], F32, ctx)
        stats = sb("stats4", [P, 2, 6], F32, ctx)
        mv = sb("mv4", [P, 2, 2], F32, ctx)
        rstd = sb("rstd4", [P, 2, 3], F32, ctx)
        pQK = ps("pQK4", [P, 2, 2, C, P], F32, ctx)
        pV = ps("pV4", [P, H], F32, ctx)
        pS = ps("pS4", [P, 512], F32, ctx)
        pPT = ps("pPT4", [P, 512], F32, ctx)
        pC = ps("pC4", [P, C, P], F32, ctx)
        pO = ps("pO4", [P, H], F32, ctx)
        names = ("xs_in", "qk_mm", "qk_out", "v_mm", "v_out", "scores", "rowmax", "negmax", "expd", "rowsum", "weighed",
                 "probT_mm", "probT_out", "ctx_mm", "ctx_out", "out_mm", "z_sum", "z_stats", "z_mv", "z_rstd", "pow_in",
                 "z_norm", "x1_out", "zero4")
        s = Names({n: sem("w_" + n) for n in names})

        def pipelined(eng, step):
            for t in (0, 1):
                step(t, t, t)
            with eng.Fori(1, T // 2) as i:
                for k in range(2):
                    step(2 * i + k, k, 2)

        with nc.Block() as block:
            @block.gpsimd
            def _(pool):
                nc.gpsimd.memset(block_p[:, :, :], 0.0).then_inc(s.zero4, 1)

                def root(t, k, late):
                    wait_apart(pool, s.z_mv, t + 1)
                    nc.gpsimd.tensor_scalar(rstd[:, k, 0:1], mv[:, k, 1:2], 0.25, 1e-6, ALU.mult, ALU.add).then_inc(s.pow_in, 1)
                    pool.wait_ge(s.pow_in, t + 1)
                    if late:
                        pool.wait_ge(s.x1_out, t - 1)
                    nc.gpsimd.tensor_tensor(rstd[:, k, 1:2], rstd[:, k, 0:1], v.halfpow[:, :], ALU.pow).then_inc(s.z_rstd, 1)
                root(0, 0, False)
                root(1, 1, False)
                with pool.Fori(1, T // 2) as i:
                    for k in range(2):
                        root(2 * i + k, k, True)

            @block.tensor
            def _(pe):
                def project(t, k, first):
                    pe.wait_ge(s.xs_in, 2 * t + 2)
                    if first >= 2:
                        pe.wait_ge(s.qk_out, 4 * t - 4)
                    x_k = xs[:, k].rearrange("p c w n -> p c (w n)")
                    for w, W in ((0, v.wq_s), (1, v.wk_s)):
                        for m in range(C):
                            for c in range(C):
                                last = nc.tensor.matmul(pQK[:, k, w, m, :], W[:, c, m * P:(m + 1) * P], x_k[:, c, :],
                                                        start=(c == 0), stop=(c == C - 1))
                    last.then_inc(s.qk_mm, 1)
                    if first:
                        pe.wait_ge(s.v_out, t)
                    for c in range(C):
                        nc.tensor.matmul(pV[:, :], x_k[:, c, :], v.wv_s[:, c, :], start=(c == 0), stop=False)
                    nc.tensor.matmul(pV[:, :], ones[0:1, :], v.bv_r[:, :], start=False, stop=True).then_inc(s.v_mm, 1)

                def tile_scores(t, k, first):
                    pe.wait_ge(s.qk_out, 4 * t + 4)
                    if first:
                        pe.wait_ge(s.expd, t)
                    for w in range(2):
                        for c in range(C):
                            last = nc.tensor.matmul(pS[w * WIN:(w + 1) * WIN, 0:WIN],
                                                    qkT[:, k, 0, c, w * WIN:(w + 1) * WIN],
                                                    qkT[:, k, 1, c, w * WIN:(w + 1) * WIN],
                                                    start=(c == 0), stop=(c == C - 1))
                    last.then_inc(s.scores, 1)

                def tile_transposes(t, k, first):
                    pe.wait_ge(s.weighed, 2 * t + 2)
                    if first:
                        pe.wait_ge(s.probT_out, t)
                    nc.tensor.transpose(pPT[:, 0:P], block_p[:, k, :], ident[:, :]).then_inc(s.probT_mm, 1)

                def tile_context(t, k, first):
                    pe.wait_ge(s.probT_out, t + 1)
                    pe.wait_ge(s.v_out, t + 1)
                    if first:
                        pe.wait_ge(s.ctx_out, t)
                    for m in range(C):
                        last = nc.tensor.matmul(pC[:, m, :], V[:, k, m * P:(m + 1) * P], probT[:, k, :],
                                                start=True, stop=True)
                    last.then_inc(s.ctx_mm, 1)

                def tile_output(t, k, first):
                    pe.wait_ge(s.ctx_out, t + 1)
                    if first:
                        pe.wait_ge(s.z_sum, t)
                    for m in range(C):
                        last = nc.tensor.matmul(pO[:, :], ctxT[:, k, m, :], v.wo_s[:, 2 * C + m, :],
                                                start=(m == 0), stop=(m == C - 1))
                    last.then_inc(s.out_mm, 1)

                def step(t, k, first, before=True, after=True):
                    tile_scores(t, k, first)
                    if after:
                        project(t + 2, k, 2)
                    tile_transposes(t, k, first)
                    if before:
                        tile_output(t - 1, 1 - k, first if first == 2 else 0)
                    tile_context(t, k, first)
                project(0, 0, 0)
                project(1, 1, 1)
                step(0, 0, 0, before=False)
                step(1, 1, 1)
                with pe.Fori(1, T // 2 - 1) as i:
                    for k in range(2):
                        step(2 * i + k, k, 2)
                step(T - 2, 0, 2, after=False)
                step(T - 1, 1, 2, after=False)
                tile_output(T - 1, 1, 2)

            @block.scalar
            def _(act):
                def queries_keys(t, k, first):
                    act.wait_ge(s.qk_mm, t + 1)
                    if first >= 2:
                        act.wait_ge(s.scores, t - 1)
                    for w in range(2):
                        for m in range(C):
                            nc.scalar.activation(qkT[:, k, w, m, :], pQK[:, k, w, m, :], ACT.Identity,
                                                 bias=v.bqk[:, w, m:m + 1]).then_inc(s.qk_out, 1)

                def values(t, k, first):
                    act.wait_ge(s.v_mm, t + 1)
                    if first >= 2:
                        act.wait_ge(s.ctx_mm, t - 1)
                    nc.scalar.copy(V[:, k, :], pV[:, :]).then_inc(s.v_out, 1)

                def soft(t, k, first):
                    act.wait_ge(s.negmax, t + 1)
                    if first >= 2:
                        act.wait_ge(s.weighed, 2 * t - 2)
                    nc.scalar.activation(prob[:, k, :], pS[:, 0:WIN], ACT.Exp, scale=SCALE,
                                         bias=nmax[:, k, 1:2], accum_out=rs[:, k, 0:1]).then_inc(s.expd, 1)

                def context(t, k, first):
                    act.wait_ge(s.ctx_mm, t + 1)
                    if first >= 2:
                        act.wait_ge(s.out_mm, t - 1)
                    nc.scalar.copy(ctxT[:, k], pC[:, :, :]).then_inc(s.ctx_out, 1)

                def take(t, k, late=True):
                    off = WIN * t + (t // TB) * (L - WIN * TB)
                    if late:
                        act.wait_ge(s.qk_mm, t - 1)
                        wait_apart(act, s.v_mm, t - 1)
                    for w in range(2):
                        nc.scalar.copy(xs[:, k, :, w, :], xnT[:, :, bass.ds(off + w * HALF, WIN)]).then_inc(s.xs_in, 1)

                def turn(t, k, first, after=True, take_next=True):
                    soft(t, k, first)
                    if after:
                        queries_keys(t + 2, k, 2)
                    if after and take_next:
                        take(t + 3, 1 - k)
                    context(t, k, first)
                    if after:
                        values(t + 2, k, 2)
                take(0, 0, False)
                take(1, 1, False)
                queries_keys(0, 0, 0)
                values(0, 0, 0)
                take(2, 0)
                queries_keys(1, 1, 0)
                values(1, 1, 0)
                turn(0, 0, 0)
                turn(1, 1, 1)
                with act.Fori(1, T // 2 - 2) as i:
                    for k in range(2):
                        turn(2 * i + k, k, 2)
                turn(T - 4, 0, 2)
                turn(T - 3, 1, 2, take_next=False)
                turn(T - 2, 0, 2, after=False)
                turn(T - 1, 1, 2, after=False)

            @block.vector
            def _(dve):
                dve.wait_ge(s.zero4, 1)

                def soft(t, k, first):
                    dve.wait_ge(s.scores, t + 1)
                    nc.vector.reduce_max(nmax[:, k, 0:1], pS[:, 0:WIN], AX.X).then_inc(s.rowmax, 1)
                    dve.wait_ge(s.rowmax, t + 1)
                    nc.vector.tensor_scalar(nmax[:, k, 1:2], nmax[:, k, 0:1], -SCALE, None, ALU.mult).then_inc(s.negmax, 1)

                def weigh(t, k, first):
                    dve.wait_ge(s.expd, t + 1)
                    nc.vector.reciprocal(rs[:, k, 1:2], rs[:, k, 0:1]).then_inc(s.rowsum, 1)
                    dve.wait_ge(s.rowsum, t + 1)
                    for w in range(2):
                        r = slice(w * WIN, (w + 1) * WIN)
                        nc.vector.tensor_scalar(block_p[r, k, w * WIN:(w + 1) * WIN], prob[r, k, :], rs[r, k, 1:2],
                                                GS[r, t, 2:3], ALU.mult, ALU.mult).then_inc(s.weighed, 1)
                    dve.wait_ge(s.probT_mm, t + 1)
                    if first >= 2:
                        dve.wait_ge(s.ctx_mm, t - 1)
                    nc.vector.tensor_copy(probT[:, k, :], pPT[:, 0:P]).then_inc(s.probT_out, 1)

                def finish(t, k, first):
                    dve.wait_ge(s.out_mm, t + 1)
                    nc.vector.tensor_tensor(z[:, k, :], base[:, t, :], pO[:, :], ALU.add).then_inc(s.z_sum, 1)
                    dve.wait_ge(s.z_sum, t + 1)
                    nc.vector.bn_stats(stats[:, k, :], z[:, k, :]).then_inc(s.z_stats, 1)
                    wait_apart(dve, s.z_stats, t + 1)
                    nc.vector.bn_aggr(mv[:, k, :], stats[:, k, :]).then_inc(s.z_mv, 1)

                def norm(t, k, first):
                    dve.wait_ge(s.z_rstd, t + 1)
                    nc.vector.tensor_scalar(z[:, k, :], z[:, k, :], mv[:, k, 0:1], 0.5, ALU.subtract,
                                            ALU.mult).then_inc(s.z_norm, 1)
                    dve.wait_ge(s.z_norm, t + 1)
                    nc.vector.scalar_tensor_tensor(out=x1[:, t, :], in0=z[:, k, :], scalar=rstd[:, k, 1:2],
                                                   in1=x1[:, t, :], op0=ALU.mult, op1=ALU.add).then_inc(s.x1_out, 1)

                def turn(t, k, first):
                    soft(t, k, first)
                    weigh(t, k, first)
                    if first:
                        finish(t - 1, 1 - k, first)
                    if first >= 2:
                        norm(t - 2, k, first)
                pipelined(dve, turn)
                norm(T - 2, 0, 2)
                finish(T - 1, 1, 2)
                norm(T - 1, 1, 2)


def stages_layer2(nc, whole, sb, ps, sem, env):
    v = Names(env)
    with ExitStack() as late:
        ln2_b = sb("ln2_b", [P, H], F32, late)
        woT = sb("woT", [P, C, H], F32, late)
        gwT = sb("gwT", [P, C, E], F32, late)
        weights = sb("weights", [P, T, 2], F32, late)
        rows = sb("rows", [P, T, 2], I32, late)
        rowsf, shift, shifts = (sb(n, [P, T, 2], F32, late) for n in ("rowsf", "shift", "shifts"))
        pad_rows = sb("pad_rows", [P, E], I32, late)
        jrow_i = sb("jrow_i", [P, NTAB], I32, late)
        jrow, jc, ej, before, rowf = (sb(n, [P, NTAB], F32, late) for n in ("jrow", "jc", "ej", "before", "rowf"))
        cmp = sb("cmp", [P, E, NTAB], F32, late)
        steps = sb("steps", [P, T], F32, late)
        padf, ntile, ends = (sb(n, [P, E], F32, late) for n in ("padf", "ntile", "ends"))
        counts = sb("counts", [P, E], F32, late)
        lg = sb("lg", [P, T, E], F32, late)
        lastt = sb("lastt", [P, 1], F32, late)
        tile_expert, tile_in = (sb(n, [P, NTAB], I32, late) for n in ("tile_expert", "tile_in"))
        queue = nc.dram_tensor("queue", [E * CAP, H], F32).ap()
        results = nc.dram_tensor("results", [MAXT * P, H], F32).ap()
        with ExitStack() as att:
            QKV = sb("QKV", [P, T, QKVW], F32, att)
            stage5(nc, sb, ps, sem, locals(), v)
            stage6(nc, sb, ps, sem, locals(), v)
            v.free_semaphores()
            stage7(nc, sb, ps, sem, locals(), v)
            w13T = sb("w13T", [P, C, E * 2 * FFN], F32, att)
            w2T = sb("w2T", [P, FFN // P, E * H], F32, att)
            router(nc, sb, ps, sem, locals(), v)
            v.free_semaphores()
            stage8(nc, sb, ps, sem, locals(), v)
        stage9(nc, sb, ps, sem, locals(), v)


def stage5(nc, sb, ps, sem, env, base_env):
    v, u = Names(env), base_env
    x1, ident = u.x1, u.ident
    G = 4
    NGR = T // G
    QK = (NH + NKV) * HD
    with ExitStack() as ctx:
        ln1_b = sb("ln1_b", [P, H], F32, ctx)
        wqkvT = sb("wqkvT", [P, C, QKVW], F32, ctx)
        raw = sb("raw5", [P, 6, H], F32, ctx)
        cosb = sb("cosb", [P, TB, HD // 2], F32, ctx)
        sinb = sb("sinb", [P, TB, HD // 2], F32, ctx)
        stats = sb("stats5", [P, G, 6], F32, ctx)
        mv = sb("mv5", [P, G, 2], F32, ctx)
        rstd = sb("rstd5", [P, 4, G], F32, ctx)
        sq = sb("sq5", [P, G], F32, ctx)
        junk = sb("junk5", [P, G, H], F32, ctx)
        xl = sb("xl5", [P, G, H], F32, ctx)
        h = sb("h5", [P, G, H], F32, ctx)
        hT = sb("hT5", [P, G, C, P], F32, ctx)
        qk = sb("qk5", [P, 2, G, QK], F32, ctx)
        byc = sb("byc5", [P, 2, 2, QK], F32, ctx)
        bys = sb("bys5", [P, 2, 2, QK], F32, ctx)
        pT = ps("pT5", [P, G, C, P], F32, ctx)
        pQ = ps("pQ5", [P, G, 512], F32, ctx)
        names = ("raw_in", "small_in", "wT_mm", "wT_out", "stats", "mv", "eps1", "rstd1", "xl", "square", "eps2", "eps3",
                 "rstd2", "h", "hT_mm", "hT_out", "qkv_mm", "qk_out", "v_out")
        s = Names({n: sem("q_" + n) for n in names})
        turned, by_cos, by_sin = ([sem(f"q_{n}{k}") for k in range(2)] for n in ("turned", "by_cos", "by_sin"))

        def groups(eng, step):
            step(0, 0, first=True)
            step(1, 1)
            with eng.Fori(1, NGR // 2 - 1) as i:
                for k in range(2):
                    step(2 * i + k, k)
            step(NGR - 2, 0)
            step(NGR - 1, 1, last=True)

        def rotate(eng, ns, side, i, k):
            two = slice(2 * side, 2 * side + 2)
            pos = G * (i % (TB // G)) + 2 * side
            eng.wait_ge(s.qk_out, 2 * i + side + 3)
            eng.wait_ge(turned[side], 2 * i + 4)
            src = qk[:, k, two, :].rearrange("p t (n d) -> p t n d", d=8)
            for done, dst, table in ((by_cos, byc, cosb), (by_sin, bys, sinb)):
                for j in range(2):
                    ns.tensor_tensor(dst[:, side, j, :].rearrange("p (n d) -> p n d", d=8), src[:, j],
                                     table[:, pos + j, :].unsqueeze(1).to_broadcast([P, QK // 8, 8]),
                                     ALU.mult).then_inc(done[side], 1)
            eng.wait_ge(by_cos[side], 2 * i + 2)
            eng.wait_ge(by_sin[side], 2 * i + 2)
            for j in range(2):
                o = v.QKV[:, G * i + 2 * side + j, 0:QK].rearrange("p (n a d) -> p n a d", a=2, d=8)
                yc, ys = (y[:, side, j, :].rearrange("p (n a d) -> p n a d", a=2, d=8) for y in (byc, bys))
                ns.tensor_tensor(o[:, :, 0, :], yc[:, :, 0, :], ys[:, :, 1, :], ALU.subtract)
                ns.tensor_tensor(o[:, :, 1, :], yc[:, :, 1, :], ys[:, :, 0, :], ALU.add).then_inc(turned[side], 1)

        with nc.Block() as block:
            @block.sync
            def _(sp):
                sp.dma_start(raw[:, 0:3, :], u.wqkv.rearrange("(t p) h -> p t h", p=P)).then_inc(s.raw_in, 16)
                sp.dma_start(raw[:, 3:5, :], u.wo.rearrange("(t p) h -> p t h", p=P)).then_inc(s.raw_in, 16)
                sp.dma_start(raw[0:E, 5, :], u.gate_w).then_inc(s.raw_in, 16)
                sp.dma_start(ln1_b[:, :], u.ln1_w.partition_broadcast(P)).then_inc(s.small_in, 16)
                sp.dma_start(v.ln2_b[:, :], u.ln2_w.partition_broadcast(P)).then_inc(s.small_in, 16)
                sp.dma_start(cosb[:, :, :], u.cos_t.rearrange("(t p) n -> p t n", p=P)).then_inc(s.small_in, 16)
                sp.dma_start(sinb[:, :, :], u.sin_t.rearrange("(t p) n -> p t n", p=P)).then_inc(s.small_in, 16)

            @block.tensor
            def _(pe):
                pe.wait_ge(s.raw_in, 48)
                for n in range(6):
                    rows = E if n == 5 else P
                    for c in range(C):
                        k = 2 * n + c
                        if k >= 2:
                            pe.wait_ge(s.wT_out, k - 1)
                        nc.tensor.transpose(pT[:, 2 * (k % 2), 0, 0:rows], raw[0:rows, n, c * P:(c + 1) * P],
                                            ident[0:rows, 0:rows]).then_inc(s.wT_mm, 1)
                pe.wait_ge(s.wT_out, 12)
                pe.sem_inc(s.hT_mm, 1)
                pe.sem_inc(s.qkv_mm, 2)

                def step(i, k, first=False, last=False):
                    pe.wait_ge(s.h, G * i + G)
                    for g in range(G):
                        for c in range(C):
                            done = nc.tensor.transpose(pT[:, g, c, :], h[:, g, c * P:(c + 1) * P], ident[:, :])
                    done.then_inc(s.hT_mm, 1)
                    pe.wait_ge(s.hT_out, i + 1)
                    for g in range(2):
                        pe.wait_ge(s.v_out, 2 * i + g + 1)
                        pe.wait_ge(s.qk_out, 2 * i + g + 1)
                        for j in range(2 * g, 2 * g + 2):
                            for c in range(C):
                                done = nc.tensor.matmul(pQ[:, j, 0:QKVW], hT[:, j, c, :], wqkvT[:, c, :],
                                                        start=(c == 0), stop=(c == C - 1))
                        done.then_inc(s.qkv_mm, 1)
                groups(pe, step)

            @block.scalar
            def _(act):
                act.sem_inc(s.v_out, 2)
                act.sem_inc(s.qk_out, 2)

                def step(i, k, first=False, last=False):
                    act.wait_ge(s.hT_mm, i + 2)
                    act.wait_ge(s.qkv_mm, 2 * i + 2)
                    nc.scalar.copy(hT[:, :, :, :], pT[:, :, :, :]).then_inc(s.hT_out, 1)
                    for g in range(2):
                        act.wait_ge(s.qkv_mm, 2 * i + g + 3)
                        act.wait_ge(turned[g], 2 * i + 2)
                        nc.scalar.copy(qk[:, k, 2 * g:2 * g + 2, :], pQ[:, 2 * g:2 * g + 2, 0:QK]).then_inc(s.qk_out, 1)
                        nc.scalar.copy(v.QKV[:, bass.ds(G * i + 2 * g, 2), QK:QKVW],
                                       pQ[:, 2 * g:2 * g + 2, QK:QKVW]).then_inc(s.v_out, 1)
                groups(act, step)

            @block.gpsimd
            def _(pool):
                pool.sem_inc(turned[0], 4)

                def root1(i):
                    wait_apart(pool, s.mv, G * i + G)
                    nc.gpsimd.tensor_scalar(rstd[:, 0, :], mv[:, :, 1], 1e-5, None, ALU.add).then_inc(s.eps1, 1)
                    pool.wait_ge(s.eps1, i + 1)
                    nc.gpsimd.tensor_tensor(rstd[:, 1, :], rstd[:, 0, :], u.halfpow[:, :].to_broadcast([P, G]),
                                            ALU.pow).then_inc(s.rstd1, 1)

                def step(i, k, first=False, last=False):
                    wait_apart(pool, s.square, G * i + G)
                    nc.gpsimd.tensor_scalar(rstd[:, 2, :], sq[:, :], 1.0 / H, 1e-5, ALU.mult, ALU.add).then_inc(s.eps2, 1)
                    pool.wait_ge(s.eps2, i + 1)
                    nc.gpsimd.tensor_tensor(rstd[:, 3, :], rstd[:, 2, :], u.halfpow[:, :].to_broadcast([P, G]),
                                            ALU.pow).then_inc(s.rstd2, 1)
                    if not last:
                        root1(i + 1)
                    if not first:
                        rotate(pool, nc.gpsimd, 0, i - 1, 1 - k)
                root1(0)
                groups(pool, step)
                rotate(pool, nc.gpsimd, 0, NGR - 1, 1)

            @block.vector
            def _(dve):
                k = 0
                for n in range(6):
                    for c in range(C):
                        dve.wait_ge(s.wT_mm, k + 1)
                        rows = E if n == 5 else P
                        dst = (wqkvT[:, c, n * P:(n + 1) * P] if n < 3 else v.woT[:, c, (n - 3) * P:(n - 2) * P]
                               if n < 5 else v.gwT[:, c, :])
                        nc.vector.tensor_copy(dst, pT[:, 2 * (k % 2), 0, 0:rows]).then_inc(s.wT_out, 1)
                        k += 1
                dve.wait_ge(s.small_in, 64)
                dve.sem_inc(turned[1], 4)

                def moments(i, first=False):
                    if not first:
                        dve.wait_ge(s.xl, G * i)
                    for g in range(G):
                        nc.vector.bn_stats(stats[:, g, :], x1[:, G * i + g, :]).then_inc(s.stats, 1)
                    for g in range(G):
                        wait_apart(dve, s.stats, G * i + g + 1)
                        nc.vector.bn_aggr(mv[:, g, :], stats[:, g, :]).then_inc(s.mv, 1)

                def step(i, k, first=False, last=False):
                    dve.wait_ge(s.rstd1, i + 1)
                    if not first:
                        dve.wait_ge(s.h, G * i)
                    for g in range(G):
                        nc.vector.tensor_scalar(xl[:, g, :], x1[:, G * i + g, :], mv[:, g, 0:1], rstd[:, 1, g:g + 1],
                                                ALU.subtract, ALU.mult).then_inc(s.xl, 1)
                    for g in range(G):
                        dve.wait_ge(s.xl, G * i + g + 1)
                        nc.vector.tensor_tensor_reduce(junk[:, g, :], xl[:, g, :], xl[:, g, :], 1.0, 0.0, ALU.mult, ALU.add,
                                                       sq[:, g:g + 1]).then_inc(s.square, 1)
                    if not last:
                        moments(i + 1)
                    dve.wait_ge(s.rstd2, i + 1)
                    dve.wait_ge(s.hT_mm, i + 1)
                    for g in range(G):
                        nc.vector.scalar_tensor_tensor(out=h[:, g, :], in0=xl[:, g, :], scalar=rstd[:, 3, g:g + 1],
                                                       in1=ln1_b[:, :], op0=ALU.mult, op1=ALU.mult).then_inc(s.h, 1)
                    if not first:
                        rotate(dve, nc.vector, 1, i - 1, 1 - k)
                moments(0, first=True)
                groups(dve, step)
                rotate(dve, nc.vector, 1, NGR - 1, 1)


PARTS_Q = (0, 0, 1, 1, 0, 2)
PARTS_K = (0, 1, 0, 1, 2, 0)
NPART = len(PARTS_Q)
ROWS = NPART * HD
CH = L // 512


def key_order(c):
    if c == 0:
        return list(range(4))
    return [kt for n in range(4) for kt in list(range(n * c, n * c + c)) + [4 * c + n]]


KSTEPS = [(c, kt) for c in range(CH) for kt in key_order(c)]
UNITS = [(h, qt, part) for h in range(GRP) for qt in range(TB) for part in range(qt // 4 + 1)]


def background():
    items = []
    for h in range(GRP):
        units = [("U", n) for n, unit in enumerate(UNITS) if unit[0] == h]
        first = sum(1 for unit in UNITS if unit[0] == 0 and unit[1] < TB // 2)
        if h == 0:
            items += [("K", 0), ("Q", 0, 0)] + units[:first] + [("K", 1), ("Q", 0, 1)]
            units = units[first:]
            turns = [("Q", 1, 0), ("Q", 1, 1)]
        else:
            turns = [("Q", k, f) for k in range(2, GRP) for f in range(2)] if h == 1 else []
        every = len(units) // (len(turns) + 1)
        for n, unit in enumerate(units):
            if turns and n and n % every == 0:
                items.append(turns.pop(0))
            items.append(unit)
        items += turns
    return items + [("M", 0), ("M", 1)]


def interleave():
    items = background()
    width = [min(512, P * (UNITS[x[1]][1] + 1) - 512 * UNITS[x[1]][2]) + 64 if x[0] == "U" else 600 for x in items]
    step = [512 - max(0, kt - 4 * c) * P + 64 for c, kt in KSTEPS]
    out, at = [], 0
    for n in range(len(KSTEPS)):
        share = min(1.0, sum(step[:n + 1]) / (0.98 * sum(step)))
        upto = at
        while upto < len(items) and sum(width[:upto + 1]) <= share * sum(width) + 1e-6:
            upto += 1
        out.append(items[at:upto])
        at = upto
    assert at == len(items)
    return out


class Uses:

    def __init__(self, passes):
        kq = 2 + 2 * GRP
        if isinstance(passes, int) and passes == 0:
            self.t, self.a, self.d = 0, 1, 1
        else:
            self.t, self.a, self.d = (kq + 2) + (kq + 2 + CH) * (passes - 1), 1 + kq * passes, 3 + (2 + CH) * (passes - 1)

    def use(self, by):
        self.t += 1
        if by == "a":
            self.a += 1
        else:
            self.d += 1


class Ring:
    BANKS = 3

    def __init__(self):
        self.at, self.last = -1, [None] * self.BANKS

    def take(self, item):
        self.at = (self.at + 1) % self.BANKS
        before, self.last[self.at] = self.last[self.at], item
        return self.at, before


def stage6(nc, sb, ps, sem, env, base_env):
    v, u = Names(env), base_env
    QKV, ident = v.QKV, u.ident
    NG = B * NKV
    NU, NS_ = len(UNITS), len(KSTEPS)
    BESIDE = interleave()
    EARLY = 2
    HEAD_UNITS = sum(1 for unit in UNITS if unit[0] == 0)
    with ExitStack() as ctx:
        identb = sb("identb", [P, P], BF16, ctx)
        maskf = sb("maskf", [P, P], F32, ctx)
        mask_qk = sb("mask_qk", [P, P], BF16, ctx)
        mask_kq = sb("mask_kq", [P, P], BF16, ctx)
        Qt = sb("Qt", [P, TB, GRP, ROWS], BF16, ctx)
        Kt = sb("Kt", [P, TB, ROWS], BF16, ctx)
        rem = sb("rem", [P, 2, TB, GRP * HD], F32, ctx)
        KT = sb("KT", [P, 2, L], BF16, ctx)
        QT = sb("QT", [P, 2, GRP, L], BF16, ctx)
        VV = sb("VV", [P, 2, TB, 32], F32, ctx)
        prob = sb("prob6", [P, 3, 2, 2, 512], F32, ctx)
        mx = sb("mx", [P, GRP, TB, CH], F32, ctx)
        mrem = sb("mrem", [P, 3, TB, GRP], F32, ctx)
        mpart = sb("mpart", [P, TB, GRP, 3], BF16, ctx)
        mrow = sb("mrow", [GRP * 3, L], BF16, ctx)
        oS = sb("oS", [P, 512], F32, ctx)
        den = sb("den", [P, 4, GRP], F32, ctx)
        pS = ps("pS6", [P, 2, 2, 512], F32, ctx)
        pO = ps("pO6", [P, 512], F32, ctx)
        pM = ps("pM6", [P, Ring.BANKS, 512], F32, ctx)
        pMb = [pM[:, k, :].bitcast(BF16) for k in range(Ring.BANKS)]
        names = ("zero", "masks", "masks_b", "kparts", "vparts", "T_mm", "T_out", "TA_out", "unit_mm", "unit_max",
                 "mparts", "mrow_in", "pair_mm", "pair_exp", "pv", "o_out", "den_out", "o_put", "vv_init", "ones_in",
                 "qchain", "mchain", "first_chain", "first_copied")
        s = Names({n: sem("c_" + n) for n in names})

        def group(gi):
            b, g = gi // NKV, gi % NKV
            return b * TB, g

        def split(ns, ch, copied, src, parts, slots, rests):
            for part in range(3):
                at = [n for n in range(NPART) if slots[n] == part]
                now = src if part == 0 else rests[part - 1]
                ch.link(ns.tensor_copy(parts(at[0]), now), apart=True)
                for n in at[1:]:
                    ns.tensor_copy(parts(n), parts(at[0])).then_inc(copied, 1)
                if part < 2:
                    ch.link(ns.tensor_tensor(rests[part], now, parts(at[0]), ALU.subtract), apart=True)

        def split_queries(ns, ch, copied, t0, g, room):
            q = QKV[:, bass.ds(t0, TB), bass.ds(g * GRP * HD, GRP * HD)].rearrange("p t (h d) -> p t h d", d=HD)
            split(ns, ch, copied, q, lambda n: Qt[:, :, :, n * HD:(n + 1) * HD], PARTS_Q,
                  [r.rearrange("p t (h d) -> p t h d", d=HD) for r in room])

        with nc.Block() as block:
            @block.sync
            def _(sp):
                def send(gi, par, maxima_out):
                    sp.wait_ge(s.T_out, maxima_out)
                    for h in range(GRP):
                        sp.dma_start(QT[ROWS:ROWS + 3, par, h, :], mrow[3 * h:3 * h + 3, :]).then_inc(s.mrow_in, 16)
                sp.wait_ge(s.ones_in, 1)
                send(0, 0, 1 + 2)
                send(1, 1, 1 + 2 + (2 + CH - 1))
                with sp.Fori(1, NG // 2) as i:
                    for k in range(2):
                        gi = 2 * i + k
                        send(gi, k, (2 + CH) * gi + 2)
                sp.wait_ge(s.mrow_in, 64 * NG)

            @block.gpsimd
            def _(pool):
                nc.gpsimd.memset(maskf[:, :], 0.0).then_inc(s.zero, 1)
                nc.gpsimd.memset(VV[:, :, :, :], 0.0).then_inc(s.zero, 1)
                nc.gpsimd.tensor_copy(identb[:, :], ident[:, :]).then_inc(s.masks_b, 1)
                pool.wait_ge(s.zero, 2)
                nc.gpsimd.affine_select(out=maskf[:, :], in_=maskf[:, :], compare_op=ALU.is_ge, fill=NEG, base=0,
                                        pattern=[[-1, P]], channel_multiplier=1).then_inc(s.masks, 1)
                nc.gpsimd.memset(VV[:, :, :, HD:HD + 1], 1.0).then_inc(s.vv_init, 1)
                pool.wait_ge(s.masks, 1)
                nc.gpsimd.tensor_copy(mask_qk[:, :], maskf[:, :]).then_inc(s.masks_b, 1)
                pool.wait_ge(s.masks_b, 2)
                nc.gpsimd.memset(maskf[:, :], 0.0).then_inc(s.zero, 1)
                pool.wait_ge(s.zero, 3)
                nc.gpsimd.affine_select(out=maskf[:, :], in_=maskf[:, :], compare_op=ALU.is_ge, fill=NEG, base=0,
                                        pattern=[[1, P]], channel_multiplier=-1).then_inc(s.masks, 1)
                pool.wait_ge(s.masks, 2)
                nc.gpsimd.tensor_copy(mask_kq[:, :], maskf[:, :]).then_inc(s.masks_b, 1)
                pool.wait_ge(s.vv_init, 1)
                ch = Chain(pool, s.qchain)

                def prepare(gi, par, later=False):
                    t0, g = group(gi)
                    tiles = bass.ds(t0, TB)
                    ch.at(10 * gi)
                    k = QKV[:, tiles, bass.ds(NH * HD + g * HD, HD)]
                    split(nc.gpsimd, ch, s.kparts, k, lambda n: Kt[:, :, n * HD:(n + 1) * HD], PARTS_K,
                          [rem[:, r, :, 0:HD] for r in range(2)])
                    if not (isinstance(gi, int) and gi == 0):
                        split_queries(nc.gpsimd, ch, s.kparts, t0, g, [rem[:, r] for r in range(2)])
                        assert ch.k == 10
                    if later:
                        wait_apart(pool, s.pv, NS_ * (gi - 1) + 2)
                    nc.gpsimd.tensor_copy(VV[:, par, :, 0:HD],
                                          QKV[:, tiles, bass.ds((NH + NKV) * HD + g * HD, HD)]).then_inc(s.vparts, 1)
                prepare(0, 0)
                pool.wait_ge(s.unit_mm, 2 * HEAD_UNITS + 1)
                prepare(1, 1)
                with pool.Fori(1, NG // 2) as i:
                    for k in range(2):
                        gi = 2 * i + k
                        pool.wait_ge(s.unit_mm, NU * (gi - 1) + 2 * HEAD_UNITS + 1)
                        prepare(gi, k, later=True)

            @block.tensor
            def _(pe):
                pe.wait_ge(s.masks_b, 3)
                pe.wait_ge(s.ones_in, 1)
                pe.sem_inc(s.pv, 2)

                def take(ring, item):
                    bank, before = ring.take(item)
                    if before is not None:
                        pe.wait_ge(*before)
                    return bank

                def beside(item, gi, par, cnt, ring):
                    kind = item[0]
                    if kind in "KQM":
                        cnt.use("a" if kind in "KQ" else "d")
                        bank = take(ring, (s.TA_out, cnt.a) if kind in "KQ" else (s.T_out, cnt.d))
                        f = item[-1]
                        if kind == "M":
                            pe.wait_ge(s.mparts, gi + 1)
                        else:
                            pe.wait_ge(s.qchain, 10 * gi + (5 if kind == "K" else 10))
                            pe.wait_ge(s.kparts, 6 * gi + (3 if kind == "K" else 6))
                        for k in range(8):
                            t = 8 * f + k
                            if kind == "K":
                                src, rows = Kt[:, t, :], ROWS
                            elif kind == "Q":
                                src, rows = Qt[:, t, item[1], :], ROWS
                            else:
                                src, rows = mpart[:, t, :, :].rearrange("p h a -> p (h a)"), 3 * GRP
                            last = nc.tensor.transpose(pMb[bank][0:rows, k * P:(k + 1) * P], src, identb[:, :])
                        last.then_inc(s.T_mm, 1)
                        return
                    n = item[1]
                    h, qt, part = UNITS[n]
                    bank = take(ring, (s.unit_max, NU * gi + n + 1))
                    if qt == 0 or (h == 0 and qt == TB // 2):
                        pe.wait_ge(s.TA_out, cnt.a)
                    w = min(512, (qt + 1) * P - 512 * part)
                    last = nc.tensor.matmul(pM[:, bank, 0:w], QT[0:ROWS, par, h, qt * P:(qt + 1) * P],
                                            KT[0:ROWS, par, 512 * part:512 * part + w], start=True, stop=part < qt // 4)
                    if part == qt // 4:
                        last = nc.tensor.matmul(pM[:, bank, w - P:w], identb[:, :], mask_qk[:, :], start=False, stop=True)
                    last.then_inc(s.unit_mm, 1)

                def pair(gi, par, n, pr, between):
                    c, kt = KSTEPS[n]
                    lo = max(0, kt - 4 * c) * P
                    idx = 2 * (NS_ * gi + n) + pr
                    pe.wait_ge(s.pair_exp, idx + 1)
                    for hh in range(2):
                        h = 2 * pr + hh
                        diag = kt >= 4 * c
                        last = nc.tensor.matmul(pS[:, pr, hh, lo:512], KT[0:ROWS + 3, par, kt * P:(kt + 1) * P],
                                                QT[0:ROWS + 3, par, h, 512 * c + lo:512 * c + 512], start=True,
                                                stop=not diag)
                        if diag:
                            last = nc.tensor.matmul(pS[:, pr, hh, lo:lo + P], identb[:, :], mask_kq[:, :], start=False,
                                                    stop=True)
                        if hh == 0:
                            between()
                    last.then_inc(s.pair_mm, 1)

                def values(gi, par, n):
                    c, kt = KSTEPS[n]
                    lo = max(0, kt - 4 * c) * P
                    pe.wait_ge(s.pair_exp, 2 * (NS_ * gi + n) + 4)
                    if kt == 0:
                        pe.wait_ge(s.o_out, CH * gi + c + 1)
                    if n == 0:
                        pe.wait_ge(s.vparts, gi + 1)
                    for h in range(GRP):
                        last = nc.tensor.matmul(pO[32 * h:32 * h + 32, lo:512], VV[:, par, kt, :],
                                                prob[:, n % 3, h // 2, h % 2, lo:512], start=(kt == 0),
                                                stop=(kt == 4 * c + 3), tile_position=(0, 32 * h))
                    last.then_inc(s.pv, 1)

                def chunk_out(gi, c, cnt, ring):
                    pe.wait_ge(s.o_out, CH * gi + c + 2)
                    cnt.use("d")
                    bank = take(ring, (s.T_out, cnt.d))
                    for k in range(4):
                        last = nc.tensor.transpose(pM[:, bank, k * P:(k + 1) * P], oS[:, k * P:(k + 1) * P], ident[:, :])
                    last.then_inc(s.T_mm, 1)

                def one(gi, par, more):
                    cnt, ring = Uses(gi + 1), Ring()
                    pe.wait_ge(s.T_out, cnt.d)
                    for x in BESIDE[0][:EARLY] if more else []:
                        beside(x, gi + 1, 1 - par, cnt, ring)
                    pe.wait_ge(s.mrow_in, 64 * gi + 64)
                    pair(gi, par, 0, 0, lambda: None)
                    pair(gi, par, 0, 1, lambda: None)
                    for n in range(NS_):
                        extra = BESIDE[n][0 if n else EARLY:] if more else []

                        def some(place):
                            for x in extra[place * len(extra) // 5:(place + 1) * len(extra) // 5]:
                                beside(x, gi + 1, 1 - par, cnt, ring)
                        some(0)
                        if n + 1 < NS_:
                            pair(gi, par, n + 1, 0, lambda: some(1))
                        else:
                            some(1)
                        some(2)
                        if n:
                            values(gi, par, n - 1)
                        some(3)
                        if n + 1 < NS_:
                            pair(gi, par, n + 1, 1, lambda: some(4))
                        else:
                            some(4)
                        if n > 1 and KSTEPS[n - 1][1] == 0:
                            chunk_out(gi, KSTEPS[n][0] - 1, cnt, ring)
                    values(gi, par, NS_ - 1)
                    chunk_out(gi, CH - 1, cnt, ring)
                cnt, ring = Uses(0), Ring()
                for item in background():
                    beside(item, 0, 0, cnt, ring)
                with pe.Fori(0, NG // 2 - 1) as i:
                    for k in range(2):
                        one(2 * i + k, k, True)
                one(NG - 2, 0, True)
                one(NG - 1, 1, False)

            @block.scalar
            def _(act):
                act.sem_inc(s.pair_exp, 2)
                act.sem_inc(s.TA_out, 1)
                act.wait_ge(s.vv_init, 1)

                def beside(item, par, cnt, ring):
                    bank, _before = ring.take(item)
                    if item[0] == "U":
                        return
                    cnt.use("a" if item[0] in "KQ" else "d")
                    if item[0] == "M":
                        return
                    act.wait_ge(s.T_mm, cnt.t)
                    cols = slice(item[-1] * 1024, item[-1] * 1024 + 1024)
                    dst = KT[0:ROWS, par, cols] if item[0] == "K" else QT[0:ROWS, par, item[1], cols]
                    nc.scalar.copy(dst, pMb[bank][0:ROWS, :]).then_inc(s.TA_out, 1)

                def one(gi, par, more):
                    cnt, ring = Uses(gi + 1), Ring()
                    for x in BESIDE[0][:EARLY] if more else []:
                        beside(x, 1 - par, cnt, ring)
                    for n in range(NS_):
                        c, kt = KSTEPS[n]
                        lo = max(0, kt - 4 * c) * P
                        act.wait_ge(s.pv, NS_ * gi + 2 + max(0, n - 2))
                        for pr in range(2):
                            act.wait_ge(s.pair_mm, 2 * (NS_ * gi + n) + pr + 1)
                            nc.scalar.activation(prob[:, n % 3, pr, :, lo:512], pS[:, pr, :, lo:512], ACT.Exp,
                                                 scale=SCALE).then_inc(s.pair_exp, 1)
                        for x in BESIDE[n][0 if n else EARLY:] if more else []:
                            beside(x, 1 - par, cnt, ring)
                        if n > 1 and KSTEPS[n - 1][1] == 0:
                            cnt.use("d")
                            ring.take("context")
                cnt, ring = Uses(0), Ring()
                for item in background():
                    beside(item, 0, cnt, ring)
                with act.Fori(0, NG // 2 - 1) as i:
                    for k in range(2):
                        one(2 * i + k, k, True)
                one(NG - 2, 0, True)
                one(NG - 1, 1, False)

            @block.vector
            def _(dve):
                dve.sem_inc(s.T_out, 1)
                dve.sem_inc(s.o_out, 1)
                nc.vector.memset(KT[ROWS:ROWS + 3, :, :], 1.0).then_inc(s.ones_in, 1)
                ch = Chain(dve, s.mchain)
                first = Chain(dve, s.first_chain)
                spare = prob[:, 0:2, :, :, :].rearrange("p r a b n -> p r (a b n)")
                split_queries(nc.vector, first, s.first_copied, 0, 0,
                              [spare[:, r, 0:TB * GRP * HD].rearrange("p (t n) -> p t n", t=TB) for r in range(2)])
                dve.wait_ge(s.first_copied, 3)
                dve.wait_ge(s.qchain, 5)
                dve.wait_ge(s.kparts, 3)
                dve.sem_inc(s.qchain, 5)
                dve.sem_inc(s.kparts, 3)
                ch.link(nc.vector.memset(mx[:, :, :, :], -3e38))

                def beside(item, gi, par, cnt, ring):
                    kind = item[0]
                    bank, _before = ring.take(item)
                    if kind in "KQM":
                        f = item[-1]
                        if kind == "M" and f == 0:
                            dve.wait_ge(s.unit_max, NU * gi + NU)
                            ch.at(6 * gi + 1)
                            ch.link(nc.vector.reduce_max(mrem[:, 1].rearrange("p t h -> p h t"), mx[:, :, :, :], AX.X))
                            ch.link(nc.vector.tensor_scalar(mrem[:, 0], mrem[:, 1], -1.0, None, ALU.mult))
                            ch.link(nc.vector.tensor_copy(mpart[:, :, :, 0], mrem[:, 0]))
                            ch.link(nc.vector.tensor_tensor(mrem[:, 1], mrem[:, 0], mpart[:, :, :, 0], ALU.subtract))
                            ch.link(nc.vector.tensor_copy(mpart[:, :, :, 1], mrem[:, 1]))
                            ch.link(nc.vector.tensor_tensor(mrem[:, 2], mrem[:, 1], mpart[:, :, :, 1], ALU.subtract))
                            nc.vector.tensor_copy(mpart[:, :, :, 2], mrem[:, 2]).then_inc(s.mparts, 1)
                        cnt.use("a" if kind in "KQ" else "d")
                        if kind in "KQ":
                            return
                        dve.wait_ge(s.T_mm, cnt.t)
                        if f == 0 and not (isinstance(gi, int) and gi == 0):
                            dve.wait_ge(s.mrow_in, 64 * gi)
                        nc.vector.tensor_copy(mrow[:, f * 1024:f * 1024 + 1024], pMb[bank][0:3 * GRP, :]).then_inc(s.T_out, 1)
                        return
                    n = item[1]
                    h, qt, part = UNITS[n]
                    dve.wait_ge(s.unit_mm, NU * gi + n + 1)
                    w = min(512, (qt + 1) * P - 512 * part)
                    nc.vector.reduce_max(mx[:, h, qt, part:part + 1], pM[:, bank, 0:w], AX.X).then_inc(s.unit_max, 1)

                def chunk(gi, c, cnt, after):
                    dve.wait_ge(s.pv, NS_ * gi + after + 2)
                    nc.vector.tensor_copy(oS[:, :], pO[:, :]).then_inc(s.o_out, 1)

                def chunk_put(gi, c, cnt, ring):
                    t0, g = group(gi)
                    cnt.use("d")
                    bank, _before = ring.take("context")
                    dve.wait_ge(s.T_mm, cnt.t)
                    o = pM[:, bank, :].rearrange("p (k h d) -> p k h d", k=4, h=GRP)
                    nc.vector.reciprocal(den[:, :, :], o[:, :, :, HD]).then_inc(s.den_out, 1)
                    dve.wait_ge(s.den_out, CH * gi + c + 1)
                    nc.vector.tensor_tensor(
                        QKV[:, bass.ds(t0 + 4 * c, 4), bass.ds(g * GRP * HD, GRP * HD)].rearrange("p k (h d) -> p k h d", d=HD),
                        o[:, :, :, 0:HD], den[:, :, :].unsqueeze(3).to_broadcast([P, 4, GRP, HD]),
                        ALU.mult).then_inc(s.T_out, 1)

                def one(gi, par, more):
                    cnt, ring = Uses(gi + 1), Ring()
                    for n in range(NS_):
                        for x in BESIDE[n] if more else []:
                            beside(x, gi + 1, 1 - par, cnt, ring)
                        if n > 1 and KSTEPS[n - 1][1] == 0:
                            chunk_put(gi, KSTEPS[n][0] - 1, cnt, ring)
                        if n and KSTEPS[n][1] == 0:
                            chunk(gi, KSTEPS[n - 1][0], cnt, n)
                    chunk(gi, CH - 1, cnt, NS_)
                    chunk_put(gi, CH - 1, cnt, ring)
                cnt, ring = Uses(0), Ring()
                for item in background():
                    beside(item, 0, 0, cnt, ring)
                with dve.Fori(0, NG // 2 - 1) as i:
                    for k in range(2):
                        one(2 * i + k, k, True)
                one(NG - 2, 0, True)
                one(NG - 1, 1, False)


CAP = B * L + P
MAXT = 2 * B * L // P + E
NTAB = MAXT + 2


BOTH = 9


def stage7(nc, sb, ps, sem, env, base_env):
    v, u = Names(env), base_env
    x1, ident, QKV = u.x1, u.ident, v.QKV
    G = 4
    NGR = T // G
    with ExitStack() as ctx:
        stats = sb("stats7", [P, G, 6], F32, ctx)
        mv = sb("mv7", [P, G, 2], F32, ctx)
        rstd = sb("rstd7", [P, 4, G], F32, ctx)
        sq = sb("sq7", [P, G], F32, ctx)
        junk = sb("junk7", [P, G, H], F32, ctx)
        xl = sb("xl7", [P, G, H], F32, ctx)
        x2 = sb("x27", [P, 2, G, H], F32, ctx)
        at = sb("at7", [P, 2, G, H], F32, ctx)
        aT = sb("aT7", [P, 2, G, C, P], F32, ctx)
        hs = sb("hs7", [P, G, H], F32, ctx)
        hT = sb("hT7", [P, G, C, P], F32, ctx)
        pA = ps("pA7", [P, G, C, P], F32, ctx)
        pX = ps("pX7", [P, G, H], F32, ctx)
        pH = ps("pH7", [P, G, C, P], F32, ctx)
        pL = ps("pL7", [P, G, E], F32, ctx)
        names = ("stats", "mv", "eps1", "rstd1", "xl", "x2", "square", "eps2", "rstd2", "h", "resid", "at_in", "aT_mm",
                 "aT_out", "proj", "hs_in", "hT_mm", "hT_out", "logits", "lg_out")
        s = Names({n: sem("r_" + n) for n in names})

        def groups(eng, step):
            step(0, 0, False, 2)
            step(1, 1, True, 2)
            with eng.Fori(1, NGR // 2 - 1) as i:
                for k in range(2):
                    step(2 * i + k, k, True, 2)
            step(NGR - 2, 0, True, 1)
            step(NGR - 1, 1, True, 0)

        with nc.Block() as block:
            @block.gpsimd
            def _(pool):
                def root1(i):
                    wait_apart(pool, s.mv, G * i + G)
                    nc.gpsimd.tensor_scalar(rstd[:, 0, :], mv[:, :, 1], 1e-5, None, ALU.add).then_inc(s.eps1, 1)
                    pool.wait_ge(s.eps1, i + 1)
                    nc.gpsimd.tensor_tensor(rstd[:, 1, :], rstd[:, 0, :], u.halfpow[:, :].to_broadcast([P, G]),
                                            ALU.pow).then_inc(s.rstd1, 1)

                pool.sem_inc(s.resid, 2)

                def step(i, k, before, behind):
                    wait_apart(pool, s.square, G * i + G)
                    nc.gpsimd.tensor_scalar(rstd[:, 2, :], sq[:, :], 1.0 / H, 1e-5, ALU.mult, ALU.add).then_inc(s.eps2, 1)
                    pool.wait_ge(s.eps2, i + 1)
                    nc.gpsimd.tensor_tensor(rstd[:, 3, :], rstd[:, 2, :], u.halfpow[:, :].to_broadcast([P, G]),
                                            ALU.pow).then_inc(s.rstd2, 1)
                    if behind:
                        root1(i + 1)
                    nc.gpsimd.tensor_tensor(x1[:, bass.ds(G * i, G), :], x1[:, bass.ds(G * i, G), :], x2[:, k],
                                            ALU.add).then_inc(s.resid, 1)
                root1(0)
                groups(pool, step)

            @block.tensor
            def _(pe):
                pe.sem_inc(s.aT_mm, 1)
                pe.sem_inc(s.proj, 1)
                pe.sem_inc(s.hT_mm, 1)
                pe.sem_inc(s.logits, 1)

                def turn_attended(i, k):
                    pe.wait_ge(s.at_in, i + 1)
                    pe.wait_ge(s.aT_out, i + 1)
                    for g in range(G):
                        for c in range(C):
                            last = nc.tensor.transpose(pA[:, g, c, :], at[:, k, g, c * P:(c + 1) * P], ident[:, :])
                    last.then_inc(s.aT_mm, 1)

                def project(i, k):
                    pe.wait_ge(s.aT_out, i + 2)
                    pe.wait_ge(s.x2, G * i + G)
                    for g in range(G):
                        for c in range(C):
                            last = nc.tensor.matmul(pX[:, g, :], aT[:, k, g, c, :], v.woT[:, c, :],
                                                    start=(c == 0), stop=(c == C - 1))
                    last.then_inc(s.proj, 1)

                def turn_h(i):
                    pe.wait_ge(s.hs_in, i + 1)
                    pe.wait_ge(s.hT_out, i + 1)
                    for g in range(G):
                        for c in range(C):
                            last = nc.tensor.transpose(pH[:, g, c, :], hs[:, g, c * P:(c + 1) * P], ident[:, :])
                    last.then_inc(s.hT_mm, 1)

                def logits(i):
                    pe.wait_ge(s.hT_out, i + 2)
                    pe.wait_ge(s.lg_out, i + 1)
                    for g in range(G):
                        for c in range(C):
                            last = nc.tensor.matmul(pL[:, g, :], hT[:, g, c, :], v.gwT[:, c, :],
                                                    start=(c == 0), stop=(c == C - 1))
                    last.then_inc(s.logits, 1)

                def step(i, k, before, behind):
                    if behind:
                        turn_attended(i + 1, 1 - k)
                    if before:
                        turn_h(i - 1)
                    if behind:
                        project(i + 1, 1 - k)
                    if before:
                        logits(i - 1)
                turn_attended(0, 0)
                project(0, 0)
                groups(pe, step)
                turn_h(NGR - 1)
                logits(NGR - 1)

            @block.scalar
            def _(act):
                act.sem_inc(s.aT_out, 1)
                act.sem_inc(s.hT_out, 1)
                act.sem_inc(s.lg_out, 1)

                def attended(i, k):
                    wait_apart(act, s.aT_mm, i + 1)
                    nc.scalar.copy(at[:, k], QKV[:, bass.ds(G * i, G), 0:H]).then_inc(s.at_in, 1)

                def attended_out(i, k):
                    act.wait_ge(s.aT_mm, i + 2)
                    act.wait_ge(s.proj, i + 1)
                    nc.scalar.copy(aT[:, k], pA[:, :, :, :]).then_inc(s.aT_out, 1)

                def h_out(i):
                    act.wait_ge(s.hT_mm, i + 2)
                    act.wait_ge(s.logits, i + 1)
                    nc.scalar.copy(hT[:, :, :, :], pH[:, :, :, :]).then_inc(s.hT_out, 1)

                def logits_out(i):
                    wait_apart(act, s.logits, i + 2)
                    nc.scalar.copy(v.lg[:, bass.ds(G * i, G), :], pL[:, :, :]).then_inc(s.lg_out, 1)

                def step(i, k, before, behind):
                    if behind:
                        attended_out(i + 1, 1 - k)
                    if before:
                        h_out(i - 1)
                        logits_out(i - 1)
                    if behind == 2:
                        attended(i + 2, k)
                    act.wait_ge(s.h, G * i + G)
                    wait_apart(act, s.hT_mm, i + 1)
                    nc.scalar.copy(hs[:, :, :], QKV[:, bass.ds(G * i, G), 0:H]).then_inc(s.hs_in, 1)
                attended(0, 0)
                attended_out(0, 0)
                attended(1, 1)
                groups(act, step)
                h_out(NGR - 1)
                logits_out(NGR - 1)

            @block.vector
            def _(dve):
                dve.sem_inc(s.x2, G)

                def moments(i, first=False):
                    if not first:
                        dve.wait_ge(s.xl, G * i)
                    for g in range(G):
                        nc.vector.bn_stats(stats[:, g, :], x1[:, G * i + g, :]).then_inc(s.stats, 1)
                    for g in range(G):
                        wait_apart(dve, s.stats, G * i + g + 1)
                        nc.vector.bn_aggr(mv[:, g, :], stats[:, g, :]).then_inc(s.mv, 1)

                def step(i, k, before, behind):
                    dve.wait_ge(s.rstd1, i + 1)
                    for g in range(G):
                        nc.vector.tensor_scalar(xl[:, g, :], x1[:, G * i + g, :], mv[:, g, 0:1], rstd[:, 1, g:g + 1],
                                                ALU.subtract, ALU.mult).then_inc(s.xl, 1)
                    dve.wait_ge(s.proj, i + 2)
                    dve.wait_ge(s.resid, i + 1)
                    for g in range(G):
                        dve.wait_ge(s.xl, G * i + g + 1)
                        nc.vector.tensor_tensor(x2[:, k, g, :], xl[:, g, :], pX[:, g, :], ALU.add).then_inc(s.x2, 1)
                    for g in range(G):
                        dve.wait_ge(s.x2, G * i + g + 1 + G)
                        nc.vector.tensor_tensor_reduce(junk[:, g, :], x2[:, k, g, :], x2[:, k, g, :], 1.0, 0.0, ALU.mult,
                                                       ALU.add, sq[:, g:g + 1]).then_inc(s.square, 1)
                    if behind:
                        moments(i + 1)
                    dve.wait_ge(s.rstd2, i + 1)
                    for g in range(G):
                        nc.vector.scalar_tensor_tensor(out=QKV[:, G * i + g, 0:H], in0=x2[:, k, g, :],
                                                       scalar=rstd[:, 3, g:g + 1], in1=v.ln2_b[:, :], op0=ALU.mult,
                                                       op1=ALU.mult).then_inc(s.h, 1)
                moments(0, first=True)
                groups(dve, step)


def router(nc, sb, ps, sem, env, base_env):
    v, u = Names(env), base_env
    ident, ones, QKV, lg = u.ident, u.ones, v.QKV, v.lg
    w13T, w2T = v.w13T, v.w2T
    R = 4
    TE = T * E
    N1 = E * 2 * FFN // P // 2
    N2 = E * H // P
    with ExitStack() as ctx:
        hs = sb("hs_r", [P, R, H], F32, ctx)
        raw = sb("raw8", [P, R, 512], F32, ctx)
        tri = sb("tri", [P, P], F32, ctx)
        iota_i = sb("iota_i7", [P, E], I32, ctx)
        iota8 = sb("iota8", [P, E], F32, ctx)
        iotap_i = sb("iotap_i", [P, 1], I32, ctx)
        iotap = sb("iotap", [P, 1], F32, ctx)
        pr = sb("pr", [P, T, E], F32, ctx)
        red = sb("red7", [P, 4, T], F32, ctx)
        top = sb("top7", [P, T, 8], F32, ctx)
        topf = sb("topf7", [P, T, 2], F32, ctx)
        hot = sb("hot7", [P, 2, T, E], F32, ctx)
        sums = sb("sums7", [P, 2, T, E], F32, ctx)
        slots = sb("slots7", [P, T, 2], I32, ctx)
        slot_now = sb("slot_now", [P, R, 2], I32, ctx)
        pR = ps("pR7", [P, 2, TE], F32, ctx)
        pW = ps("pW8", [P, R, 512], F32, ctx)
        names = ("consts", "consts2", "tri_in", "ex", "chain", "tops", "indices", "ranks", "slots", "kept", "tab_chain",
                 "tab_ready", "zero_in", "padded", "hs_in", "slot_in", "wT_mm", "wT_out")
        s = Names({n: sem("s_" + n) for n in names})
        scattered = [sem(f"s_scattered{k}") for k in range(R)]
        raw_in = [sem(f"s_raw_in{k}") for k in range(R)]
        w13v = u.w13.rearrange("e (r a p) h -> p (e r) a h", a=2, p=P)
        w2v = u.w2.rearrange("e (r p) f -> p (e r) f", p=P)
        both, place, picked = pr, lg, sums
        topi = sums[:, 1, :, :].bitcast(U32)
        with nc.Block() as block:
            @block.sync
            def _(sp):
                for i0, count, src in ((0, N1, w13v), (N1, N2, w2v)):
                    with sp.Fori(0, count // R) as i:
                        for k in range(R):
                            sp.wait_ge(s.wT_mm, i0 + R * i + k + 1)
                            if src is w13v:
                                sp.dma_start(raw[:, k, :].rearrange("p (a h) -> p a h", a=2),
                                             w13v[:, R * i + k, :, :]).then_inc(raw_in[k], 16)
                            else:
                                sp.dma_start(raw[:, k, :], w2v[:, R * i + k, :]).then_inc(raw_in[k], 16)

            @block.gpsimd
            def _(pool):
                nc.gpsimd.iota(iota_i[:, :], pattern=[[1, E]], base=0, channel_multiplier=0).then_inc(s.consts, 1)
                nc.gpsimd.iota(iotap_i[:, :], pattern=[[0, 1]], base=0, channel_multiplier=1).then_inc(s.consts, 1)
                nc.gpsimd.memset(tri[:, :], 1.0).then_inc(s.consts, 1)
                nc.gpsimd.iota(v.jrow_i[:, :], pattern=[[1, NTAB]], base=0, channel_multiplier=0).then_inc(s.consts, 1)
                pool.wait_ge(s.consts, 4)
                nc.gpsimd.tensor_copy(v.jrow[:, :], v.jrow_i[:, :]).then_inc(s.consts2, 1)
                nc.gpsimd.tensor_copy(iota8[:, :], iota_i[:, :]).then_inc(s.consts2, 1)
                nc.gpsimd.tensor_copy(iotap[:, :], iotap_i[:, :]).then_inc(s.consts2, 1)
                nc.gpsimd.affine_select(out=tri[:, :], in_=tri[:, :], compare_op=ALU.is_gt, fill=0.0, base=0,
                                        pattern=[[1, P]], channel_multiplier=-1).then_inc(s.tri_in, 1)
                pool.wait_ge(s.slots, 1)

                def scatter(i, k):
                    nc.gpsimd.tensor_copy(slot_now[:, k, :], slots[:, R * i + k, :]).then_inc(s.slot_in, 1)
                    pool.wait_ge(s.hs_in, R * i + k + 1)
                    wait_apart(pool, s.slot_in, R * i + k + 1)
                    for a in range(2):
                        nc.gpsimd.indirect_dma_start(
                            out=v.queue[:, :], out_offset=bass.IndirectOffsetOnAxis(ap=slot_now[:, k, a:a + 1], axis=0),
                            in_=hs[:, k, :], in_offset=None).then_inc(scattered[k], 16)
                for k in range(R):
                    scatter(0, k)
                with pool.Fori(1, T // R) as i:
                    for k in range(R):
                        wait_apart(pool, scattered[k], 32 * i)
                        scatter(i, k)
                for k in range(R):
                    pool.wait_ge(scattered[k], 32 * (T // R))
                pool.wait_ge(s.tab_ready, 1)
                nc.gpsimd.memset(hs[:, 0, :], 0.0).then_inc(s.zero_in, 1)
                pool.wait_ge(s.zero_in, 1)
                for e in range(E):
                    nc.gpsimd.indirect_dma_start(
                        out=v.queue[:, :], out_offset=bass.IndirectOffsetOnAxis(ap=v.pad_rows[:, e:e + 1], axis=0),
                        in_=hs[:, 0, :], in_offset=None).then_inc(s.padded, 16)
                pool.wait_ge(s.padded, 16 * E)

            @block.tensor
            def _(pe):
                pe.sem_inc(s.wT_mm, R)
                pe.wait_ge(s.tri_in, 1)
                pe.wait_ge(s.chain, BOTH)
                b2 = both[:, :, :].rearrange("p k e -> p (k e)")
                nc.tensor.matmul(pR[:, 0, :], tri[:, :], b2, start=True, stop=True)
                nc.tensor.matmul(pR[:, 1, :], ones[:, :], b2, start=True, stop=True).then_inc(s.ranks, 1)
                with pe.Fori(0, (N1 + N2) // R) as i:
                    for k in range(R):
                        pe.wait_ge(raw_in[k], 16 * i + 16)
                        pe.wait_ge(s.wT_out, R * i + k + 1)
                        for a in range(4):
                            last = nc.tensor.transpose(pW[:, k, a * P:(a + 1) * P], raw[:, k, a * P:(a + 1) * P],
                                                       ident[:, :])
                        last.then_inc(s.wT_mm, 1)

            @block.scalar
            def _(act):
                act.wait_ge(s.chain, 2)
                nc.scalar.activation(pr[:, :, :], pr[:, :, :], ACT.Exp).then_inc(s.ex, 1)
                for k in range(R):
                    nc.scalar.copy(hs[:, k, :], QKV[:, k, 0:H]).then_inc(s.hs_in, 1)
                with act.Fori(1, T // R) as i:
                    for k in range(R):
                        wait_apart(act, scattered[k], 32 * i)
                        nc.scalar.copy(hs[:, k, :], QKV[:, R * i + k, 0:H]).then_inc(s.hs_in, 1)

            @block.vector
            def _(dve):
                ch = Chain(dve, s.chain)

                def bc(ap):
                    return ap.unsqueeze(2).to_broadcast([P, T, E])
                dve.sem_inc(s.wT_out, R)
                ch.link(nc.vector.reduce_max(red[:, 0, :], lg[:, :, :], AX.X))
                nc.vector.tensor_tensor(pr[:, :, :], lg[:, :, :], bc(red[:, 0, :]), ALU.subtract).then_inc(s.chain, 1)
                ch.k += 1
                dve.wait_ge(s.ex, 1)
                ch.link(nc.vector.reduce_sum(red[:, 1, :], pr[:, :, :], AX.X))
                ch.link(nc.vector.reciprocal(red[:, 2, :], red[:, 1, :]))
                ch.link(nc.vector.tensor_tensor(lg[:, :, :], pr[:, :, :], bc(red[:, 2, :]), ALU.mult))
                for t in range(T):
                    nc.vector.max(top[:, t, :], lg[:, t, :]).then_inc(s.tops, 1)
                for t in range(T):
                    dve.wait_ge(s.tops, t + 1)
                    nc.vector.max_index(topi[:, t, :], top[:, t, :], lg[:, t, :]).then_inc(s.indices, 1)
                dve.wait_ge(s.indices, T)
                dve.wait_ge(s.consts2, 3)
                ch.link(nc.vector.tensor_copy(topf[:, :, :], topi[:, :, 0:2]))
                for a in range(2):
                    ch.link(nc.vector.tensor_tensor(hot[:, a], iota8[:, :].unsqueeze(1).to_broadcast([P, T, E]),
                                                    bc(topf[:, :, a]), ALU.is_equal))
                ch.link(nc.vector.tensor_tensor(both[:, :, :], hot[:, 0], hot[:, 1], ALU.add))
                assert ch.k == BOTH
                ch.link(nc.vector.tensor_tensor(red[:, 3, :], top[:, :, 0], top[:, :, 1], ALU.add))
                ch.link(nc.vector.reciprocal(red[:, 0, :], red[:, 3, :]))
                ch.link(nc.vector.tensor_tensor(v.weights[:, :, :], top[:, :, 0:2],
                                                red[:, 0, :].unsqueeze(2).to_broadcast([P, T, 2]), ALU.mult))
                dve.wait_ge(s.ranks, 1)
                ch.link(nc.vector.tensor_copy(sums[:, 0], pR[:, 1, :].rearrange("p (t e) -> p t e", e=E)))
                now, d = 0, 1
                while d < T:
                    nc.vector.tensor_copy(sums[:, 1 - now, 0:d, :], sums[:, now, 0:d, :]).then_inc(s.chain, 1)
                    ch.k += 1
                    ch.link(nc.vector.tensor_tensor(sums[:, 1 - now, d:T, :], sums[:, now, d:T, :],
                                                    sums[:, now, 0:T - d, :], ALU.add))
                    now, d = 1 - now, 2 * d
                ch.link(nc.vector.tensor_copy(v.counts[:, :], sums[:, now, T - 1, :]))
                ranks = pR[:, 0, :].rearrange("p (t e) -> p t e", e=E)
                nc.vector.tensor_copy(place[:, 0, :], ranks[:, 0, :]).then_inc(s.chain, 1)
                ch.k += 1
                ch.link(nc.vector.tensor_tensor(place[:, 1:T, :], sums[:, now, 0:T - 1, :], ranks[:, 1:T, :], ALU.add))
                ch.link(nc.vector.scalar_tensor_tensor(out=place[:, :, :],
                                                       in0=iota8[:, :].unsqueeze(1).to_broadcast([P, T, E]),
                                                       scalar=float(CAP), in1=place[:, :, :], op0=ALU.mult, op1=ALU.add))
                ch.link(nc.vector.tensor_tensor(picked[:, :, :, :], hot[:, :, :, :],
                                                place[:, :, :].unsqueeze(1).to_broadcast([P, 2, T, E]), ALU.mult))
                ch.link(nc.vector.reduce_sum(v.rowsf[:, :, :].rearrange("p k a -> p a k"), picked[:, :, :, :], AX.X))
                nc.vector.tensor_copy(slots[:, :, :], v.rowsf[:, :, :]).then_inc(s.slots, 1)
                tc = Chain(dve, s.tab_chain)
                tables(nc, tc, v, s, v.counts, iota8, iotap)
                nc.vector.tensor_copy(v.pad_rows[:, :], v.padf[:, :]).then_inc(s.tab_ready, 1)
                dve.wait_ge(s.tab_ready, 1)
                with dve.Fori(0, N1 // R) as i:
                    for k in range(R):
                        dve.wait_ge(s.wT_mm, R * i + k + 1 + R)
                        nc.vector.tensor_copy(
                            w13T[:, :, bass.ds((R * i + k) * 2 * P, 2 * P)].rearrange("p c (a n) -> p a c n", a=2),
                            pW[:, k, :].rearrange("p (a c n) -> p a c n", a=2, c=C)).then_inc(s.wT_out, 1)
                with dve.Fori(0, N2 // R) as i:
                    for k in range(R):
                        dve.wait_ge(s.wT_mm, N1 + R * i + k + 1 + R)
                        nc.vector.tensor_copy(w2T[:, :, bass.ds((R * i + k) * P, P)],
                                              pW[:, k, :].rearrange("p (a n) -> p a n", a=4)).then_inc(s.wT_out, 1)


def tables(nc, tc, v, s, counts, iota8, iotap):
    count = counts[:, :]
    tc.link(nc.vector.scalar_tensor_tensor(out=v.padf[:, :], in0=iota8[:, :], scalar=float(CAP), in1=count,
                                           op0=ALU.mult, op1=ALU.add))
    tc.link(nc.vector.tensor_scalar(v.padf[:, :], v.padf[:, :], iotap[:, :], None, ALU.add))
    tc.link(nc.vector.tensor_scalar(v.steps[:, :], v.jrow[:, 0:T], float(P), None, ALU.mult))
    tc.link(nc.vector.tensor_tensor(v.cmp[:, :, 0:T], v.steps[:, :].unsqueeze(1).to_broadcast([P, E, T]),
                                    count.unsqueeze(2).to_broadcast([P, E, T]), ALU.is_lt))
    tc.link(nc.vector.reduce_sum(v.ntile[:, :], v.cmp[:, :, 0:T], AX.X))
    tc.link(nc.vector.tensor_copy(v.ends[:, 0:1], v.ntile[:, 0:1]))
    for e in range(1, E):
        tc.link(nc.vector.tensor_tensor(v.ends[:, e:e + 1], v.ends[:, e - 1:e], v.ntile[:, e:e + 1], ALU.add))
    total = v.ends[:, E - 1:E]
    tc.link(nc.vector.tensor_scalar(v.lastt[:, :], total, -1.0, None, ALU.add))
    tc.link(nc.vector.tensor_scalar(v.jc[:, :], v.jrow[:, :], v.lastt[:, :], None, ALU.min))
    tc.link(nc.vector.tensor_tensor(v.cmp[:, :, :], v.jc[:, :].unsqueeze(1).to_broadcast([P, E, NTAB]),
                                    v.ends[:, :].unsqueeze(2).to_broadcast([P, E, NTAB]), ALU.is_ge))
    tc.link(nc.vector.reduce_sum(v.ej[:, :], v.cmp[:, :, :].rearrange("p e j -> p j e"), AX.X))
    tc.link(nc.vector.tensor_tensor(v.cmp[:, :, :], v.cmp[:, :, :], v.ntile[:, :].unsqueeze(2).to_broadcast([P, E, NTAB]),
                                    ALU.mult))
    tc.link(nc.vector.reduce_sum(v.before[:, :], v.cmp[:, :, :].rearrange("p e j -> p j e"), AX.X))
    tc.link(nc.vector.tensor_tensor(v.rowf[:, :], v.jc[:, :], v.before[:, :], ALU.subtract))
    tc.link(nc.vector.tensor_scalar(v.rowf[:, :], v.rowf[:, :], float(P), None, ALU.mult))
    tc.link(nc.vector.scalar_tensor_tensor(out=v.rowf[:, :], in0=v.ej[:, :], scalar=float(CAP), in1=v.rowf[:, :],
                                           op0=ALU.mult, op1=ALU.add))
    tc.link(nc.vector.tensor_copy(v.tile_expert[:, :], v.ej[:, :]))
    tc.link(nc.vector.tensor_copy(v.tile_in[:, :], v.rowf[:, :]))
    for e in range(1, E):
        tc.link(nc.vector.tensor_scalar(v.lastt[:, :], v.ntile[:, e - 1:e], -float(P), float(CAP), ALU.mult, ALU.add))
        tc.link(nc.vector.tensor_scalar(v.shift[:, :, :], v.rowsf[:, :, :], float(e * CAP), v.lastt[:, :], ALU.is_ge,
                                        ALU.mult))
        tc.link(nc.vector.tensor_tensor(v.shifts[:, :, :], v.shifts[:, :, :] if e > 1 else v.rowsf[:, :, :],
                                        v.shift[:, :, :], ALU.subtract))
    tc.link(nc.vector.tensor_copy(v.rows[:, :, :], v.shifts[:, :, :]))


def stage8(nc, sb, ps, sem, env, base_env):
    v, u = Names(env), base_env
    ident = u.ident
    with ExitStack() as ctx:
        w13T, w2T = v.w13T, v.w2T
        with ExitStack() as c2:
            FC = FFN // P
            R = 4
            LAST = MAXT - 1
            room = v.QKV[:, :, :].rearrange("p t w -> p (t w)")
            at = 0

            def carve(*shape):
                nonlocal at
                size = int(np.prod(shape))
                flat = room[:, at:at + size]
                at += size
                names = " ".join("abc"[:len(shape)])
                return flat.rearrange(f"p ({names}) -> p {names}", **dict(zip("abc", shape)))
            xq, xqT = carve(R, H), carve(2, C, P)
            sil, gg, gT = carve(2, FFN), carve(2, FFN), carve(2, FC, P)
            y = carve(R, H)
            pH = ps("pH8", [P, 2, 2, FFN], F32, c2)
            pX = ps("pX8", [P, C, P], F32, c2)
            pG = ps("pG8", [P, FC, P], F32, c2)
            pY = ps("pY8", [P, H], F32, c2)
            xq_in = [sem(f"m_xq_in{k}") for k in range(R)]
            y_put = [sem(f"m_y_put{k}") for k in range(R)]
            names = ("x_T", "x_out", "up", "sil", "gated", "g_T", "g_out", "down", "y_out")
            s = Names({n: sem("m_" + n) for n in names})
            assert (MAXT - R) % R == 0

            def steps(eng, step):
                with eng.Fori(0, MAXT // R - 1) as i:
                    for k in range(R):
                        step(R * i + k + 1, (k + 1) % R, i + (k + 1) // R)
                for j in range(MAXT - R + 1, MAXT):
                    step(j, j % R, j // R)

            with nc.Block() as block:
                @block.sync
                def _(sp):
                    def load(j, k):
                        row = sp.value_load(v.tile_in[0:1, bass.ds(j, 1)], min_val=0, max_val=E * CAP - P)
                        sp.dma_start(xq[:, k, :], v.queue[bass.ds(row, P), :]).then_inc(xq_in[k], 16)

                    def put(j, k):
                        sp.wait_ge(s.y_out, j + 2)
                        sp.dma_start(v.results[bass.ds(j * P, P), :], y[:, k, :]).then_inc(y_put[k], 16)
                    for k in range(R):
                        load(k, k)
                    with sp.Fori(0, MAXT // R - 1) as i:
                        for k in range(R):
                            wait_apart(sp, s.x_T, R * i + k + 1)
                            load(R * i + k + R, k)
                            put(R * i + k, k)
                    for k in range(R):
                        put(MAXT - R + k, k)
                    for k in range(R):
                        sp.wait_ge(y_put[k], 16 * (MAXT // R) + 16)

                @block.tensor
                def _(pe):
                    def turn(j, k, i):
                        pe.wait_ge(xq_in[k], 16 * i + 16)
                        pe.wait_ge(s.x_out, j + 1)
                        for c in range(C):
                            last = nc.tensor.transpose(pX[:, c, :], xq[:, k, c * P:(c + 1) * P], ident[:, :])
                        last.then_inc(s.x_T, 1)

                    def up(j, k):
                        e = pe.value_load(v.tile_expert[0:1, bass.ds(j, 1)], min_val=0, max_val=E - 1)
                        pe.wait_ge(s.x_out, j + 2)
                        pe.wait_ge(s.gated, j + 1)
                        for a in range(2):
                            for c in range(C):
                                last = nc.tensor.matmul(pH[:, k % 2, a, :], xqT[:, k % 2, c, :],
                                                        w13T[:, c, bass.ds(e * (2 * FFN) + a * FFN, FFN)],
                                                        start=(c == 0), stop=(c == C - 1))
                        last.then_inc(s.up, 1)

                    def turn_gated(j, k):
                        pe.wait_ge(s.gated, j + 3)
                        pe.wait_ge(s.g_out, j + 1)
                        for f in range(FC):
                            last = nc.tensor.transpose(pG[:, f, :], gg[:, k % 2, f * P:(f + 1) * P], ident[:, :])
                        last.then_inc(s.g_T, 1)

                    def down(j, k):
                        e = pe.value_load(v.tile_expert[0:1, bass.ds(j, 1)], min_val=0, max_val=E - 1)
                        pe.wait_ge(s.g_out, j + 2)
                        pe.wait_ge(s.y_out, j + 1)
                        for f in range(FC):
                            last = nc.tensor.matmul(pY[:, :], gT[:, k % 2, f, :], w2T[:, f, bass.ds(e * H, H)],
                                                    start=(f == 0), stop=(f == FC - 1))
                        last.then_inc(s.down, 1)

                    def step(j, k, i):
                        if not isinstance(j, int) or j < LAST:
                            up(j + 1, k + 1)
                        turn_gated(j, k)
                        if not isinstance(j, int) or j + 1 < LAST:
                            turn(j + 2, (k + 2) % R, i + (k + 2) // R)
                        down(j - 1, k + 1)
                    turn(0, 0, 0)
                    up(0, 0)
                    turn(1, 1, 0)
                    up(1, 1)
                    turn_gated(0, 0)
                    turn(2, 2, 0)
                    steps(pe, step)
                    down(LAST, LAST % R)

                @block.scalar
                def _(act):
                    act.sem_inc(s.x_out, 1)
                    act.sem_inc(s.y_out, 1)

                    def turned(j, k, first=False):
                        act.wait_ge(s.x_T, j + 1)
                        if not first:
                            act.wait_ge(s.up, j - 1)
                        nc.scalar.copy(xqT[:, k % 2], pX[:, :, :]).then_inc(s.x_out, 1)

                    def silu(j, k):
                        act.wait_ge(s.up, j + 1)
                        act.wait_ge(s.gated, j + 1)
                        nc.scalar.activation(sil[:, k % 2, :], pH[:, k % 2, 0, :], ACT.Silu).then_inc(s.sil, 1)

                    def result(j, k, i):
                        act.wait_ge(s.down, j + 1)
                        act.wait_ge(y_put[k], 16 * i + 16)
                        nc.scalar.copy(y[:, k, :], pY[:, :]).then_inc(s.y_out, 1)

                    def step(j, k, i):
                        if not isinstance(j, int) or j < LAST:
                            silu(j + 1, k + 1)
                        if not isinstance(j, int) or j + 1 < LAST:
                            turned(j + 2, k)
                        result(j - 1, (k - 1) % R, i + (k - 1) // R)
                    for k in range(R):
                        act.sem_inc(y_put[k], 16)
                    turned(0, 0, True)
                    turned(1, 1, True)
                    silu(0, 0)
                    silu(1, 1)
                    turned(2, 2)
                    steps(act, step)
                    result(LAST, LAST % R, LAST // R)

                @block.vector
                def _(dve):
                    dve.sem_inc(s.gated, 2)
                    dve.sem_inc(s.g_out, 1)

                    def gate(j, k):
                        dve.wait_ge(s.sil, j + 1)
                        nc.vector.tensor_tensor(gg[:, k % 2, :], sil[:, k % 2, :], pH[:, k % 2, 1, :],
                                                ALU.mult).then_inc(s.gated, 1)

                    def turned(j, k):
                        dve.wait_ge(s.g_T, j + 1)
                        nc.vector.tensor_copy(gT[:, k % 2], pG[:, :, :]).then_inc(s.g_out, 1)

                    def step(j, k, i):
                        turned(j, k)
                        if not isinstance(j, int) or j < LAST:
                            gate(j + 1, k + 1)
                    gate(0, 0)
                    gate(1, 1)
                    turned(0, 0)
                    steps(dve, step)


def stage9(nc, sb, ps, sem, env, base_env):
    v, u = Names(env), base_env
    G = 4
    with ExitStack() as ctx:
        rows_now = sb("rows_now", [P, G, 2], I32, ctx)
        yy = sb("yy9", [P, G, 2, H], F32, ctx)
        got = [sem(f"f_got{k}") for k in range(G)]
        put = [sem(f"f_put{k}") for k in range(G)]
        s = Names({n: sem("f_" + n) for n in ("rows", "half", "sum")})
        out_rows = u.out.rearrange("b (t p) h -> p (b t) h", p=P)
        with nc.Block() as block:
            @block.gpsimd
            def _(pool):
                with pool.Fori(0, T // G) as i:
                    for k in range(G):
                        wait_apart(pool, s.half, G * i + k + 1)
                        wait_apart(pool, s.sum, G * i + k + 1)
                        nc.gpsimd.tensor_copy(rows_now[:, k, :], v.rows[:, G * i + k, :]).then_inc(s.rows, 1)
                        wait_apart(pool, s.rows, G * i + k + 1)
                        for a in range(2):
                            nc.gpsimd.indirect_dma_start(
                                out=yy[:, k, a, :], out_offset=None, in_=v.results[:, :],
                                in_offset=bass.IndirectOffsetOnAxis(ap=rows_now[:, k, a:a + 1], axis=0)).then_inc(got[k], 16)
                for k in range(G):
                    pool.wait_ge(got[k], 32 * (T // G))

            @block.vector
            def _(dve):
                dve.sem_inc(s.half, G)
                dve.sem_inc(s.sum, G)
                with dve.Fori(0, T // G) as i:
                    for k in range(G):
                        t = G * i + k
                        dve.wait_ge(got[k], 32 * i + 32)
                        nc.vector.scalar_tensor_tensor(out=yy[:, k, 0, :], in0=yy[:, k, 0, :],
                                                       scalar=v.weights[:, t, 0:1], in1=u.x1[:, t, :], op0=ALU.mult,
                                                       op1=ALU.add).then_inc(s.half, 1)
                        dve.wait_ge(s.half, t + G + 1)
                        nc.vector.scalar_tensor_tensor(out=u.x1[:, t, :], in0=yy[:, k, 1, :],
                                                       scalar=v.weights[:, t, 1:2], in1=yy[:, k, 0, :], op0=ALU.mult,
                                                       op1=ALU.add).then_inc(s.sum, 1)

            @block.sync
            def _(sp):
                with sp.Fori(0, T // G) as i:
                    for k in range(G):
                        sp.wait_ge(s.sum, G * i + k + 1 + G)
                        sp.dma_start(out_rows[:, G * i + k, :], u.x1[:, G * i + k, :]).then_inc(put[k], 16)
                for k in range(G):
                    sp.wait_ge(put[k], 16 * (T // G))


_INS = ["attn_" + n for n in ("hidden_states", "Wq", "bq", "Wk", "bk", "Wv", "bv", "Wo", "bo", "Wg", "bg", "Wc", "bc", "Ws",
                              "bs")] + ["ffn_" + n for n in ("ln1_w", "ln2_w", "wqkv", "wo", "gate_w", "w13", "w2")]


def rotary_tables():
    inv = (1.0 / np.power(np.float32(10000.0), np.arange(0, HD, 2, dtype=np.float32) / np.float32(HD))).astype(np.float32)
    angle = np.arange(L, dtype=np.float32)[:, None] * inv[None, :]
    return np.cos(angle).astype(np.float32), np.sin(angle).astype(np.float32)


def kernel(**inputs):
    import concourse.bacc as _bacc
    from concourse.bass_utils import run_bass_kernel_spmd as _run

    nc = _bacc.Bacc("TRN2", target_bir_lowering=False, num_devices=1)
    arrays, args = {}, []
    for name in _INS:
        arrays[f"in_{name}_dram"] = np.ascontiguousarray(inputs["L0_" + name])
    arrays["in_cos_dram"], arrays["in_sin_dram"] = rotary_tables()
    for name, a in arrays.items():
        args.append(nc.dram_tensor(name, a.shape, mybir.dt.from_np(a.dtype), kind="ExternalInput").ap())
    args.append(nc.dram_tensor("out_0_dram", (B, L, H), F32, kind="ExternalOutput").ap())
    build(nc, *args)
    r = _run(nc, [arrays], core_ids=[0])
    return r.results[0]["out_0_dram"]
```
